# Optimizing a Trainium2 kernel written in Bass

```python
import numpy as np
import jax
import jax.numpy as jnp

def _softmax(x, axis=-1):
    return jax.nn.softmax(x, axis=axis)

def _gelu(x):
    return jax.nn.gelu(x, approximate=True)

def _silu(x):
    return jax.nn.silu(x)

def _sigmoid(x):
    return jax.nn.sigmoid(x)

def _layernorm(x, axis=-1, eps=1e-05):
    m = jnp.mean(x, axis=axis, keepdims=True)
    v = jnp.var(x, axis=axis, keepdims=True)
    return (x - m) / jnp.sqrt(v + eps)

def _scatter_add(tgt, idx, src, axis=0):
    return tgt.at[idx].add(src)

def _segment_sum(src, seg, n):
    return jax.ops.segment_sum(src, seg, n)
kernel_name = 'mk_gnn_resnorm_d4_gnn_r64_1d29be'

def setup_inputs(seed: int=0):
    np.random.seed(seed)
    _w = jnp.asarray

    def _rec_inputs():
        import jax
        import jax.numpy as jnp
        _gk = jax.random.key(seed)
        x = -8.776e-05 + 1 * jax.random.normal(jax.random.fold_in(_gk, 1), (10000, 512), jnp.float32)
        src = jax.random.randint(jax.random.fold_in(_gk, 2), (5000,), 0, 10000, jnp.int32)
        dst = jnp.minimum((10000 * jax.random.uniform(jax.random.fold_in(_gk, 3), (5000,)) ** 2.0).astype(jnp.int32), 9999)
        _o = jnp.argsort(dst, stable=True)
        src = src[_o]
        dst = dst[_o]
        edge_attr_4 = 0.00171547 + 0.999346 * jax.random.normal(jax.random.fold_in(_gk, 11), (5000, 4), jnp.float32)
        edge_attr_8 = 0.000126197 + 0.999763 * jax.random.normal(jax.random.fold_in(_gk, 12), (5000, 8), jnp.float32)
        return (x, src, dst, edge_attr_4, edge_attr_8)
    x, src, dst, edge_attr_4, edge_attr_8 = _rec_inputs()

    def _L0_gnn_setup():
        import jax, jax.numpy as jnp
        import numpy as np
        MUL = 128
        N_NODES = 10000
        N_EDGES = 2500
        R_BASIS = 8
        HIDDEN = 64
        W_NUMEL = 4 * MUL
        SQRT3 = 3.0 ** 0.5
        SILU_2MOM = 1.679177
        AVG_NUM_NEIGHBORS = 10.0

        def _lin_irreps(x0, x1, W0, W1):
            y0 = x0 @ W0 / jnp.sqrt(jnp.float32(W0.shape[0]))
            y1 = jnp.einsum('num,uv->nvm', x1, W1) / jnp.sqrt(jnp.float32(W1.shape[0]))
            return (y0, y1)

        def _forward(node_feats, edge_attrs, edge_feats, edge_index, W_up0, W_up1, W_mlp1, W_mlp2, W_mlp3, W_mlp4, W_out0, W_out1):
            num_nodes = node_feats.shape[0]
            sender, receiver = (edge_index[0], edge_index[1])
            x0 = node_feats[:, :MUL]
            x1 = node_feats[:, MUL:].reshape(num_nodes, MUL, 3)
            x0, x1 = _lin_irreps(x0, x1, W_up0, W_up1)
            h = edge_feats
            for W in (W_mlp1, W_mlp2, W_mlp3):
                h = SILU_2MOM * jax.nn.silu(h @ W / jnp.sqrt(jnp.float32(W.shape[0])))
            tpw = h @ W_mlp4 / jnp.sqrt(jnp.float32(W_mlp4.shape[0]))
            w1, w2, w3, w4 = jnp.split(tpw, 4, axis=-1)
            s0 = x0[sender]
            s1 = x1[sender]
            y0 = edge_attrs[:, 0:1]
            y1 = edge_attrs[:, 1:4]
            p1 = w1 * s0 * y0
            p2 = (w2 * s0)[:, :, None] * y1[:, None, :]
            p3 = w3[:, :, None] * s1 * y0[:, None, :]
            p4 = w4 * jnp.einsum('eum,em->eu', s1, y1) / SQRT3
            m0 = jnp.concatenate([p1, p4], axis=-1)
            m1 = jnp.concatenate([p2, p3], axis=1)
            msg0 = jax.ops.segment_sum(m0, receiver, num_segments=num_nodes)
            msg1 = jax.ops.segment_sum(m1, receiver, num_segments=num_nodes)
            o0, o1 = _lin_irreps(msg0, msg1, W_out0, W_out1)
            out = jnp.concatenate([o0, o1.reshape(num_nodes, 3 * MUL)], axis=-1)
            return out / AVG_NUM_NEIGHBORS
        key = jax.random.key(seed)
        ks = jax.random.split(key, 12)
        rn = lambda k, s: jax.random.normal(k, s, dtype=jnp.float32)
        return {'node_feats': rn(ks[0], (N_NODES, 4 * MUL)), 'edge_attrs': rn(ks[1], (N_EDGES, 4)), 'edge_feats': rn(ks[2], (N_EDGES, R_BASIS)), 'edge_index': jax.random.randint(ks[3], (2, N_EDGES), 0, N_NODES), 'W_up0': rn(ks[4], (MUL, MUL)), 'W_up1': rn(ks[5], (MUL, MUL)), 'W_mlp1': rn(ks[6], (R_BASIS, HIDDEN)), 'W_mlp2': rn(ks[7], (HIDDEN, HIDDEN)), 'W_mlp3': rn(ks[8], (HIDDEN, HIDDEN)), 'W_mlp4': rn(ks[9], (HIDDEN, W_NUMEL)), 'W_out0': rn(ks[10], (2 * MUL, MUL)), 'W_out1': rn(ks[11], (2 * MUL, MUL))}
    _L0_gnn_all = _L0_gnn_setup()
    _L0_gnn_in = {k: v for k, v in _L0_gnn_all.items() if k in ('W_up0', 'W_up1', 'W_mlp1', 'W_mlp2', 'W_mlp3', 'W_mlp4', 'W_out0', 'W_out1')}
    del _L0_gnn_all

    def _L1_gnn_setup():
        import jax, jax.numpy as jnp
        import numpy as np
        N_NODES = 10000
        N_EDGES = 2500
        D = 512
        key = jax.random.key(seed)
        k_h, k_e, k_w1, k_w2 = jax.random.split(key, 4)
        h = jax.random.normal(k_h, (N_NODES, D), dtype=jnp.float32)
        edge_index = jax.random.randint(k_e, (2, N_EDGES), 0, N_NODES, dtype=jnp.int64)
        scale = 1.0 / np.sqrt(D)
        W1 = jax.random.normal(k_w1, (D, D), dtype=jnp.float32) * scale
        b1 = jnp.zeros((D,), dtype=jnp.float32)
        W2 = jax.random.normal(k_w2, (D, D), dtype=jnp.float32) * scale
        b2 = jnp.zeros((D,), dtype=jnp.float32)
        return {'h': h, 'edge_index': edge_index, 'W1': W1, 'b1': b1, 'W2': W2, 'b2': b2}
    _L1_gnn_all = _L1_gnn_setup()
    _L1_gnn_in = {k: v for k, v in _L1_gnn_all.items() if k in ('W1', 'b1', 'W2', 'b2')}
    del _L1_gnn_all

    def _L2_gnn_setup():
        import jax, jax.numpy as jnp
        import numpy as np
        N = 20000
        E = 5000
        D = 512
        H = 8
        DK = D // H
        key = jax.random.key(seed)
        ks = jax.random.split(key, 12)
        x = jax.random.normal(ks[0], (N, D), jnp.float32)
        rows = jnp.sort(jax.random.randint(ks[1], (E,), 0, N))
        cols = jax.random.randint(ks[2], (E,), 0, N)
        edge_index = jnp.stack([rows, cols]).astype(jnp.int32)
        att_bias = jax.random.normal(ks[3], (E, H), jnp.float32)
        s = float(1.0 / np.sqrt(D))
        Wq = jax.random.normal(ks[4], (D, D), jnp.float32) * s
        Wk = jax.random.normal(ks[5], (D, D), jnp.float32) * s
        Wv = jax.random.normal(ks[6], (D, D), jnp.float32) * s
        Wo = jax.random.normal(ks[7], (D, D), jnp.float32) * s
        bq = jnp.zeros((D,), jnp.float32)
        bk = jnp.zeros((D,), jnp.float32)
        bv = jnp.zeros((D,), jnp.float32)
        bo = jnp.zeros((D,), jnp.float32)
        return dict(x=x, edge_index=edge_index, att_bias=att_bias, Wq=Wq, bq=bq, Wk=Wk, bk=bk, Wv=Wv, bv=bv, Wo=Wo, bo=bo)
    _L2_gnn_all = _L2_gnn_setup()
    _L2_gnn_in = {k: v for k, v in _L2_gnn_all.items() if k in ('Wq', 'bq', 'Wk', 'bk', 'Wv', 'bv', 'Wo', 'bo')}
    del _L2_gnn_all

    def _L3_gnn_setup():
        import jax, jax.numpy as jnp
        import numpy as np
        N_NODES = 10000

        def gcn_conv(x, edge_index, W, b):
            n = x.shape[0]
            h = x @ W
            loop = jnp.arange(n, dtype=edge_index.dtype)
            src = jnp.concatenate([edge_index[0], loop])
            dst = jnp.concatenate([edge_index[1], loop])
            ones = jnp.ones(src.shape[0], dtype=h.dtype)
            deg = jax.ops.segment_sum(ones, dst, num_segments=n)
            dis = jnp.where(deg > 0, jax.lax.rsqrt(deg), 0.0)
            norm = dis[src] * dis[dst]
            msg = h[src] * norm[:, None]
            out = jax.ops.segment_sum(msg, dst, num_segments=n)
            return out + b
        key = jax.random.key(seed)
        k1, k2, k3, k4, k5 = jax.random.split(key, 5)
        num_features, hidden, num_classes = (512, 512, 512)
        x = jax.random.normal(k1, (N_NODES, num_features), dtype=jnp.float32)
        edge_index = jax.random.randint(k2, (2, 2500), 0, N_NODES, dtype=jnp.int64)
        s1 = 1.0 / np.sqrt(num_features)
        s2 = 1.0 / np.sqrt(hidden)
        W1 = jax.random.uniform(k3, (num_features, hidden), jnp.float32, -s1, s1)
        b1 = jnp.zeros((hidden,), jnp.float32)
        W2 = jax.random.uniform(k4, (hidden, num_classes), jnp.float32, -s2, s2)
        b2 = jnp.zeros((num_classes,), jnp.float32)
        return {'x': x, 'edge_index': edge_index, 'W1': W1, 'b1': b1, 'W2': W2, 'b2': b2}
    _L3_gnn_all = _L3_gnn_setup()
    _L3_gnn_in = {k: v for k, v in _L3_gnn_all.items() if k in ('W1', 'b1', 'W2', 'b2')}
    del _L3_gnn_all
    return {'x': x, 'src': src, 'dst': dst, 'edge_attr_4': edge_attr_4, 'edge_attr_8': edge_attr_8, 'L0_gnn_W_up0': _L0_gnn_in['W_up0'], 'L0_gnn_W_up1': _L0_gnn_in['W_up1'], 'L0_gnn_W_mlp1': _L0_gnn_in['W_mlp1'], 'L0_gnn_W_mlp2': _L0_gnn_in['W_mlp2'], 'L0_gnn_W_mlp3': _L0_gnn_in['W_mlp3'], 'L0_gnn_W_mlp4': _L0_gnn_in['W_mlp4'], 'L0_gnn_W_out0': _L0_gnn_in['W_out0'], 'L0_gnn_W_out1': _L0_gnn_in['W_out1'], 'L1_gnn_W1': _L1_gnn_in['W1'], 'L1_gnn_b1': _L1_gnn_in['b1'], 'L1_gnn_W2': _L1_gnn_in['W2'], 'L1_gnn_b2': _L1_gnn_in['b2'], 'L2_gnn_Wq': _L2_gnn_in['Wq'], 'L2_gnn_bq': _L2_gnn_in['bq'], 'L2_gnn_Wk': _L2_gnn_in['Wk'], 'L2_gnn_bk': _L2_gnn_in['bk'], 'L2_gnn_Wv': _L2_gnn_in['Wv'], 'L2_gnn_bv': _L2_gnn_in['bv'], 'L2_gnn_Wo': _L2_gnn_in['Wo'], 'L2_gnn_bo': _L2_gnn_in['bo'], 'L3_gnn_W1': _L3_gnn_in['W1'], 'L3_gnn_b1': _L3_gnn_in['b1'], 'L3_gnn_W2': _L3_gnn_in['W2'], 'L3_gnn_b2': _L3_gnn_in['b2']}

def reference(x, src, dst, edge_attr_4, edge_attr_8, L0_gnn_W_up0, L0_gnn_W_up1, L0_gnn_W_mlp1, L0_gnn_W_mlp2, L0_gnn_W_mlp3, L0_gnn_W_mlp4, L0_gnn_W_out0, L0_gnn_W_out1, L1_gnn_W1, L1_gnn_b1, L1_gnn_W2, L1_gnn_b2, L2_gnn_Wq, L2_gnn_bq, L2_gnn_Wk, L2_gnn_bk, L2_gnn_Wv, L2_gnn_bv, L2_gnn_Wo, L2_gnn_bo, L3_gnn_W1, L3_gnn_b1, L3_gnn_W2, L3_gnn_b2):
    import jax
    import jax.numpy as jnp

    def _L0_gnn_ref(node_feats, edge_attrs, edge_feats, edge_index, W_up0, W_up1, W_mlp1, W_mlp2, W_mlp3, W_mlp4, W_out0, W_out1):
        import jax, jax.numpy as jnp
        import numpy as np
        MUL = 128
        N_NODES = 10000
        N_EDGES = 2500
        R_BASIS = 8
        HIDDEN = 64
        W_NUMEL = 4 * MUL
        SQRT3 = 3.0 ** 0.5
        SILU_2MOM = 1.679177
        AVG_NUM_NEIGHBORS = 10.0

        def _lin_irreps(x0, x1, W0, W1):
            y0 = x0 @ W0 / jnp.sqrt(jnp.float32(W0.shape[0]))
            y1 = jnp.einsum('num,uv->nvm', x1, W1) / jnp.sqrt(jnp.float32(W1.shape[0]))
            return (y0, y1)

        def _forward(node_feats, edge_attrs, edge_feats, edge_index, W_up0, W_up1, W_mlp1, W_mlp2, W_mlp3, W_mlp4, W_out0, W_out1):
            num_nodes = node_feats.shape[0]
            sender, receiver = (edge_index[0], edge_index[1])
            x0 = node_feats[:, :MUL]
            x1 = node_feats[:, MUL:].reshape(num_nodes, MUL, 3)
            x0, x1 = _lin_irreps(x0, x1, W_up0, W_up1)
            h = edge_feats
            for W in (W_mlp1, W_mlp2, W_mlp3):
                h = SILU_2MOM * jax.nn.silu(h @ W / jnp.sqrt(jnp.float32(W.shape[0])))
            tpw = h @ W_mlp4 / jnp.sqrt(jnp.float32(W_mlp4.shape[0]))
            w1, w2, w3, w4 = jnp.split(tpw, 4, axis=-1)
            s0 = x0[sender]
            s1 = x1[sender]
            y0 = edge_attrs[:, 0:1]
            y1 = edge_attrs[:, 1:4]
            p1 = w1 * s0 * y0
            p2 = (w2 * s0)[:, :, None] * y1[:, None, :]
            p3 = w3[:, :, None] * s1 * y0[:, None, :]
            p4 = w4 * jnp.einsum('eum,em->eu', s1, y1) / SQRT3
            m0 = jnp.concatenate([p1, p4], axis=-1)
            m1 = jnp.concatenate([p2, p3], axis=1)
            msg0 = jax.ops.segment_sum(m0, receiver, num_segments=num_nodes)
            msg1 = jax.ops.segment_sum(m1, receiver, num_segments=num_nodes)
            o0, o1 = _lin_irreps(msg0, msg1, W_out0, W_out1)
            out = jnp.concatenate([o0, o1.reshape(num_nodes, 3 * MUL)], axis=-1)
            return out / AVG_NUM_NEIGHBORS
        return _forward(node_feats, edge_attrs, edge_feats, edge_index, W_up0, W_up1, W_mlp1, W_mlp2, W_mlp3, W_mlp4, W_out0, W_out1)

    def _L1_gnn_ref(h, edge_index, W1, b1, W2, b2):
        import jax, jax.numpy as jnp
        import numpy as np
        N_NODES = 10000
        N_EDGES = 2500
        D = 512
        send, rec = (edge_index[0], edge_index[1])
        agg = jax.ops.segment_sum(h[send], rec, num_segments=h.shape[0])
        x = h + agg
        x = jax.nn.relu(x @ W1 + b1)
        x = x @ W2 + b2
        return x

    def _L2_gnn_ref(x, edge_index, att_bias, Wq, bq, Wk, bk, Wv, bv, Wo, bo):
        import jax, jax.numpy as jnp
        import numpy as np
        N = 20000
        E = 5000
        D = 512
        H = 8
        DK = D // H
        n = x.shape[0]
        rows, cols = (edge_index[0], edge_index[1])
        q = (x @ Wq + bq).reshape(n, H, DK)
        k = (x @ Wk + bk).reshape(n, H, DK)
        v = (x @ Wv + bv).reshape(n, H, DK)
        scale = 1.0 / jnp.sqrt(jnp.asarray(DK, x.dtype))
        logits = jnp.einsum('ehd,ehd->eh', q[rows] * scale, k[cols]) + att_bias
        row_max = jax.ops.segment_max(logits, rows, num_segments=n)
        p = jnp.exp(logits - row_max[rows])
        denom = jax.ops.segment_sum(p, rows, num_segments=n)
        att = p / denom[rows]
        y = jax.ops.segment_sum(att[:, :, None] * v[cols], rows, num_segments=n)
        out = y.reshape(n, H * DK) @ Wo + bo
        return out

    def _L3_gnn_ref(x, edge_index, W1, b1, W2, b2):
        import jax, jax.numpy as jnp
        import numpy as np
        N_NODES = 10000

        def gcn_conv(x, edge_index, W, b):
            n = x.shape[0]
            h = x @ W
            loop = jnp.arange(n, dtype=edge_index.dtype)
            src = jnp.concatenate([edge_index[0], loop])
            dst = jnp.concatenate([edge_index[1], loop])
            ones = jnp.ones(src.shape[0], dtype=h.dtype)
            deg = jax.ops.segment_sum(ones, dst, num_segments=n)
            dis = jnp.where(deg > 0, jax.lax.rsqrt(deg), 0.0)
            norm = dis[src] * dis[dst]
            msg = h[src] * norm[:, None]
            out = jax.ops.segment_sum(msg, dst, num_segments=n)
            return out + b
        h = jax.nn.relu(gcn_conv(x, edge_index, W1, b1))
        out = gcn_conv(h, edge_index, W2, b2)
        return out
    edge_index = jnp.stack([src, dst])
    x = _layernorm(x + _L0_gnn_ref(x, edge_attr_4, edge_attr_8, edge_index, L0_gnn_W_up0, L0_gnn_W_up1, L0_gnn_W_mlp1, L0_gnn_W_mlp2, L0_gnn_W_mlp3, L0_gnn_W_mlp4, L0_gnn_W_out0, L0_gnn_W_out1), axis=-1)
    x = _layernorm(x + _L1_gnn_ref(x, edge_index, L1_gnn_W1, L1_gnn_b1, L1_gnn_W2, L1_gnn_b2), axis=-1)
    x = _layernorm(x + _L2_gnn_ref(x, edge_index, edge_attr_8, L2_gnn_Wq, L2_gnn_bq, L2_gnn_Wk, L2_gnn_bk, L2_gnn_Wv, L2_gnn_bv, L2_gnn_Wo, L2_gnn_bo), axis=-1)
    x = _layernorm(x + _L3_gnn_ref(x, edge_index, L3_gnn_W1, L3_gnn_b1, L3_gnn_W2, L3_gnn_b2), axis=-1)
    return x

_drawn_inputs = setup_inputs


def setup_inputs(seed=0):
    import zlib

    import numpy as np

    out = dict(_drawn_inputs(seed))
    spreads = {'L1_gnn_b1': (0.0, 0.1),
     'L1_gnn_b2': (0.0, 0.1),
     'L2_gnn_bq': (0.0, 0.8),
     'L2_gnn_bk': (0.0, 0.8),
     'L2_gnn_bv': (0.0, 0.1),
     'L2_gnn_bo': (0.0, 0.1),
     'L3_gnn_b1': (0.0, 0.1),
     'L3_gnn_b2': (0.0, 0.1)}
    factors = {}
    for name, (base, spread) in spreads.items():
        noise = np.random.default_rng([zlib.crc32(name.encode()), seed]).standard_normal(out[name].shape)
        drawn = base * np.exp(spread * noise) if base else spread * noise
        out[name] = jnp.asarray(drawn.astype(out[name].dtype))
    for name, factor in factors.items():
        out[name] = (out[name] * factor).astype(out[name].dtype)
    return out
```

```python
import concourse.bass as bass
from concourse import mybir
from contextlib import ExitStack

F32 = mybir.dt.float32
F32R = mybir.dt.float32r
BF16 = mybir.dt.bfloat16
I32 = mybir.dt.int32
ALU = mybir.AluOpType
ACT = mybir.ActivationFunctionType
AX = mybir.AxisListType

P = 128
N = 10000
E = 5000
D = 512
KC = D // P
NT = -(-N // P)
NLAST = N - (NT - 1) * P
ET = 40
EP = E // ET
EPAD = ET * P
PAD_NODE = N + 100
SKIP = 16384
REC = 16


def tile_loop(eng, n, step, ahead=2):
    pairs_end = 2 + (n - 2 - ahead) // 2 * 2
    step(0, 0, True, False)
    step(1, 1, True, False)
    with eng.Fori(1, pairs_end // 2) as pair:
        step(pair * 2, 0, False, False)
        step(pair * 2 + 1, 1, False, False)
    for t in range(pairs_end, n):
        step(t, t % 2, False, t == n - 1)


K = 4


def rounds(eng, n, step, peel=1):
    for i in range(peel):
        for s in range(K):
            step(i, s)
    with eng.Fori(peel, n // K - 1) as i:
        for s in range(K):
            step(i, s)
    for t in range((n // K - 1) * K, n):
        step(t // K, t % K)


def back(i, s, k):
    return (i, s - k) if s >= k else (i - 1, s - k + K)


def exists(i):
    return not isinstance(i, int) or i >= 0


def later(i):
    return not isinstance(i, int) or i >= 1


def hold(eng, sem, value, held):
    eng.wait_ge(sem, value)
    eng.sem_inc(held, 1)


def load_edges(nc, g):
    with ExitStack() as ctx:
        a4 = ctx.enter_context(nc.sbuf_tensor("a4_in", [P, ET * 4], F32))
        a8 = ctx.enter_context(nc.sbuf_tensor("a8_in", [P, ET * 8], F32))
        his = ctx.enter_context(nc.sbuf_tensor("hi_int", [P, 2, ET], I32))
        los = ctx.enter_context(nc.sbuf_tensor("lo_int", [P, 2, ET], I32))
        hif = ctx.enter_context(nc.sbuf_tensor("hi_f", [P, 2, ET], F32))
        lof = ctx.enter_context(nc.sbuf_tensor("lo_f", [P, 2, ET], F32))
        ids = ctx.enter_context(nc.sbuf_tensor("ids_int", [P, 2, ET], I32))
        iota = ctx.enter_context(nc.sbuf_tensor("iota_row", [P, P], F32))
        sem = lambda n: nc.alloc_semaphore(n)
        filled, loaded, attrs_loaded, made = sem("le_filled"), sem("le_loaded"), sem("le_attrs"), sem("le_made")
        block = ctx.enter_context(nc.Block())

        @block.sync
        def _(sp):
            sp.wait_ge(filled, 1)
            sp.dma_start(ids[0:EP, 0, :], g.src.rearrange("(p t) -> p t", t=ET)).then_inc(loaded, 16)
            sp.dma_start(ids[0:EP, 1, :], g.dst.rearrange("(p t) -> p t", t=ET)).then_inc(loaded, 16)
            sp.dma_start(a4[0:EP, :], g.edge_attr_4.rearrange("(p t) c -> p (t c)", t=ET)).then_inc(attrs_loaded, 16)
            sp.dma_start(a8[0:EP, :], g.edge_attr_8.rearrange("(p t) c -> p (t c)", t=ET)).then_inc(attrs_loaded, 16)

        @block.gpsimd
        def _(pool):
            nc.gpsimd.iota(iota[:, :], [[1, P]], base=0, channel_multiplier=0,
                           allow_small_or_imprecise_dtypes=True).then_inc(made, 1)
            nc.gpsimd.memset(g.ident[:, :], 0.0).then_inc(made, 1)
            nc.gpsimd.memset(g.ones[:, :], 1.0).then_inc(made, 1)
            nc.gpsimd.memset(g.before[:, :], 1.0).then_inc(made, 1)
            pool.wait_ge(made, 4)
            nc.gpsimd.affine_select(out=g.ident[:, :], in_=g.ident[:, :], compare_op=ALU.not_equal, fill=1.0,
                                    base=0, pattern=[[-1, P]], channel_multiplier=1).then_inc(made, 1)
            nc.gpsimd.affine_select(out=g.before[:, :], in_=g.before[:, :], compare_op=ALU.is_gt, fill=0.0,
                                    base=0, pattern=[[1, P]], channel_multiplier=-1).then_inc(made, 1)

        @block.vector
        def _(dve):
            nc.vector.memset(ids[:, :, :], PAD_NODE).then_inc(filled, 1)
            nc.vector.memset(g.rec_in[:, :, :], 0.0).then_inc(filled, 1)
            dve.wait_ge(made, 6)
            nc.vector.tensor_copy(g.ident_bf[:, :], g.ident[:, :])
            nc.vector.tensor_copy(g.last_row[:, :], g.ident[:, P - 1:P])
            nc.vector.tensor_tensor(g.after[:, :], g.ones[:, :], g.before[:, :], ALU.subtract).then_inc(filled, 1)
            dve.wait_ge(filled, 3)
            nc.vector.tensor_tensor(g.after[:, :], g.after[:, :], g.ident[:, :], ALU.subtract)
            dve.wait_ge(loaded, 32)
            nc.vector.tensor_scalar(his[:, :, :], ids[:, :, :], 7, None, ALU.arith_shift_right).then_inc(filled, 1)
            nc.vector.tensor_scalar(los[:, :, :], ids[:, :, :], P - 1, None, ALU.bitwise_and).then_inc(filled, 1)
            nc.vector.tensor_copy(g.keys[:, :, :], ids[:, :, :]).then_inc(filled, 1)
            dve.wait_ge(filled, 6)
            nc.vector.tensor_copy(hif[:, :, :], his[:, :, :]).then_inc(filled, 1)
            nc.vector.tensor_copy(lof[:, :, :], los[:, :, :]).then_inc(filled, 1)
            dve.wait_ge(filled, 8)
            for o in range(2):
                nc.vector.tensor_tensor(g.hot_hi[:, o, :, :], iota[:, 0:NT].unsqueeze(1).to_broadcast([P, ET, NT]),
                                        hif[:, o, :].unsqueeze(2).to_broadcast([P, ET, NT]), ALU.is_equal)
                nc.vector.tensor_tensor(g.hot_lo[:, o, :, :], iota[:, :].unsqueeze(1).to_broadcast([P, ET, P]),
                                        lof[:, o, :].unsqueeze(2).to_broadcast([P, ET, P]), ALU.is_equal)
                nc.vector.tensor_copy(g.rec_in[:, :, o], g.keys[:, o, :])
            dve.wait_ge(attrs_loaded, 32)
            nc.vector.tensor_copy(g.rec_in[0:EP, :, 2:6], a4[0:EP, :].rearrange("p (t c) -> p t c", c=4))
            nc.vector.tensor_copy(g.rec_in[0:EP, :, 6:14], a8[0:EP, :].rearrange("p (t c) -> p t c", c=8))


def sort_positions(nc, g):
    with ExitStack() as ctx:
        sb = lambda n, s, d=F32: ctx.enter_context(nc.sbuf_tensor(n, s, d))
        sem = lambda n: nc.alloc_semaphore(n)
        total, upto = sb("total", [NT, 2, P]), sb("upto", [NT, 2, P])
        row_start, empty = sb("row_start", [NT, 2]), sb("empty", [NT, 2, P])
        running = [sb(f"running{s}", [NT, 2, P]) for s in range(2)]
        hot_T = [sb(f"hot_T{s}", [NT, 2, P]) for s in range(2)]
        key_diag = [sb(f"key_diag{s}", [P, 2, P]) for s in range(2)]
        picked, tied = sb("picked", [P, 2, ET]), sb("tied", [P, 2, ET])
        scrap = [sb(f"scrap{s}", [P, 4, P]) for s in range(2)]
        zeros, ndeg, root = sb("zeros", [NT, P]), sb("ndeg", [NT, P]), sb("root", [NT, 4, P])
        ps_total = ctx.enter_context(nc.psum_tensor("ps_total", [NT, 4, P], F32))
        ps_total2 = ctx.enter_context(nc.psum_tensor("ps_total2", [NT, 4, P], F32))
        ps_hot = [ctx.enter_context(nc.psum_tensor(f"ps_hot{s}", [NT, 4, P], F32)) for s in range(2)]
        ps_key = [ctx.enter_context(nc.psum_tensor(f"ps_key{s}", [P, 4, P], F32)) for s in range(2)]
        ps_pick = [ctx.enter_context(nc.psum_tensor(f"ps_pick{s}", [P, 4, P], F32)) for s in range(2)]
        counted, summed, started, chain = sem("so_counted"), sem("so_summed"), sem("so_started"), sem("so_chain")
        hot_ready, hot_copied, diag_ready = sem("so_hot_ready"), sem("so_hot_copied"), sem("so_diag_ready")
        key_ready, picked_ready, tile_done = sem("so_key_ready"), sem("so_picked_ready"), sem("so_tile_done")
        table_ready, turned, stored = sem("so_table_ready"), sem("so_turned"), sem("so_stored")
        cols_ready, running_ready = sem("so_cols_ready"), sem("so_running_ready")
        block = ctx.enter_context(nc.Block())

        @block.tensor
        def _(pe):
            for o, ps in ((0, ps_total), (1, ps_total2)):
                nc.tensor.matmul(ps[:, 0, :], g.hot_hi[:, o, 0, :], g.hot_lo[:, o, 0, :], start=True, stop=False)
                with pe.Fori(1, ET - 1) as t:
                    nc.tensor.matmul(ps[:, 0, :], g.hot_hi[:, o, bass.ds(t, 1), :].rearrange("p a b -> p (a b)"),
                                     g.hot_lo[:, o, bass.ds(t, 1), :].rearrange("p a b -> p (a b)"),
                                     start=False, stop=False)
                nc.tensor.matmul(ps[:, 0, :], g.hot_hi[:, o, ET - 1, :], g.hot_lo[:, o, ET - 1, :],
                                 start=False, stop=True).then_inc(counted, 1)
            pe.wait_ge(summed, 1)
            nc.tensor.matmul(ps_total[:, 1, 0:2], g.before[0:NT, 0:NT], upto[:, :, P - 1], start=True,
                             stop=True).then_inc(started, 1)

            def step(t, s, first, last):
                if not first:
                    pe.wait_ge(hot_copied, t - 1)
                    pe.wait_ge(tile_done, t - 1)
                for o in range(2):
                    hot = g.hot_hi[:, o, bass.ds(t, 1), :].rearrange("p a b -> p (a b)")
                    nc.tensor.matmul(ps_hot[s][:, o, :], hot, g.ident_bf[:, :], start=True, stop=True)
                    m = nc.tensor.matmul(ps_key[s][0:NT, 2 + o, :], hot,
                                         g.hot_lo[:, o, bass.ds(t, 1), :].rearrange("p a b -> p (a b)"),
                                         start=True, stop=True)
                m.then_inc(hot_ready, 1)
                pe.wait_ge(diag_ready, t + 1)
                for o in range(2):
                    m = nc.tensor.matmul(ps_key[s][:, o, :], g.ones[:, :], key_diag[s][:, o, :], start=True, stop=True)
                m.then_inc(key_ready, 1)
                pe.wait_ge(hot_copied, t + 1)
                pe.wait_ge(running_ready, t + 1)
                for o in range(2):
                    m = nc.tensor.matmul(ps_pick[s][:, o, :], hot_T[s][:, o, :], running[s][:, o, :],
                                         start=True, stop=True)
                m.then_inc(picked_ready, 1)

            tile_loop(pe, ET, step)
            pe.wait_ge(table_ready, 1)
            for n in range(3):
                m = nc.tensor.transpose(ps_key[0][:, n, 0:NT], g.ntab[:, :, n], g.ident[0:NT, 0:NT])
            m.then_inc(turned, 1)

        @block.scalar
        def _(act):
            def step(t, s, first, last):
                if not first:
                    act.wait_ge(key_ready, t - 1)
                for o in range(2):
                    m = nc.scalar.activation(key_diag[s][:, o, :], g.ident[:, :], ACT.Copy,
                                             scale=g.keys[:, o, bass.ds(t, 1)])
                m.then_inc(diag_ready, 1)
                act.wait_ge(hot_ready, t + 1)
                if not first:
                    act.wait_ge(picked_ready, t - 1)
                nc.scalar.activation(hot_T[s][:, :, :], ps_hot[s][:, 0:2, :], ACT.Copy).then_inc(hot_copied, 1)

            tile_loop(act, ET, step)
            act.wait_ge(cols_ready, 1)
            nc.scalar.activation(ndeg[:, :], total[:, 1, :], ACT.Sqrt, bias=g.one_col[0:NT, :]).then_inc(cols_ready, 1)

        @block.vector
        def _(dve):
            n_chain = [0]

            def link(ins):
                n_chain[0] += 1
                ins.then_inc(chain, 1)
                dve.wait_ge(chain, n_chain[0])

            nc.vector.memset(zeros[:, :], 0.0)
            link(nc.vector.memset(g.one_col[:, :], 1.0))
            dve.wait_ge(counted, 2)
            nc.vector.tensor_copy(total[:, 0, :], ps_total[:, 0, :])
            link(nc.vector.tensor_copy(total[:, 1, :], ps_total2[:, 0, :]))
            for o in range(2):
                m = nc.vector.tensor_tensor_scan(upto[:, o, :], total[:, o, :], zeros[:, :], 0.0, ALU.add, ALU.add)
            m.then_inc(summed, 1)
            dve.wait_ge(started, 1)
            link(nc.vector.tensor_copy(row_start[:, :], ps_total[:, 1, 0:2]))
            for o in range(2):
                link(nc.vector.tensor_scalar(upto[:, o, :], upto[:, o, :], row_start[:, o:o + 1], None, ALU.add))
            nc.vector.tensor_tensor(running[0][:, :, :], upto[:, :, :], total[:, :, :], ALU.subtract)\
              .then_inc(running_ready, 1)
            dve.wait_ge(running_ready, 1)

            def step(t, s, first, last):
                dve.wait_ge(key_ready, t + 1)
                if not first:
                    dve.wait_ge(picked_ready, t)
                elif s == 1:
                    dve.wait_ge(picked_ready, 1)
                nc.vector.tensor_tensor(running[1 - s][:, :, :], running[s][:, :, :], ps_key[s][0:NT, 2:4, :],
                                        ALU.add).then_inc(running_ready, 1)
                if not first:
                    dve.wait_ge(tile_done, t - 1)
                for o in range(2):
                    nc.vector.scalar_tensor_tensor(scrap[s][:, o, :], ps_key[s][:, o, :], g.keys[:, o, bass.ds(t, 1)],
                                                   g.after[:, :], ALU.is_equal, ALU.mult,
                                                   accum_out=tied[:, o, bass.ds(t, 1)])
                dve.wait_ge(picked_ready, t + 1)
                for o in range(2):
                    m = nc.vector.scalar_tensor_tensor(scrap[s][:, 2 + o, :], ps_pick[s][:, o, :], 1.0,
                                                       g.hot_lo[:, o, bass.ds(t, 1), :].rearrange("p a b -> p (a b)"),
                                                       ALU.mult, ALU.mult, accum_out=picked[:, o, bass.ds(t, 1)])
                m.then_inc(tile_done, 1)
                dve.wait_ge(running_ready, t + 2)

            tile_loop(dve, ET, step)
            dve.wait_ge(tile_done, ET)
            nc.vector.tensor_tensor(g.position[:, :, :], picked[:, :, :], tied[:, :, :], ALU.add)
            link(nc.vector.tensor_scalar(empty[:, :, :], total[:, :, :], 0.5, float(SKIP), ALU.is_lt, ALU.mult))
            link(nc.vector.tensor_tensor(upto[:, :, :], upto[:, :, :], empty[:, :, :], ALU.add))
            for o in range(2):
                nc.vector.tensor_scalar(g.ntab[:, :, o], upto[:, o, :], 1.0, None, ALU.subtract)
            m = nc.vector.memset(g.ntab[:, :, 3], 0.0)
            m.then_inc(cols_ready, 1)
            dve.wait_ge(cols_ready, 2)
            link(nc.vector.reciprocal(root[:, 0, :], ndeg[:, :]))
            link(nc.vector.tensor_tensor(root[:, 1, :], root[:, 0, :], root[:, 0, :], ALU.mult))
            link(nc.vector.scalar_tensor_tensor(root[:, 2, :], total[:, 1, :], 1.0, root[:, 1, :], ALU.add, ALU.mult))
            link(nc.vector.tensor_scalar(root[:, 3, :], root[:, 2, :], -0.5, 1.5, ALU.mult, ALU.add))
            nc.vector.tensor_tensor(g.ntab[:, :, 2], root[:, 0, :], root[:, 3, :], ALU.mult).then_inc(table_ready, 1)
            dve.wait_ge(turned, 1)
            nc.vector.tensor_copy(g.node_row[:, 0, :], ps_key[0][:, 0, 0:NT])
            nc.vector.tensor_copy(g.node_row[:, 1, :], ps_key[0][:, 1, 0:NT])
            nc.vector.tensor_copy(g.dis[:, :], ps_key[0][:, 2, 0:NT])

        @block.sync
        def _(sp):
            sp.wait_ge(table_ready, 1)
            sp.dma_start(g.ntab_dram.rearrange("(h l) c -> h l c", l=P), g.ntab[:, :, :]).then_inc(stored, 16)
            sp.wait_ge(stored, 16)


def permute_edges(nc, g):
    SL = 4
    with ExitStack() as ctx:
        sb = lambda n, s, d=F32: ctx.enter_context(nc.sbuf_tensor(n, s, d))
        sem = lambda n: nc.alloc_semaphore(n)
        rec_out, pos_out = sb("rec_out", [P, 2, SL, REC]), sb("pos_out", [P, 2, SL], I32)
        key_diag = [sb(f"sorted_diag{s}", [P, P]) for s in range(2)]
        ps_row = [ctx.enter_context(nc.psum_tensor(f"ps_row{s}", [P, D], F32)) for s in range(2)]
        scattered = [[sem(f"pe_scattered{o}{s}") for s in range(SL)] for o in range(2)]
        staged, reloaded, ids_ready = sem("pe_staged"), sem("pe_reloaded"), sem("pe_ids_ready")
        diag_ready, row_ready, row_copied = sem("pe_diag_ready"), sem("pe_row_ready"), sem("pe_row_copied")
        tab_slot, tab_idx = sb("tab_slot", [P, SL, 4]), sb("tab_idx", [P, SL], I32)
        tab_got = [sem(f"pe_tab_got{s}") for s in range(SL)]
        held = sem("pe_held")
        tab_staged, tab_kept = sem("pe_tab_staged"), sem("pe_tab_kept")
        block = ctx.enter_context(nc.Block())

        @block.gpsimd
        def _(pool):
            def scatter(i):
                for o in range(2):
                    hold(pool, staged, i * 2 * SL + (o + 1) * SL, held)
                    for s in range(SL):
                        nc.gpsimd.indirect_dma_start(
                            g.rec_dram[o], bass.IndirectOffsetOnAxis(pos_out[:, o, s:s + 1], 0),
                            rec_out[:, o, s, :], None, bounds_check=last_edge, oob_is_err=False)\
                          .then_inc(scattered[o][s], 16)

            last_edge, last_node = pool.to_reg(EPAD - 1), pool.to_reg(NT * P - 1)
            with pool.Fori(0, ET // SL) as i:
                scatter(i)

            def look_up(i):
                hold(pool, tab_staged, i * SL + SL, held)
                for s in range(SL):
                    nc.gpsimd.indirect_dma_start(
                        tab_slot[:, s, :], None, g.ntab_dram, bass.IndirectOffsetOnAxis(tab_idx[:, s:s + 1], 0),
                        bounds_check=last_node, oob_is_err=False).then_inc(tab_got[s], 16)

            with pool.Fori(0, ET // SL) as i:
                look_up(i)

        @block.sync
        def _(sp):
            for o in range(2):
                for s in range(SL):
                    sp.wait_ge(scattered[o][s], ET // SL * 16)
            for o in range(2):
                sp.dma_start(g.rec[o][:, :, :], g.rec_dram[o].rearrange("(t p) c -> p t c", p=P)).then_inc(reloaded, 16)

        @block.vector
        def _(dve):
            def stage(i):
                for o in range(2):
                    for s in range(SL):
                        if not isinstance(i, int):
                            dve.wait_ge(scattered[o][s], i * 16)
                        nc.vector.tensor_scalar(rec_out[:, o, s, :],
                                                g.rec_in[:, bass.ds(i * SL + s, 1), :].rearrange("p a b -> p (a b)"),
                                                0.0, None, ALU.add)
                        nc.vector.tensor_scalar(pos_out[:, o, s:s + 1], g.position[:, o, bass.ds(i * SL + s, 1)],
                                                0.0, None, ALU.add).then_inc(staged, 1)

            stage(0)
            with dve.Fori(1, ET // SL) as i:
                stage(i)
            dve.wait_ge(reloaded, 32)
            for o in range(2):
                nc.vector.tensor_copy(g.src_any[:, o, :], g.rec[o][:, :, 0])
                nc.vector.tensor_scalar(g.src_row[:, o, :], g.rec[o][:, :, 0], float(N - 1), None, ALU.min)
                nc.vector.tensor_scalar(g.dst_row[:, o, :], g.rec[o][:, :, 1], float(N - 1), None, ALU.min)
                nc.vector.memset(g.prev_last[:, o, 0:1], -1.0)
                nc.vector.tensor_scalar(g.prev_last[:, o, 1:ET], g.rec[o][:, 0:ET - 1, o], 1.0,
                                        g.last_row[:, 0:1], ALU.add, ALU.mult)
            nc.vector.memset(g.eps_col[:, :], 1e-5).then_inc(ids_ready, 1)
            dve.wait_ge(ids_ready, 1)
            for o in range(2):
                nc.vector.tensor_scalar(g.prev_last[:, o, 1:ET], g.prev_last[:, o, 1:ET], 1.0, None, ALU.subtract).then_inc(ids_ready, 1)

            def look_up(i):
                for s in range(SL):
                    nc.vector.tensor_scalar(tab_idx[:, s:s + 1], g.src_any[:, 1, bass.ds(i * SL + s, 1)],
                                            0.0, None, ALU.add).then_inc(tab_staged, 1)
                for s in range(SL):
                    dve.wait_ge(tab_got[s], i * 16 + 16)
                    nc.vector.tensor_scalar(g.src_tab[:, bass.ds(i * SL + s, 1), :].rearrange("p a b -> p (a b)"),
                                            tab_slot[:, s, :], 0.0, None, ALU.add).then_inc(tab_kept, 1)

            dve.wait_ge(ids_ready, 3)
            with dve.Fori(0, ET // SL) as i:
                look_up(i)
            dve.wait_ge(tab_kept, ET)
            nc.vector.tensor_copy(g.src_comp[:, :, :], g.src_tab[:, :, 0:2].rearrange("p t o -> p o t"))

        @block.scalar
        def _(act):
            act.wait_ge(reloaded, 32)
            for o in range(2):
                def step(t, s, first, last, o=o):
                    if not (first and o == 0):
                        act.wait_ge(row_ready, t + o * ET - 1)
                    nc.scalar.activation(key_diag[s][:, :], g.ident[:, :], ACT.Copy,
                                         scale=g.rec[o][:, bass.ds(t, 1), o]).then_inc(diag_ready, 1)
                    act.wait_ge(row_ready, t + o * ET + 1)
                    nc.scalar.activation(g.key_row[:, o, bass.ds(t * P, P)], ps_row[s][:, 0:P], ACT.Copy)\
                       .then_inc(row_copied, 1)

                tile_loop(act, ET, step)

        @block.tensor
        def _(pe):
            for o in range(2):
                def step(t, s, first, last, o=o):
                    pe.wait_ge(diag_ready, t + o * ET + 1)
                    if not (first and o == 0):
                        pe.wait_ge(row_copied, t + o * ET - 1)
                    nc.tensor.matmul(ps_row[s][:, 0:P], g.ones[:, :], key_diag[s][:, :], start=True, stop=True)\
                      .then_inc(row_ready, 1)

                tile_loop(pe, ET, step)


def load_split(nc, weights):
    with ExitStack() as ctx:
        names = [w[0] for w in weights]
        full = [ctx.enter_context(nc.sbuf_tensor(f"full_{n}", list(hi.shape), F32)) for n, _, hi, _ in weights]
        loaded = [nc.alloc_semaphore(f"ls_loaded_{n}") for n in names]
        high = nc.alloc_semaphore(f"ls_high_{names[0]}")
        low = nc.alloc_semaphore(f"ls_low_{names[0]}")
        block = ctx.enter_context(nc.Block())

        @block.sync
        def _(sp):
            for (_, src, _, _), f, sem in zip(weights, full, loaded):
                sp.dma_start(f[:, :, :], src).then_inc(sem, 16)

        @block.scalar
        def _(act):
            for (_, _, hi, _), f, sem in zip(weights, full, loaded):
                act.wait_ge(sem, 16)
                nc.scalar.activation(hi[:, :, :], f[:, :, :], ACT.Copy).then_inc(high, 1)

        @block.vector
        def _(dve):
            for k, ((_, _, hi, lo), f, sem) in enumerate(zip(weights, full, loaded)):
                dve.wait_ge(sem, 16)
                dve.wait_ge(high, k + 1)
                nc.vector.tensor_tensor(lo[:, :, :], f[:, :, :], hi[:, :, :].bitcast(F32), ALU.subtract)\
                  .then_inc(low, 1)


def split_weight(nc, ctx, name, src, k, n):
    hi = ctx.enter_context(nc.sbuf_tensor(f"{name}_hi", [P, k, n], F32R))
    lo = ctx.enter_context(nc.sbuf_tensor(f"{name}_lo", [P, k, n], F32R))
    return (name, src.rearrange("(k p) n -> p k n", p=P), hi, lo)


def edge_sums(nc, g, tag, rows, out, comp=None, comp_order=0, bias=None, by_degree=False, normed=True):
    with ExitStack() as ctx:
        sb = lambda n, s, d=F32: ctx.enter_context(nc.sbuf_tensor(f"{tag}_{n}", s, d))
        sem = lambda n: nc.alloc_semaphore(f"{tag}_{n}")
        x = [sb(f"x{s}", [P, D]) for s in range(K)]
        same = [sb(f"same{s}", [P, P]) for s in range(K)]
        carry = [sb(f"carry{s}", [P, P]) for s in range(K)]
        sums = [sb(f"sums{s}", [P, D]) for s in range(K)]
        row_idx = sb("row_idx", [P, K], I32)
        ps = [ctx.enter_context(nc.psum_tensor(f"{tag}_ps{s}", [P, D], F32)) for s in range(K)]
        m = x
        if normed:
            c = [sb(f"c{s}", [P, D]) for s in range(K)]
            comp_idx = sb("comp_idx", [P, K], I32)
            pre = [sb(f"pre{s}", [P, D]) for s in range(K)]
            m = [sb(f"m{s}", [P, D]) for s in range(K)]
            stats, mv = sb("stats", [P, K, 6]), sb("mv", [P, K, 2])
            std, rstd, shift = sb("std", [P, K]), sb("rstd", [P, K]), sb("shift", [P, K])
            rdis = sb("rdis", [P, K])
            if bias is not None:
                bias_row = sb("bias_row", [P, D])
        got_x, got_c = [sem(f"got_x{s}") for s in range(K)], [sem(f"got_c{s}") for s in range(K)]
        stored = [sem(f"stored{s}") for s in range(K)]
        ready, held = sem("slot_ready"), sem("held")
        added, measured, var_ready, std_ready = sem("added"), sem("measured"), sem("var_ready"), sem("std_ready")
        inverted, coef_ready, m_ready, masks_ready = sem("inverted"), sem("coef_ready"), sem("m_ready"), sem("masks_ready")
        summed, emptied = sem("summed"), sem("emptied")
        scaled, biased, bias_in = sem("scaled"), sem("biased"), sem("bias_in")
        block = ctx.enter_context(nc.Block())

        @block.gpsimd
        def _(pool):
            last_row, last_sum = pool.to_reg(N - 1), pool.to_reg(EPAD - 1)

            def step(i, s):
                t = i * K + s
                if later(i) and not normed:
                    pool.wait_ge(summed, t - K + 1)
                hold(pool, ready, t + 1, held)
                nc.gpsimd.indirect_dma_start(x[s][:, :], None, rows, bass.IndirectOffsetOnAxis(row_idx[:, s:s + 1], 0),
                                             bounds_check=last_row, oob_is_err=False).then_inc(got_x[s], 16)
                if normed:
                    nc.gpsimd.indirect_dma_start(c[s][:, :], None, comp,
                                                 bass.IndirectOffsetOnAxis(comp_idx[:, s:s + 1], 0),
                                                 bounds_check=last_sum, oob_is_err=False).then_inc(got_c[s], 16)

            rounds(pool, ET, step)

        @block.vector
        def _(dve):
            def stage(t, s):
                if normed:
                    nc.vector.memset(c[s][:, :], 0.0)
                    nc.vector.tensor_scalar(comp_idx[:, s:s + 1], g.src_comp[:, comp_order, bass.ds(t, 1)],
                                            0.0, None, ALU.add)
                nc.vector.tensor_scalar(row_idx[:, s:s + 1], g.src_row[:, 1, bass.ds(t, 1)], 0.0, None, ALU.add)\
                  .then_inc(ready, 1)

            def coefs(i, s):
                t = i * K + s
                dve.wait_ge(std_ready, t + 1)
                nc.vector.reciprocal(rstd[:, s:s + 1], std[:, s:s + 1]).then_inc(inverted, 1)
                dve.wait_ge(inverted, t + 1)
                if by_degree:
                    nc.vector.tensor_scalar(rdis[:, s:s + 1], rstd[:, s:s + 1], g.src_tab[:, bass.ds(t, 1), 2],
                                            None, ALU.mult).then_inc(scaled, 1)
                    dve.wait_ge(scaled, t + 1)
                r = rdis if by_degree else rstd
                nc.vector.tensor_scalar(shift[:, s:s + 1], mv[:, s, 0:1], r[:, s:s + 1], -1.0,
                                        ALU.mult, ALU.mult).then_inc(coef_ready, 1)

            for s in range(K):
                stage(s, s)
            if bias is not None:
                dve.wait_ge(bias_in, 16)

            def step(i, s):
                t = i * K + s
                dve.wait_ge(got_x[s], i * 16 + 16)
                if normed:
                    dve.wait_ge(got_c[s], i * 16 + 16)
                    if later(i):
                        dve.wait_ge(m_ready, t - K + 1)
                    if bias is not None:
                        nc.vector.tensor_tensor(c[s][:, :], c[s][:, :], bias_row[:, :], ALU.add).then_inc(biased, 1)
                        dve.wait_ge(biased, t + 1)
                    nc.vector.tensor_tensor(pre[s][:, :], x[s][:, :], c[s][:, :], ALU.add).then_inc(added, 1)
                    dve.wait_ge(added, t + 1)
                    nc.vector.bn_stats(stats[:, s, :], pre[s][:, :]).then_inc(measured, 1)
                if not (isinstance(t, int) and t + K >= ET):
                    stage(t + K, s)
                if later(i):
                    dve.wait_ge(summed, t - K + 1)
                if normed:
                    dve.wait_ge(measured, t + 1)
                nc.vector.tensor_scalar(same[s][:, :], g.key_row[:, 1, bass.ds(t * P, P)],
                                        g.rec[1][:, bass.ds(t, 1), 1], None, ALU.is_equal)
                nc.vector.tensor_scalar(carry[s][:, :], g.key_row[:, 1, bass.ds(t * P, P)],
                                        g.prev_last[:, 1, bass.ds(t, 1)], None, ALU.is_equal).then_inc(masks_ready, 1)
                if normed:
                    nc.vector.bn_aggr(mv[:, s, :], stats[:, s, :]).then_inc(var_ready, 1)
                    if exists(back(i, s, 1)[0]):
                        coefs(*back(i, s, 1))

            rounds(dve, ET, step)
            if normed:
                coefs(ET // K - 1, K - 1)

        @block.scalar
        def _(act):
            def apply(i, s):
                t = i * K + s
                act.wait_ge(coef_ready, t + 1)
                if later(i):
                    act.wait_ge(summed, t - K + 1)
                nc.scalar.activation(m[s][:, :], pre[s][:, :], ACT.Identity, bias=shift[:, s:s + 1],
                                     scale=(rdis if by_degree else rstd)[:, s:s + 1]).then_inc(m_ready, 1)

            def empty(i, s):
                act.wait_ge(summed, i * K + s + 1)
                if later(i):
                    act.wait_ge(stored[s], i * 16)
                nc.scalar.activation(sums[s][:, :], ps[s][:, :], ACT.Copy).then_inc(emptied, 1)

            def step(i, s):
                t = i * K + s
                if normed:
                    act.wait_ge(var_ready, t + 1)
                    nc.scalar.activation(std[:, s:s + 1], mv[:, s, 1:2], ACT.Sqrt, bias=g.eps_col[:, :])\
                       .then_inc(std_ready, 1)
                    if exists(back(i, s, 1)[0]):
                        apply(*back(i, s, 1))
                    if exists(back(i, s, 2)[0]):
                        empty(*back(i, s, 2))
                else:
                    empty(i, s)

            rounds(act, ET, step)
            if normed:
                apply(ET // K - 1, K - 1)
                empty(ET // K - 1, K - 2)
                empty(ET // K - 1, K - 1)

        @block.tensor
        def _(pe):
            def step(i, s):
                t = i * K + s
                pe.wait_ge(masks_ready, t + 1)
                if normed:
                    pe.wait_ge(m_ready, t + 1)
                else:
                    pe.wait_ge(got_x[s], i * 16 + 16)
                if later(i):
                    pe.wait_ge(emptied, t - K + 1)
                alone = isinstance(t, int) and t == 0
                last = nc.tensor.matmul(ps[s][:, :], same[s][:, :], m[s][:, :], start=True, stop=alone)
                if not alone:
                    pe.wait_ge(emptied, t)
                    last = nc.tensor.matmul(ps[s][:, :], carry[s][:, :], sums[s - 1][:, :], start=False, stop=True)
                last.then_inc(summed, 1)

            rounds(pe, ET, step)

        @block.sync
        def _(sp):
            if bias is not None:
                sp.dma_start(bias_row[:, :], bias.rearrange("(a n) -> a n", a=1).to_broadcast([P, D])).then_inc(bias_in, 16)

            def step(i, s):
                t = i * K + s
                sp.wait_ge(emptied, t + 1)
                sp.dma_start(out[bass.ds(t * P, P), :], sums[s][:, :]).then_inc(stored[s], 16)

            rounds(sp, ET, step)
            for s in range(K):
                sp.wait_ge(stored[s], ET // K * 16)


BIG = 3.0e38
HEADS = 8
DK = D // HEADS


def edge_logits(nc, g, x, weights, biases, v_dram):
    with ExitStack() as ctx:
        sb = lambda n, s, d=F32: ctx.enter_context(nc.sbuf_tensor(f"el_{n}", s, d))
        pb = lambda n, s: ctx.enter_context(nc.psum_tensor(f"el_{n}", s, F32))
        sem = lambda n: nc.alloc_semaphore(f"el_{n}")
        split = [split_weight(nc, ctx, n, w, KC, D) for n, w in zip(("wq", "wk", "wv"), weights)]
        load_split(nc, split)
        (_, _, wq_hi, wq_lo), (_, _, wk_hi, wk_lo), (_, _, wv_hi, wv_lo) = split
        xs, xd = [sb(f"xs{s}", [P, D]) for s in range(K)], [sb(f"xd{s}", [P, D]) for s in range(K)]
        xT_hi = [[sb(f"xT_hi{w}{s}", [P, KC, P], F32R) for s in range(2)] for w in range(2)]
        xT_lo = [[sb(f"xT_lo{w}{s}", [P, KC, P], F32R) for s in range(2)] for w in range(2)]
        q, k, prod = [sb(f"q{s}", [P, D]) for s in range(2)], [sb(f"k{s}", [P, D]) for s in range(2)], [sb(f"qk{s}", [P, D]) for s in range(2)]
        v = [sb(f"v{s}", [P, D]) for s in range(K)]
        bias = [sb(f"bias{n}", [P, D]) for n in range(3)]
        dots, logit = sb("dots", [P, K, HEADS]), sb("logit", [P, K, HEADS])
        idx = sb("idx", [P, 2, K], I32)
        psT = [pb(f"psT{w}", [P, KC, P]) for w in range(2)]
        psq, psk, psv, psL = [pb(f"psq{s}", [P, D]) for s in range(2)], [pb(f"psk{s}", [P, D]) for s in range(2)], pb("psv", [P, D]), pb("psL", [HEADS, P])
        got = [[sem(f"got{w}{s}") for s in range(K)] for w in range(2)]
        ready, held, bias_in = sem("slot_ready"), sem("held"), sem("bias_in")
        turned, high, low = sem("turned"), sem("high"), sem("low")
        q_done, k_done, v_done = sem("q_done"), sem("k_done"), sem("v_done")
        q_out, k_out, v_out, multiplied, reduced = sem("q_out"), sem("k_out"), sem("v_out"), sem("multiplied"), sem("reduced")
        logit_ready, logit_turned, logit_kept = sem("logit_ready"), sem("logit_turned"), sem("logit_kept")
        stored = [sem(f"stored{s}") for s in range(K)]
        block = ctx.enter_context(nc.Block())

        @block.gpsimd
        def _(pool):
            last_row = pool.to_reg(N - 1)

            def step(i, s):
                t = i * K + s
                if later(i):
                    pool.wait_ge(turned, t - K + 1)
                hold(pool, ready, t + 1, held)
                for w, x_w in enumerate((xs, xd)):
                    nc.gpsimd.indirect_dma_start(x_w[s][:, :], None, x,
                                                 bass.IndirectOffsetOnAxis(idx[:, w, s:s + 1], 0),
                                                 bounds_check=last_row, oob_is_err=False).then_inc(got[w][s], 16)

            rounds(pool, ET, step)

        @block.tensor
        def _(pe):
            def project(i, s):
                t, h = i * K + s, s % 2
                pe.wait_ge(low, t + 1)
                for ps, w, (hi, lo), done, out in ((psq[h], 0, (wq_hi, wq_lo), q_done, q_out),
                                                   (psk[h], 1, (wk_hi, wk_lo), k_done, k_out),
                                                   (psv, 1, (wv_hi, wv_lo), v_done, v_out)):
                    if ps is psv:
                        if exists(back(i, s, 1)[0]):
                            pe.wait_ge(out, t)
                    elif exists(back(i, s, 2)[0]):
                        pe.wait_ge(out, t - 1)
                    n = 0
                    for a, b in ((xT_hi, hi), (xT_hi, lo), (xT_lo, hi)):
                        for c in range(KC):
                            last = nc.tensor.matmul(ps[:, :], a[w][h][:, c, :], b[:, c, :], start=n == 0,
                                                    stop=n == 3 * KC - 1)
                            n += 1
                    last.then_inc(done, 1)

            def turn_logits(i, s):
                t = i * K + s
                pe.wait_ge(logit_ready, t + 1)
                if not (isinstance(t, int) and t == 0):
                    pe.wait_ge(logit_kept, t)
                nc.tensor.transpose(psL[:, :], logit[:, s, :], g.ident[:, :]).then_inc(logit_turned, 1)

            def step(i, s):
                t = i * K + s
                for w, x_w in enumerate((xs, xd)):
                    pe.wait_ge(got[w][s], i * 16 + 16)
                if not (isinstance(t, int) and t == 0):
                    pe.wait_ge(low, t)
                for w, x_w in enumerate((xs, xd)):
                    for c in range(KC):
                        last = nc.tensor.transpose(psT[w][:, c, :], x_w[s][:, c * P:(c + 1) * P], g.ident[:, :])
                last.then_inc(turned, 1)
                if exists(back(i, s, 1)[0]):
                    project(*back(i, s, 1))
                if exists(back(i, s, 2)[0]):
                    turn_logits(*back(i, s, 2))

            rounds(pe, ET, step)
            project(ET // K - 1, K - 1)
            turn_logits(ET // K - 1, K - 2)
            turn_logits(ET // K - 1, K - 1)

        @block.scalar
        def _(act):
            def keep_logits(i, s):
                t = i * K + s
                act.wait_ge(logit_turned, t + 1)
                nc.scalar.activation(g.logits_T[:, bass.ds(t * P, P)], psL[:, :], ACT.Copy).then_inc(logit_kept, 1)

            def step(i, s):
                t = i * K + s
                act.wait_ge(turned, t + 1)
                if exists(back(i, s, 2)[0]):
                    act.wait_ge(v_done, t - 1)
                for w in range(2):
                    last = nc.scalar.activation(xT_hi[w][s % 2][:, :, :], psT[w][:, :, :], ACT.Copy)
                last.then_inc(high, 1)
                if exists(back(i, s, 3)[0]):
                    keep_logits(*back(i, s, 3))

            rounds(act, ET, step)
            for b in range(3, 0, -1):
                keep_logits(ET // K - 1, K - b)

        @block.vector
        def _(dve):
            def stage(t, s):
                nc.vector.tensor_scalar(idx[:, 0, s:s + 1], g.src_row[:, 0, bass.ds(t, 1)], 0.0, None, ALU.add)
                nc.vector.tensor_scalar(idx[:, 1, s:s + 1], g.dst_row[:, 0, bass.ds(t, 1)], 0.0, None, ALU.add)\
                  .then_inc(ready, 1)

            for s in range(K):
                stage(s, s)
            dve.wait_ge(bias_in, 48)

            def finish(i, s):
                t, h = i * K + s, s % 2
                dve.wait_ge(q_done, t + 1)
                if exists(back(i, s, 2)[0]):
                    dve.wait_ge(multiplied, t - 1)
                nc.vector.tensor_tensor(q[h][:, :], psq[h][:, :], bias[0][:, :], ALU.add).then_inc(q_out, 1)
                dve.wait_ge(k_done, t + 1)
                nc.vector.tensor_tensor(k[h][:, :], psk[h][:, :], bias[1][:, :], ALU.add).then_inc(k_out, 1)
                dve.wait_ge(k_out, t + 1)
                dve.wait_ge(q_out, t + 1)
                if exists(back(i, s, 2)[0]):
                    dve.wait_ge(reduced, t - 1)
                nc.vector.tensor_tensor(prod[h][:, :], q[h][:, :], k[h][:, :], ALU.mult).then_inc(multiplied, 1)
                dve.wait_ge(v_done, t + 1)
                if later(i):
                    dve.wait_ge(stored[s], i * 16)
                nc.vector.tensor_tensor(v[s][:, :], psv[:, :], bias[2][:, :], ALU.add).then_inc(v_out, 1)
                dve.wait_ge(multiplied, t + 1)
                if later(i):
                    dve.wait_ge(logit_ready, t - K + 1)
                nc.vector.tensor_reduce(dots[:, s, :], prod[h][:, :].rearrange("p (h d) -> p h d", h=HEADS),
                                        AX.X, ALU.add).then_inc(reduced, 1)
                dve.wait_ge(reduced, t + 1)
                if later(i):
                    dve.wait_ge(logit_turned, t - K + 1)
                nc.vector.scalar_tensor_tensor(logit[:, s, :], dots[:, s, :], float(DK) ** -0.5,
                                               g.rec[0][:, bass.ds(t, 1), 6:14].rearrange("p a b -> p (a b)"),
                                               ALU.mult, ALU.add).then_inc(logit_ready, 1)

            def step(i, s):
                t = i * K + s
                dve.wait_ge(high, t + 1)
                for w in range(2):
                    last = nc.vector.tensor_tensor(xT_lo[w][s % 2][:, :, :], psT[w][:, :, :],
                                                   xT_hi[w][s % 2][:, :, :].bitcast(F32), ALU.subtract)
                last.then_inc(low, 1)
                if not (isinstance(t, int) and t + K >= ET):
                    dve.wait_ge(got[0][s], i * 16 + 16)
                    dve.wait_ge(got[1][s], i * 16 + 16)
                    stage(t + K, s)
                if exists(back(i, s, 1)[0]):
                    finish(*back(i, s, 1))

            rounds(dve, ET, step)
            finish(ET // K - 1, K - 1)

        @block.sync
        def _(sp):
            for b, src in zip(bias, biases):
                sp.dma_start(b[:, :], src.rearrange("(a n) -> a n", a=1).to_broadcast([P, D])).then_inc(bias_in, 16)

            def step(i, s):
                t = i * K + s
                sp.wait_ge(v_out, t + 1)
                sp.dma_start(v_dram[bass.ds(t * P, P), :], v[s][:, :]).then_inc(stored[s], 16)

            rounds(sp, ET, step)
            for s in range(K):
                sp.wait_ge(stored[s], ET // K * 16)


def edge_softmax(nc, g):
    with ExitStack() as ctx:
        sb = lambda n, s, d=F32: ctx.enter_context(nc.sbuf_tensor(f"es_{n}", s, d))
        sem = lambda n: nc.alloc_semaphore(f"es_{n}")
        joined, gap = sb("joined", [HEADS, EPAD + 1]), sb("gap", [HEADS, EPAD + 1])
        upto, top = sb("upto", [HEADS, EPAD]), sb("top", [HEADS, EPAD])
        p, after = sb("p", [HEADS, EPAD]), sb("after", [HEADS, EPAD])
        ps = ctx.enter_context(nc.psum_tensor("es_ps", [P, ET, HEADS], F32))
        chain, centred, expd, att_ready, turned = sem("chain"), sem("centred"), sem("expd"), sem("att_ready"), sem("turned")
        block = ctx.enter_context(nc.Block())
        backwards = lambda ap: ap[:, ::-1]

        @block.vector
        def _(dve):
            n_chain = [0]

            def link(ins):
                n_chain[0] += 1
                ins.then_inc(chain, 1)
                dve.wait_ge(chain, n_chain[0])

            nc.vector.memset(joined[:, 0:1], 0.0)
            nc.vector.memset(joined[:, EPAD:EPAD + 1], 0.0)
            link(nc.vector.tensor_tensor(joined[:, 1:EPAD], g.key_row[0:HEADS, 0, 1:EPAD],
                                         g.key_row[0:HEADS, 0, 0:EPAD - 1], ALU.is_equal))
            link(nc.vector.tensor_scalar(gap[:, :], joined[:, :], 1.0, BIG, ALU.subtract, ALU.mult))
            link(nc.vector.tensor_tensor_scan(upto[:, :], gap[:, 0:EPAD], g.logits_T[:, :], -BIG, ALU.add, ALU.max))
            link(nc.vector.tensor_tensor_scan(backwards(top), backwards(gap[:, 1:EPAD + 1]), backwards(upto),
                                              -BIG, ALU.add, ALU.max))
            nc.vector.tensor_tensor(p[:, :], g.logits_T[:, :], top[:, :], ALU.subtract).then_inc(centred, 1)
            dve.wait_ge(expd, 1)
            nc.vector.tensor_tensor_scan(upto[:, :], joined[:, 0:EPAD], p[:, :], 0.0, ALU.mult, ALU.add)
            link(nc.vector.tensor_tensor_scan(backwards(after), backwards(joined[:, 1:EPAD + 1]), backwards(p),
                                              0.0, ALU.mult, ALU.add))
            link(nc.vector.tensor_tensor(after[:, :], after[:, :], p[:, :], ALU.subtract))
            link(nc.vector.tensor_tensor(top[:, :], upto[:, :], after[:, :], ALU.add))
            link(nc.vector.reciprocal(after[:, :], top[:, :]))
            nc.vector.tensor_tensor(upto[:, :], p[:, :], after[:, :], ALU.mult).then_inc(att_ready, 1)
            dve.wait_ge(turned, 1)
            nc.vector.tensor_copy(g.att[:, :, :], ps[:, :, :])

        @block.scalar
        def _(act):
            act.wait_ge(centred, 1)
            nc.scalar.activation(p[:, :], p[:, :], ACT.Exp).then_inc(expd, 1)

        @block.tensor
        def _(pe):
            pe.wait_ge(att_ready, 1)
            for t in range(ET):
                last = nc.tensor.transpose(ps[:, t, :], upto[:, t * P:(t + 1) * P], g.ident[0:HEADS, 0:HEADS])
            last.then_inc(turned, 1)


def edge_attend(nc, g, v_dram, wo, out):
    with ExitStack() as ctx:
        sb = lambda n, s, d=F32: ctx.enter_context(nc.sbuf_tensor(f"ea_{n}", s, d))
        sem = lambda n: nc.alloc_semaphore(f"ea_{n}")
        split = split_weight(nc, ctx, "wo", wo, KC, D)
        load_split(nc, [split])
        _, _, wo_hi, wo_lo = split
        v, av = [sb(f"v{s}", [P, D]) for s in range(K)], [sb(f"av{s}", [P, D]) for s in range(K)]
        same, carry = [sb(f"same{s}", [P, P]) for s in range(K)], [sb(f"carry{s}", [P, P]) for s in range(K)]
        y_hi, y_lo = [sb(f"y_hi{s}", [P, KC, P], F32R) for s in range(2)], [sb(f"y_lo{s}", [P, KC, P], F32R) for s in range(2)]
        sums = [sb(f"sums{s}", [P, D]) for s in range(K)]
        psY = [ctx.enter_context(nc.psum_tensor(f"ea_psY{s}", [P, KC, P], F32)) for s in range(2)]
        ps = [ctx.enter_context(nc.psum_tensor(f"ea_ps{s}", [P, D], F32)) for s in range(K)]
        loaded, stored = [sem(f"loaded{s}") for s in range(K)], [sem(f"stored{s}") for s in range(K)]
        weighed, masks_ready, y_done, high, low = sem("weighed"), sem("masks_ready"), sem("y_done"), sem("high"), sem("low")
        summed, emptied = sem("summed"), sem("emptied")
        block = ctx.enter_context(nc.Block())

        @block.sync
        def _(sp):
            def load(i, s):
                if later(i):
                    sp.wait_ge(weighed, i * K + s - K + 1)
                sp.dma_start(v[s][:, :], v_dram[bass.ds((i * K + s) * P, P), :]).then_inc(loaded[s], 16)

            def store(i, s):
                sp.wait_ge(emptied, i * K + s + 1)
                sp.dma_start(out[bass.ds((i * K + s) * P, P), :], sums[s][:, :]).then_inc(stored[s], 16)

            for s in range(K - 1):
                load(0, s)

            def step(i, s):
                t = i * K + s
                if not (isinstance(t, int) and t + K - 1 >= ET):
                    load(*((i, K - 1) if s == 0 else (i + 1, s - 1)))
                store(i, s)

            rounds(sp, ET, step)
            for s in range(K):
                sp.wait_ge(stored[s], ET // K * 16)

        @block.vector
        def _(dve):
            def lows(i, s):
                dve.wait_ge(high, i * K + s + 1)
                nc.vector.tensor_tensor(y_lo[s % 2][:, :, :], psY[s % 2][:, :, :], y_hi[s % 2][:, :, :].bitcast(F32),
                                        ALU.subtract).then_inc(low, 1)

            def step(i, s):
                t = i * K + s
                dve.wait_ge(loaded[s], i * 16 + 16)
                if later(i):
                    dve.wait_ge(summed, t - K + 1)
                nc.vector.tensor_tensor(av[s][:, :].rearrange("p (h d) -> p h d", h=HEADS),
                                        v[s][:, :].rearrange("p (h d) -> p h d", h=HEADS),
                                        g.att[:, bass.ds(t, 1), :].rearrange("p a b -> p (a b)").unsqueeze(2)
                                        .to_broadcast([P, HEADS, DK]), ALU.mult).then_inc(weighed, 1)
                nc.vector.tensor_scalar(same[s][:, :], g.key_row[:, 0, bass.ds(t * P, P)],
                                        g.rec[0][:, bass.ds(t, 1), 0], None, ALU.is_equal)
                nc.vector.tensor_scalar(carry[s][:, :], g.key_row[:, 0, bass.ds(t * P, P)],
                                        g.prev_last[:, 0, bass.ds(t, 1)], None, ALU.is_equal).then_inc(masks_ready, 1)
                if exists(back(i, s, 1)[0]):
                    lows(*back(i, s, 1))

            rounds(dve, ET, step)
            lows(ET // K - 1, K - 1)

        @block.scalar
        def _(act):
            def empty(i, s):
                act.wait_ge(summed, i * K + s + 1)
                if later(i):
                    act.wait_ge(stored[s], i * 16)
                nc.scalar.activation(sums[s][:, :], ps[s][:, :], ACT.Copy).then_inc(emptied, 1)

            def step(i, s):
                t = i * K + s
                act.wait_ge(y_done, t + 1)
                if exists(back(i, s, 2)[0]):
                    act.wait_ge(summed, t - 1)
                nc.scalar.activation(y_hi[s % 2][:, :, :], psY[s % 2][:, :, :], ACT.Copy).then_inc(high, 1)
                if exists(back(i, s, 1)[0]):
                    empty(*back(i, s, 1))

            rounds(act, ET, step)
            empty(ET // K - 1, K - 1)

        @block.tensor
        def _(pe):
            def project(i, s):
                t, h = i * K + s, s % 2
                pe.wait_ge(low, t + 1)
                if later(i):
                    pe.wait_ge(emptied, t - K + 1)
                alone = isinstance(t, int) and t == 0
                n = 0
                for a, b in ((y_hi, wo_hi), (y_hi, wo_lo), (y_lo, wo_hi)):
                    for c in range(KC):
                        last = nc.tensor.matmul(ps[s][:, :], a[h][:, c, :], b[:, c, :], start=n == 0,
                                                stop=alone and n == 3 * KC - 1)
                        n += 1
                if not alone:
                    pe.wait_ge(emptied, t)
                    last = nc.tensor.matmul(ps[s][:, :], carry[s][:, :], sums[s - 1][:, :], start=False, stop=True)
                last.then_inc(summed, 1)

            def step(i, s):
                t, h = i * K + s, s % 2
                pe.wait_ge(masks_ready, t + 1)
                if exists(back(i, s, 2)[0]):
                    pe.wait_ge(low, t - 1)
                for c in range(KC):
                    last = nc.tensor.matmul(psY[h][:, c, :], av[s][:, c * P:(c + 1) * P], same[s][:, :],
                                            start=True, stop=True)
                last.then_inc(y_done, 1)
                if exists(back(i, s, 1)[0]):
                    project(*back(i, s, 1))

            rounds(pe, ET, step)
            project(ET // K - 1, K - 1)


G4 = 4
NG = -(-NT // G4)


def bias_rows(src):
    return src.rearrange("(a n) -> a n", a=1).to_broadcast([P, D])


def tile_rows(t):
    return NLAST if isinstance(t, int) and t == NT - 1 else P


def node_mlp(nc, g, x, comp_a, comp_b, w1, b1, w2, b2, out):
    with ExitStack() as ctx:
        sb = lambda n, s, d=F32: ctx.enter_context(nc.sbuf_tensor(f"nm_{n}", s, d))
        sem = lambda n: nc.alloc_semaphore(f"nm_{n}")
        split = [split_weight(nc, ctx, n, w, KC, D) for n, w in (("w1", w1), ("w2", w2))]
        load_split(nc, split)
        (_, _, w1_hi, w1_lo), (_, _, w2_hi, w2_lo) = split
        xb, a, c = ([sb(f"{n}{r}", [P, D]) for r in range(G4)] for n in ("x", "a", "c"))
        pre, ypre, y = ([sb(f"{n}{r}", [P, D]) for r in range(G4)] for n in ("pre", "ypre", "y"))
        x1 = [[sb(f"x1_{h}{r}", [P, D]) for r in range(G4)] for h in range(2)]
        uT_hi, uT_lo = sb("uT_hi", [P, KC, D], F32R), sb("uT_lo", [P, KC, D], F32R)
        hT = [sb(f"hT{m}", [P, D]) for m in range(KC)]
        hT_hi, hT_lo = sb("hT_hi", [P, KC, D], F32R), sb("hT_lo", [P, KC, D], F32R)
        b1_col, b2_row = sb("b1_col", [P, KC]), sb("b2_row", [P, D])
        idx = sb("idx", [P, 2, G4], I32)
        st, mv = [sb(f"st{w}", [P, G4, 6]) for w in range(2)], [sb(f"mv{w}", [P, G4, 2]) for w in range(2)]
        std, rstd, shift = ([sb(f"{n}{w}", [P, G4]) for w in range(2)] for n in ("std", "rstd", "shift"))
        psT = [ctx.enter_context(nc.psum_tensor(f"nm_psT{s}", [P, KC, P], F32)) for s in range(2)]
        ps1 = [ctx.enter_context(nc.psum_tensor(f"nm_ps1{s}", [P, D], F32)) for s in range(KC)]
        ps2 = [ctx.enter_context(nc.psum_tensor(f"nm_ps2{s}", [P, D], F32)) for s in range(2)]
        got_x, got_a, got_c, stored = ([sem(f"{n}{r}") for r in range(G4)] for n in ("got_x", "got_a", "got_c", "stored"))
        a_ready, c_ready, held, bias_in = sem("a_ready"), sem("c_ready"), sem("held"), sem("bias_in")
        added, measured, var_ready, std_ready, inverted, coef_ready = (sem(n) for n in (
            "added", "measured", "var_ready", "std_ready", "inverted", "coef_ready"))
        y_added, y_measured, y_var_ready, y_std_ready, y_inverted, y_coef_ready = (sem(n) for n in (
            "y_added", "y_measured", "y_var_ready", "y_std_ready", "y_inverted", "y_coef_ready"))
        x1_ready, u_ready, x1_biased, turned, high, low = (sem(n) for n in (
            "x1_ready", "u_ready", "x1_biased", "turned", "high", "low"))
        h_done, h_ready, h_high, h_low, y_done, y_ready = (sem(n) for n in (
            "h_done", "h_ready", "h_high", "h_low", "y_done", "y_ready"))
        block = ctx.enter_context(nc.Block())

        def tiles(q):
            return range(NT - (NG - 1) * G4 if isinstance(q, int) and q == NG - 1 else G4)

        def width(q):
            return len(tiles(q)) * P

        @block.sync
        def _(sp):
            with nc.allow_non_contiguous_dma(reason="a bias onto the partitions, once"):
                sp.dma_start(b1_col[:, :], b1.rearrange("(m p) -> p m", p=P)).then_inc(bias_in, 16)
            sp.dma_start(b2_row[:, :], bias_rows(b2)).then_inc(bias_in, 16)

            def load(q):
                for r in tiles(q):
                    t = q * G4 + r
                    if later(q):
                        sp.wait_ge(added, t - G4 + 1)
                    n = tile_rows(t)
                    sp.dma_start(xb[r][0:n, :], x[bass.ds(t * P, n), :]).then_inc(got_x[r], 16)

            def store(q):
                for r in tiles(q):
                    t = q * G4 + r
                    sp.wait_ge(y_ready, t + 1)
                    n = tile_rows(t)
                    sp.dma_start(out[bass.ds(t * P, n), :], y[r][0:n, :]).then_inc(stored[r], 16)

            load(0)

            def step(q, h, first, last):
                if not last:
                    load(q + 1)
                if later(q):
                    store(q - 1)

            tile_loop(sp, NG, step, ahead=3)
            store(NG - 1)
            for r in range(G4):
                sp.wait_ge(stored[r], 16 * (NG if r in tiles(NG - 1) else NG - 1))

        @block.gpsimd
        def _(pool):
            last_sum = pool.to_reg(EPAD - 1)

            def gather(q):
                for ready, buf, comp, k, got in ((a_ready, a, comp_a, 0, got_a), (c_ready, c, comp_b, 1, got_c)):
                    for r in tiles(q):
                        hold(pool, ready, q * G4 + r + 1, held)
                        nc.gpsimd.indirect_dma_start(buf[r][:, :], None, comp,
                                                     bass.IndirectOffsetOnAxis(idx[:, k, r:r + 1], 0),
                                                     bounds_check=last_sum, oob_is_err=False).then_inc(got[r], 16)

            def add_bias(q, h):
                for r in tiles(q):
                    pool.wait_ge(u_ready, q * G4 + r + 1)
                    nc.gpsimd.tensor_tensor(x1[h][r][:, :], x1[h][r][:, :], b2_row[:, :], ALU.add)\
                      .then_inc(x1_biased, 1)

            pool.wait_ge(bias_in, 32)
            gather(0)

            def step(q, h, first, last):
                if not last:
                    gather(q + 1)
                add_bias(q, h)

            tile_loop(pool, NG, step, ahead=3)

        @block.tensor
        def _(pe):
            def turn(q):
                for r in tiles(q):
                    t = q * G4 + r
                    pe.wait_ge(u_ready, t + 1)
                    if not (isinstance(t, int) and t < 2):
                        pe.wait_ge(low, t - 1)
                    for k in range(KC):
                        last = nc.tensor.transpose(psT[r % 2][:, k, :], pre[r][:, k * P:(k + 1) * P], g.ident[:, :])
                    last.then_inc(turned, 1)

            def up(q):
                pe.wait_ge(low, q * G4 + len(tiles(q)))
                w = width(q)
                for m in range(KC):
                    if later(q):
                        pe.wait_ge(h_low, q * KC + m - KC + 1)
                    n = 0
                    for wt, ut in ((w1_hi, uT_hi), (w1_lo, uT_hi), (w1_hi, uT_lo)):
                        for k in range(KC):
                            last = nc.tensor.matmul(ps1[m][:, 0:w], wt[:, k, m * P:(m + 1) * P], ut[:, k, 0:w],
                                                    start=n == 0, stop=n == 3 * KC - 1)
                            n += 1
                    last.then_inc(h_done, 1)

            def down(q):
                pe.wait_ge(h_low, q * KC + KC)
                for r in tiles(q):
                    t = q * G4 + r
                    if not (isinstance(t, int) and t < 2):
                        pe.wait_ge(y_added, t - 1)
                    n = 0
                    for ht, wt in ((hT_hi, w2_hi), (hT_hi, w2_lo), (hT_lo, w2_hi)):
                        for k in range(KC):
                            last = nc.tensor.matmul(ps2[r % 2][:, :], ht[:, k, r * P:(r + 1) * P], wt[:, k, :],
                                                    start=n == 0, stop=n == 3 * KC - 1)
                            n += 1
                    last.then_inc(y_done, 1)

            turn(0)

            def step(q, h, first, last):
                up(q)
                if not last:
                    turn(q + 1)
                down(q)

            tile_loop(pe, NG, step, ahead=3)

        @block.scalar
        def _(act):
            act.wait_ge(bias_in, 32)

            def roots(q):
                for r in tiles(q):
                    act.wait_ge(var_ready, q * G4 + r + 1)
                    nc.scalar.activation(std[0][:, r:r + 1], mv[0][:, r, 1:2], ACT.Sqrt, bias=g.eps_col[:, :])\
                      .then_inc(std_ready, 1)

            def apply(q, h):
                for r in tiles(q):
                    t = q * G4 + r
                    act.wait_ge(coef_ready, t + 1)
                    if not (isinstance(q, int) and q < 2):
                        act.wait_ge(y_added, t - 2 * G4 + 1)
                    nc.scalar.activation(x1[h][r][:, :], pre[r][:, :], ACT.Identity, bias=shift[0][:, r:r + 1],
                                         scale=rstd[0][:, r:r + 1]).then_inc(x1_ready, 1)

            def highs(q):
                for r in tiles(q):
                    act.wait_ge(turned, q * G4 + r + 1)
                    if later(q):
                        act.wait_ge(h_done, q * KC)
                    nc.scalar.activation(uT_hi[:, :, r * P:(r + 1) * P], psT[r % 2][:, :, :], ACT.Copy)\
                      .then_inc(high, 1)

            def hidden(q):
                w = width(q)
                for m in range(KC):
                    act.wait_ge(h_done, q * KC + m + 1)
                    if later(q):
                        act.wait_ge(h_low, q * KC + m - KC + 1)
                        act.wait_ge(y_done, q * G4)
                    nc.scalar.activation(hT[m][:, 0:w], ps1[m][:, 0:w], ACT.Relu, bias=b1_col[:, m:m + 1])\
                      .then_inc(h_ready, 1)
                    act.wait_ge(h_ready, q * KC + m + 1)
                    nc.scalar.activation(hT_hi[:, m, 0:w], hT[m][:, 0:w], ACT.Copy).then_inc(h_high, 1)

            def finish(q):
                for r in tiles(q):
                    act.wait_ge(y_var_ready, q * G4 + r + 1)
                    nc.scalar.activation(std[1][:, r:r + 1], mv[1][:, r, 1:2], ACT.Sqrt, bias=g.eps_col[:, :])\
                      .then_inc(y_std_ready, 1)
                for r in tiles(q):
                    act.wait_ge(y_coef_ready, q * G4 + r + 1)
                    if later(q):
                        act.wait_ge(stored[r], q * 16)
                    nc.scalar.activation(y[r][:, :], ypre[r][:, :], ACT.Identity, bias=shift[1][:, r:r + 1],
                                         scale=rstd[1][:, r:r + 1]).then_inc(y_ready, 1)

            roots(0)
            apply(0, 0)
            highs(0)

            def step(q, h, first, last):
                if not last:
                    roots(q + 1)
                hidden(q)
                if not last:
                    apply(q + 1, 1 - h)
                    highs(q + 1)
                finish(q)

            tile_loop(act, NG, step, ahead=3)

        @block.vector
        def _(dve):
            def stage(q, k, buf, ready, used):
                for r in tiles(q):
                    t = q * G4 + r
                    if later(q):
                        dve.wait_ge(used, t - G4 + 1)
                    nc.vector.memset(buf[r][:, :], 0.0)
                    nc.vector.tensor_scalar(idx[:, k, r:r + 1], g.node_row[:, 1, bass.ds(t, 1)], 0.0, None, ALU.add)\
                      .then_inc(ready, 1)

            def front(q):
                for r in tiles(q):
                    t = q * G4 + r
                    dve.wait_ge(got_x[r], q * 16 + 16)
                    dve.wait_ge(got_a[r], q * 16 + 16)
                    if later(q):
                        dve.wait_ge(turned, t - G4 + 1)
                    nc.vector.tensor_tensor(pre[r][:, :], xb[r][:, :], a[r][:, :], ALU.add).then_inc(added, 1)
                for r in tiles(q):
                    t = q * G4 + r
                    dve.wait_ge(added, t + 1)
                    nc.vector.bn_stats(st[0][:, r, :], pre[r][:, :]).then_inc(measured, 1)
                for r in tiles(q):
                    hold(dve, measured, q * G4 + r + 1, held)
                    nc.vector.bn_aggr(mv[0][:, r, :], st[0][:, r, :]).then_inc(var_ready, 1)

            def coefs(q, w, std_sem, inv_sem, coef_sem):
                for r in tiles(q):
                    dve.wait_ge(std_sem, q * G4 + r + 1)
                    nc.vector.reciprocal(rstd[w][:, r:r + 1], std[w][:, r:r + 1]).then_inc(inv_sem, 1)
                for r in tiles(q):
                    dve.wait_ge(inv_sem, q * G4 + r + 1)
                    nc.vector.tensor_scalar(shift[w][:, r:r + 1], mv[w][:, r, 0:1], rstd[w][:, r:r + 1], -1.0,
                                            ALU.mult, ALU.mult).then_inc(coef_sem, 1)

            def add_sums(q, h):
                for r in tiles(q):
                    dve.wait_ge(x1_ready, q * G4 + r + 1)
                    dve.wait_ge(got_c[r], q * 16 + 16)
                    nc.vector.tensor_tensor(pre[r][:, :], x1[h][r][:, :], c[r][:, :], ALU.add).then_inc(u_ready, 1)

            def lows(q):
                for r in tiles(q):
                    dve.wait_ge(high, q * G4 + r + 1)
                    nc.vector.tensor_tensor(uT_lo[:, :, r * P:(r + 1) * P], psT[r % 2][:, :, :],
                                            uT_hi[:, :, r * P:(r + 1) * P].bitcast(F32), ALU.subtract).then_inc(low, 1)

            def hidden(q):
                w = width(q)
                for m in range(KC):
                    dve.wait_ge(h_high, q * KC + m + 1)
                    nc.vector.tensor_tensor(hT_lo[:, m, 0:w], hT[m][:, 0:w], hT_hi[:, m, 0:w].bitcast(F32),
                                            ALU.subtract).then_inc(h_low, 1)

            def finish(q, h):
                for r in tiles(q):
                    t = q * G4 + r
                    dve.wait_ge(y_done, t + 1)
                    dve.wait_ge(x1_biased, t + 1)
                    if later(q):
                        dve.wait_ge(y_ready, t - G4 + 1)
                    nc.vector.tensor_tensor(ypre[r][:, :], ps2[r % 2][:, :], x1[h][r][:, :], ALU.add).then_inc(y_added, 1)
                    dve.wait_ge(y_added, t + 1)
                    nc.vector.bn_stats(st[1][:, r, :], ypre[r][:, :]).then_inc(y_measured, 1)
                    hold(dve, y_measured, t + 1, held)
                    nc.vector.bn_aggr(mv[1][:, r, :], st[1][:, r, :]).then_inc(y_var_ready, 1)
                coefs(q, 1, y_std_ready, y_inverted, y_coef_ready)

            def middle(q, h):
                coefs(q, 0, std_ready, inverted, coef_ready)
                add_sums(q, h)
                if not (isinstance(q, int) and q == NG - 1):
                    stage(q + 1, 1, c, c_ready, u_ready)
                lows(q)

            stage(0, 0, a, a_ready, added)
            stage(0, 1, c, c_ready, u_ready)
            front(0)
            stage(1, 0, a, a_ready, added)
            middle(0, 0)

            def step(q, h, first, last):
                if not last:
                    front(q + 1)
                if not (isinstance(q, int) and q + 2 >= NG):
                    stage(q + 2, 0, a, a_ready, added)
                hidden(q)
                if not last:
                    middle(q + 1, 1 - h)
                finish(q, h)

            tile_loop(dve, NG, step, ahead=3)


def node_conv1(nc, g, x2, comp_a, bias_a, comp_b, w, b, x3_out, g_out):
    with ExitStack() as ctx:
        sb = lambda n, s, d=F32: ctx.enter_context(nc.sbuf_tensor(f"n3_{n}", s, d))
        sem = lambda n: nc.alloc_semaphore(f"n3_{n}")
        split = split_weight(nc, ctx, "conv1_w", w, KC, D)
        load_split(nc, [split])
        _, _, w_hi, w_lo = split
        xb, a, c, pre, x3, v, z, gz = ([sb(f"{n}{s}", [P, D]) for s in range(K)] for n in
                                       ("x", "a", "c", "pre", "x3", "v", "z", "gz"))
        vT_hi, vT_lo = ([sb(f"{n}{s}", [P, KC, P], F32R) for s in range(2)] for n in ("vT_hi", "vT_lo"))
        bias_row, b_row = sb("bias_row", [P, D]), sb("b_row", [P, D])
        idx = sb("idx", [P, 2, K], I32)
        stats, mv = sb("stats", [P, K, 6]), sb("mv", [P, K, 2])
        std, rstd, shift = sb("std", [P, K]), sb("rstd", [P, K]), sb("shift", [P, K])
        psT = [ctx.enter_context(nc.psum_tensor(f"n3_psT{s}", [P, KC, P], F32)) for s in range(2)]
        ps = [ctx.enter_context(nc.psum_tensor(f"n3_ps{s}", [P, D], F32)) for s in range(K)]
        got_x, got_a, got_c, x3_stored, g_stored = ([sem(f"{n}{s}") for s in range(K)] for n in
                                                    ("got_x", "got_a", "got_c", "x3_stored", "g_stored"))
        a_ready, c_ready, held, bias_in, a_biased = (sem(n) for n in ("a_ready", "c_ready", "held", "bias_in", "a_biased"))
        added, measured, var_ready, std_ready, inverted, coef_ready, x3_ready = (sem(n) for n in (
            "added", "measured", "var_ready", "std_ready", "inverted", "coef_ready", "x3_ready"))
        v_ready, turned, high, low, z_done, z_ready, g_ready = (sem(n) for n in (
            "v_ready", "turned", "high", "low", "z_done", "z_ready", "g_ready"))
        block = ctx.enter_context(nc.Block())

        @block.sync
        def _(sp):
            sp.dma_start(bias_row[:, :], bias_rows(bias_a)).then_inc(bias_in, 16)
            sp.dma_start(b_row[:, :], bias_rows(b)).then_inc(bias_in, 16)

            def load(i, s):
                t = i * K + s
                if later(i):
                    sp.wait_ge(added, t - K + 1)
                n = tile_rows(t)
                sp.dma_start(xb[s][0:n, :], x2[bass.ds(t * P, n), :]).then_inc(got_x[s], 16)

            def store(i, s):
                t = i * K + s
                n = tile_rows(t)
                sp.wait_ge(x3_ready, t + 1)
                sp.dma_start(x3_out[bass.ds(t * P, n), :], x3[s][0:n, :]).then_inc(x3_stored[s], 16)
                sp.wait_ge(g_ready, t + 1)
                sp.dma_start(g_out[bass.ds(t * P, n), :], gz[s][0:n, :]).then_inc(g_stored[s], 16)

            for s in range(K - 1):
                load(0, s)

            def step(i, s):
                t = i * K + s
                if not (isinstance(t, int) and t + K - 1 >= NT):
                    load(*((i, K - 1) if s == 0 else (i + 1, s - 1)))
                store(i, s)

            rounds(sp, NT, step)
            for s in range(K):
                sp.wait_ge(x3_stored[s], 16 * len(range(s, NT, K)))
                sp.wait_ge(g_stored[s], 16 * len(range(s, NT, K)))

        @block.gpsimd
        def _(pool):
            last_sum = pool.to_reg(EPAD - 1)

            def step(i, s):
                t = i * K + s
                hold(pool, a_ready, t + 1, held)
                nc.gpsimd.indirect_dma_start(a[s][:, :], None, comp_a, bass.IndirectOffsetOnAxis(idx[:, 0, s:s + 1], 0),
                                             bounds_check=last_sum, oob_is_err=False).then_inc(got_a[s], 16)
                hold(pool, c_ready, t + 1, held)
                nc.gpsimd.indirect_dma_start(c[s][:, :], None, comp_b, bass.IndirectOffsetOnAxis(idx[:, 1, s:s + 1], 0),
                                             bounds_check=last_sum, oob_is_err=False).then_inc(got_c[s], 16)

            rounds(pool, NT, step)

        @block.tensor
        def _(pe):
            def project(i, s):
                t, h = i * K + s, s % 2
                pe.wait_ge(low, t + 1)
                if later(i):
                    pe.wait_ge(z_ready, t - K + 1)
                n = 0
                for vt, wt in ((vT_hi, w_hi), (vT_hi, w_lo), (vT_lo, w_hi)):
                    for k in range(KC):
                        last = nc.tensor.matmul(ps[s][:, :], vt[h][:, k, :], wt[:, k, :], start=n == 0,
                                                stop=n == 3 * KC - 1)
                        n += 1
                last.then_inc(z_done, 1)

            def step(i, s):
                t = i * K + s
                pe.wait_ge(v_ready, t + 1)
                if exists(back(i, s, 2)[0]):
                    pe.wait_ge(low, t - 1)
                for k in range(KC):
                    last = nc.tensor.transpose(psT[s % 2][:, k, :], v[s][:, k * P:(k + 1) * P], g.ident[:, :])
                last.then_inc(turned, 1)
                if exists(back(i, s, 1)[0]):
                    project(*back(i, s, 1))

            rounds(pe, NT, step)
            project(*divmod(NT - 1, K))

        @block.scalar
        def _(act):
            def root(i, s):
                act.wait_ge(var_ready, i * K + s + 1)
                nc.scalar.activation(std[:, s:s + 1], mv[:, s, 1:2], ACT.Sqrt, bias=g.eps_col[:, :]).then_inc(std_ready, 1)

            def apply(i, s):
                act.wait_ge(coef_ready, i * K + s + 1)
                if later(i):
                    act.wait_ge(x3_stored[s], i * 16)
                    act.wait_ge(v_ready, i * K + s - K + 1)
                nc.scalar.activation(x3[s][:, :], pre[s][:, :], ACT.Identity, bias=shift[:, s:s + 1],
                                     scale=rstd[:, s:s + 1]).then_inc(x3_ready, 1)

            def highs(i, s):
                t = i * K + s
                act.wait_ge(turned, t + 1)
                if exists(back(i, s, 2)[0]):
                    act.wait_ge(z_done, t - 1)
                nc.scalar.activation(vT_hi[s % 2][:, :, :], psT[s % 2][:, :, :], ACT.Copy).then_inc(high, 1)

            def relu(i, s):
                t = i * K + s
                act.wait_ge(z_ready, t + 1)
                if later(i):
                    act.wait_ge(g_stored[s], i * 16)
                nc.scalar.activation(gz[s][:, :], z[s][:, :], ACT.Relu, scale=g.dis[:, bass.ds(t, 1)]).then_inc(g_ready, 1)

            def step(i, s):
                for k, f in ((4, relu), (1, apply), (2, highs)):
                    if exists(back(i, s, k)[0] if k < K else (i - 1 if not isinstance(i, int) or i >= 1 else -1)):
                        f(*(back(i, s, k) if k < K else (i - 1, s)))
                root(i, s)

            rounds(act, NT, step)
            n = NT - 1
            relu(*divmod(n - 3, K))
            apply(*divmod(n, K))
            highs(*divmod(n - 1, K))
            relu(*divmod(n - 2, K))
            highs(*divmod(n, K))
            relu(*divmod(n - 1, K))
            relu(*divmod(n, K))

        @block.vector
        def _(dve):
            def stage_a(t, s):
                nc.vector.memset(a[s][:, :], 0.0)
                nc.vector.tensor_scalar(idx[:, 0, s:s + 1], g.node_row[:, 0, bass.ds(t, 1)], 0.0, None, ALU.add)\
                  .then_inc(a_ready, 1)

            def stage_c(t, s):
                nc.vector.memset(c[s][:, :], 0.0)
                nc.vector.tensor_scalar(idx[:, 1, s:s + 1], g.node_row[:, 1, bass.ds(t, 1)], 0.0, None, ALU.add)\
                  .then_inc(c_ready, 1)

            def coefs(i, s):
                t = i * K + s
                dve.wait_ge(std_ready, t + 1)
                nc.vector.reciprocal(rstd[:, s:s + 1], std[:, s:s + 1]).then_inc(inverted, 1)
                dve.wait_ge(inverted, t + 1)
                nc.vector.tensor_scalar(shift[:, s:s + 1], mv[:, s, 0:1], rstd[:, s:s + 1], -1.0,
                                        ALU.mult, ALU.mult).then_inc(coef_ready, 1)

            def front(i, s):
                t = i * K + s
                dve.wait_ge(got_a[s], i * 16 + 16)
                nc.vector.tensor_tensor(a[s][:, :], a[s][:, :], bias_row[:, :], ALU.add).then_inc(a_biased, 1)
                dve.wait_ge(got_x[s], i * 16 + 16)
                if later(i):
                    dve.wait_ge(x3_ready, t - K + 1)
                dve.wait_ge(a_biased, t + 1)
                nc.vector.tensor_tensor(pre[s][:, :], xb[s][:, :], a[s][:, :], ALU.add).then_inc(added, 1)
                dve.wait_ge(added, t + 1)
                nc.vector.bn_stats(stats[:, s, :], pre[s][:, :]).then_inc(measured, 1)

            def lows(i, s):
                dve.wait_ge(high, i * K + s + 1)
                nc.vector.tensor_tensor(vT_lo[s % 2][:, :, :], psT[s % 2][:, :, :], vT_hi[s % 2][:, :, :].bitcast(F32),
                                        ALU.subtract).then_inc(low, 1)

            def add_sums(i, s):
                t = i * K + s
                dve.wait_ge(x3_ready, t + 1)
                dve.wait_ge(got_c[s], i * 16 + 16)
                if later(i):
                    dve.wait_ge(turned, t - K + 1)
                nc.vector.scalar_tensor_tensor(v[s][:, :], x3[s][:, :], g.dis[:, bass.ds(t, 1)], c[s][:, :],
                                               ALU.mult, ALU.add).then_inc(v_ready, 1)
                if not (isinstance(t, int) and t + K >= NT):
                    dve.wait_ge(v_ready, t + 1)
                    stage_c(t + K, s)

            def out(i, s):
                t = i * K + s
                dve.wait_ge(z_done, t + 1)
                if later(i):
                    dve.wait_ge(g_ready, t - K + 1)
                nc.vector.scalar_tensor_tensor(z[s][:, :], ps[s][:, :], g.dis[:, bass.ds(t, 1)], b_row[:, :],
                                               ALU.mult, ALU.add).then_inc(z_ready, 1)

            for s in range(K):
                stage_a(s, s)
                stage_c(s, s)
            dve.wait_ge(bias_in, 32)

            def step(i, s):
                t = i * K + s
                if exists(back(i, s, 1)[0]):
                    coefs(*back(i, s, 1))
                front(i, s)
                if not (isinstance(t, int) and t + K >= NT):
                    stage_a(t + K, s)
                hold(dve, measured, t + 1, held)
                nc.vector.bn_aggr(mv[:, s, :], stats[:, s, :]).then_inc(var_ready, 1)
                for k, f in ((2, lows), (1, add_sums), (3, out)):
                    if exists(back(i, s, k)[0]):
                        f(*back(i, s, k))

            rounds(dve, NT, step, peel=2)
            n = NT - 1
            coefs(*divmod(n, K))
            lows(*divmod(n - 1, K))
            add_sums(*divmod(n, K))
            out(*divmod(n - 2, K))
            lows(*divmod(n, K))
            out(*divmod(n - 1, K))
            out(*divmod(n, K))


def node_conv2(nc, g, x3_in, g_in, comp, w, b, out):
    with ExitStack() as ctx:
        sb = lambda n, s, d=F32: ctx.enter_context(nc.sbuf_tensor(f"n4_{n}", s, d))
        sem = lambda n: nc.alloc_semaphore(f"n4_{n}")
        split = split_weight(nc, ctx, "conv2_w", w, KC, D)
        load_split(nc, [split])
        _, _, w_hi, w_lo = split
        x3, gb, c, v, pre, y = ([sb(f"{n}{s}", [P, D]) for s in range(K)] for n in ("x3", "g", "c", "v", "pre", "y"))
        vT_hi, vT_lo = ([sb(f"{n}{s}", [P, KC, P], F32R) for s in range(2)] for n in ("vT_hi", "vT_lo"))
        b_row = sb("b_row", [P, D])
        idx = sb("idx", [P, K], I32)
        stats, mv = sb("stats", [P, K, 6]), sb("mv", [P, K, 2])
        std, rstd, shift = sb("std", [P, K]), sb("rstd", [P, K]), sb("shift", [P, K])
        psT = [ctx.enter_context(nc.psum_tensor(f"n4_psT{s}", [P, KC, P], F32)) for s in range(2)]
        ps = [ctx.enter_context(nc.psum_tensor(f"n4_ps{s}", [P, D], F32)) for s in range(K)]
        got_x, got_g, got_c, stored = ([sem(f"{n}{s}") for s in range(K)] for n in ("got_x", "got_g", "got_c", "stored"))
        c_ready, held, bias_in, x3_biased = (sem(n) for n in ("c_ready", "held", "bias_in", "x3_biased"))
        v_ready, turned, high, low, z_done = (sem(n) for n in ("v_ready", "turned", "high", "low", "z_done"))
        added, measured, var_ready, std_ready, inverted, coef_ready, y_ready = (sem(n) for n in (
            "added", "measured", "var_ready", "std_ready", "inverted", "coef_ready", "y_ready"))
        block = ctx.enter_context(nc.Block())

        @block.sync
        def _(sp):
            sp.dma_start(b_row[:, :], bias_rows(b)).then_inc(bias_in, 16)

            def load(i, s):
                t = i * K + s
                n = tile_rows(t)
                if later(i):
                    sp.wait_ge(v_ready, t - K + 1)
                sp.dma_start(gb[s][0:n, :], g_in[bass.ds(t * P, n), :]).then_inc(got_g[s], 16)
                if later(i):
                    sp.wait_ge(added, t - K + 1)
                sp.dma_start(x3[s][0:n, :], x3_in[bass.ds(t * P, n), :]).then_inc(got_x[s], 16)

            def store(i, s):
                t = i * K + s
                n = tile_rows(t)
                sp.wait_ge(y_ready, t + 1)
                sp.dma_start(out[bass.ds(t * P, n), :], y[s][0:n, :]).then_inc(stored[s], 16)

            for s in range(K - 1):
                load(0, s)

            def step(i, s):
                t = i * K + s
                if not (isinstance(t, int) and t + K - 1 >= NT):
                    load(*((i, K - 1) if s == 0 else (i + 1, s - 1)))
                if exists(back(i, s, 2)[0]):
                    store(*back(i, s, 2))

            rounds(sp, NT, step)
            store(*divmod(NT - 2, K))
            store(*divmod(NT - 1, K))
            for s in range(K):
                sp.wait_ge(stored[s], 16 * len(range(s, NT, K)))

        @block.gpsimd
        def _(pool):
            last_sum = pool.to_reg(EPAD - 1)
            pool.wait_ge(bias_in, 16)

            def add_bias(i, s):
                pool.wait_ge(got_x[s], i * 16 + 16)
                nc.gpsimd.tensor_tensor(x3[s][:, :], x3[s][:, :], b_row[:, :], ALU.add).then_inc(x3_biased, 1)

            def step(i, s):
                t = i * K + s
                hold(pool, c_ready, t + 1, held)
                nc.gpsimd.indirect_dma_start(c[s][:, :], None, comp, bass.IndirectOffsetOnAxis(idx[:, s:s + 1], 0),
                                             bounds_check=last_sum, oob_is_err=False).then_inc(got_c[s], 16)
                if exists(back(i, s, 2)[0]):
                    add_bias(*back(i, s, 2))

            rounds(pool, NT, step)
            add_bias(*divmod(NT - 2, K))
            add_bias(*divmod(NT - 1, K))

        @block.tensor
        def _(pe):
            def project(i, s):
                t, h = i * K + s, s % 2
                pe.wait_ge(low, t + 1)
                if later(i):
                    pe.wait_ge(added, t - K + 1)
                n = 0
                for vt, wt in ((vT_hi, w_hi), (vT_hi, w_lo), (vT_lo, w_hi)):
                    for k in range(KC):
                        last = nc.tensor.matmul(ps[s][:, :], vt[h][:, k, :], wt[:, k, :], start=n == 0,
                                                stop=n == 3 * KC - 1)
                        n += 1
                last.then_inc(z_done, 1)

            def step(i, s):
                t = i * K + s
                pe.wait_ge(v_ready, t + 1)
                if exists(back(i, s, 2)[0]):
                    pe.wait_ge(low, t - 1)
                for k in range(KC):
                    last = nc.tensor.transpose(psT[s % 2][:, k, :], v[s][:, k * P:(k + 1) * P], g.ident[:, :])
                last.then_inc(turned, 1)
                if exists(back(i, s, 1)[0]):
                    project(*back(i, s, 1))

            rounds(pe, NT, step)
            project(*divmod(NT - 1, K))

        @block.scalar
        def _(act):
            def highs(i, s):
                t = i * K + s
                act.wait_ge(turned, t + 1)
                if exists(back(i, s, 2)[0]):
                    act.wait_ge(z_done, t - 1)
                nc.scalar.activation(vT_hi[s % 2][:, :, :], psT[s % 2][:, :, :], ACT.Copy).then_inc(high, 1)

            def root(i, s):
                act.wait_ge(var_ready, i * K + s + 1)
                nc.scalar.activation(std[:, s:s + 1], mv[:, s, 1:2], ACT.Sqrt, bias=g.eps_col[:, :]).then_inc(std_ready, 1)

            def apply(i, s):
                act.wait_ge(coef_ready, i * K + s + 1)
                if later(i):
                    act.wait_ge(stored[s], i * 16)
                nc.scalar.activation(y[s][:, :], pre[s][:, :], ACT.Identity, bias=shift[:, s:s + 1],
                                     scale=rstd[:, s:s + 1]).then_inc(y_ready, 1)

            def step(i, s):
                for k, f in ((3, apply), (1, highs), (2, root)):
                    if exists(back(i, s, k)[0]):
                        f(*back(i, s, k))

            rounds(act, NT, step)
            n = NT - 1
            apply(*divmod(n - 2, K))
            highs(*divmod(n, K))
            root(*divmod(n - 1, K))
            apply(*divmod(n - 1, K))
            root(*divmod(n, K))
            apply(*divmod(n, K))

        @block.vector
        def _(dve):
            def stage(t, s):
                nc.vector.memset(c[s][:, :], 0.0)
                nc.vector.tensor_scalar(idx[:, s:s + 1], g.node_row[:, 1, bass.ds(t, 1)], 0.0, None, ALU.add)\
                  .then_inc(c_ready, 1)

            def coefs(i, s):
                t = i * K + s
                dve.wait_ge(std_ready, t + 1)
                nc.vector.reciprocal(rstd[:, s:s + 1], std[:, s:s + 1]).then_inc(inverted, 1)
                dve.wait_ge(inverted, t + 1)
                nc.vector.tensor_scalar(shift[:, s:s + 1], mv[:, s, 0:1], rstd[:, s:s + 1], -1.0,
                                        ALU.mult, ALU.mult).then_inc(coef_ready, 1)

            def front(i, s):
                t = i * K + s
                dve.wait_ge(got_g[s], i * 16 + 16)
                dve.wait_ge(got_c[s], i * 16 + 16)
                if later(i):
                    dve.wait_ge(turned, t - K + 1)
                nc.vector.tensor_tensor(v[s][:, :], gb[s][:, :], c[s][:, :], ALU.add).then_inc(v_ready, 1)
                if not (isinstance(t, int) and t + K >= NT):
                    dve.wait_ge(v_ready, t + 1)
                    stage(t + K, s)

            def lows(i, s):
                dve.wait_ge(high, i * K + s + 1)
                nc.vector.tensor_tensor(vT_lo[s % 2][:, :, :], psT[s % 2][:, :, :], vT_hi[s % 2][:, :, :].bitcast(F32),
                                        ALU.subtract).then_inc(low, 1)

            def out_pre(i, s):
                t = i * K + s
                dve.wait_ge(z_done, t + 1)
                dve.wait_ge(x3_biased, t + 1)
                if later(i):
                    dve.wait_ge(y_ready, t - K + 1)
                nc.vector.scalar_tensor_tensor(pre[s][:, :], ps[s][:, :], g.dis[:, bass.ds(t, 1)], x3[s][:, :],
                                               ALU.mult, ALU.add).then_inc(added, 1)
                dve.wait_ge(added, t + 1)
                nc.vector.bn_stats(stats[:, s, :], pre[s][:, :]).then_inc(measured, 1)
                hold(dve, measured, t + 1, held)
                nc.vector.bn_aggr(mv[:, s, :], stats[:, s, :]).then_inc(var_ready, 1)

            for s in range(K):
                stage(s, s)

            def step(i, s):
                if exists(back(i, s, 3)[0]):
                    coefs(*back(i, s, 3))
                front(i, s)
                for k, f in ((1, lows), (2, out_pre)):
                    if exists(back(i, s, k)[0]):
                        f(*back(i, s, k))

            rounds(dve, NT, step, peel=2)
            n = NT - 1
            coefs(*divmod(n - 2, K))
            lows(*divmod(n, K))
            out_pre(*divmod(n - 1, K))
            coefs(*divmod(n - 1, K))
            out_pre(*divmod(n, K))
            coefs(*divmod(n, K))


MUL = 128
HID = 64
RB = 8
SILU_2MOM = 1.679177
AVG_NEIGHBORS = 10.0
RW = 256
RN = EPAD // RW


def radial(nc, g, w1, w2, w3):
    with ExitStack() as ctx:
        sb = lambda n, s, d=F32: ctx.enter_context(nc.sbuf_tensor(f"ra_{n}", s, d))
        sem = lambda n: nc.alloc_semaphore(f"ra_{n}")
        wt = [sb("w1", [RB, HID]), sb("w2", [HID, HID]), sb("w3", [HID, HID])]
        attr = [sb(f"attr{h}", [P, RW // P, RB]) for h in range(2)]
        attr_T = [sb(f"attr_T{h}", [RB, RW]) for h in range(2)]
        hid = [[sb(f"hid{k}{h}", [HID, RW]) for h in range(2)] for k in range(2)]
        psA = [ctx.enter_context(nc.psum_tensor(f"ra_psA{h}", [RB, RW], F32)) for h in range(2)]
        psH = [[ctx.enter_context(nc.psum_tensor(f"ra_ps{k}{h}", [HID, RW], F32)) for h in range(2)] for k in range(3)]
        w_in, staged, turned, attr_ready = sem("w_in"), sem("staged"), sem("turned"), sem("attr_ready")
        held = sem("held")
        done, ready = [sem(f"done{k}") for k in range(3)], [sem(f"ready{k}") for k in range(3)]
        block = ctx.enter_context(nc.Block())

        @block.sync
        def _(sp):
            for t, src in zip(wt, (w1, w2, w3)):
                sp.dma_start(t[:, :], src).then_inc(w_in, 16)

        @block.vector
        def _(dve):
            def step(i, s):
                t, h = i * K + s, s % 2
                if exists(back(i, s, 2)[0]):
                    dve.wait_ge(turned, t - 1)
                nc.vector.tensor_scalar(attr[h][:, :, :], g.rec[1][:, bass.ds(t * (RW // P), RW // P), 6:14], 0.0, None,
                                        ALU.add).then_inc(staged, 1)

            rounds(dve, RN, step)

        @block.tensor
        def _(pe):
            pe.wait_ge(w_in, 48)

            def layer(k, i, s):
                t, h = i * K + s, s % 2
                if exists(back(i, s, 2)[0]):
                    pe.wait_ge(ready[k], t - 1)
                hold(pe, attr_ready if k == 0 else ready[k - 1], t + 1, held)
                src = attr_T[h] if k == 0 else hid[k - 1][h]
                nc.tensor.matmul(psH[k][h][:, :], wt[k][:, :], src[:, :], start=True, stop=True).then_inc(done[k], 1)

            def step(i, s):
                t, h = i * K + s, s % 2
                pe.wait_ge(staged, t + 1)
                if exists(back(i, s, 2)[0]):
                    pe.wait_ge(attr_ready, t - 1)
                for j in range(RW // P):
                    m = nc.tensor.transpose(psA[h][:, j * P:(j + 1) * P], attr[h][:, j, :], g.ident[:, :])
                m.then_inc(turned, 1)
                for k in range(3):
                    if exists(back(i, s, k + 1)[0]):
                        layer(k, *back(i, s, k + 1))

            rounds(pe, RN, step)
            for t in range(RN, RN + 3):
                for k in range(3):
                    if t - k - 1 < RN:
                        layer(k, *divmod(t - k - 1, K))

        @block.scalar
        def _(act):
            def layer(k, i, s):
                t, h = i * K + s, s % 2
                act.wait_ge(done[k], t + 1)
                if k < 2 and exists(back(i, s, 2)[0]):
                    act.wait_ge(done[k + 1], t - 1)
                out = hid[k][h][:, :] if k < 2 else g.hid3[:, bass.ds(t * RW, RW)]
                scale = RB ** -0.5 if k == 0 else SILU_2MOM * HID ** -0.5
                nc.scalar.activation(out, psH[k][h][:, :], ACT.Silu, scale=scale).then_inc(ready[k], 1)

            def step(i, s):
                t, h = i * K + s, s % 2
                act.wait_ge(turned, t + 1)
                if exists(back(i, s, 2)[0]):
                    act.wait_ge(done[0], t - 1)
                nc.scalar.activation(attr_T[h][:, :], psA[h][:, :], ACT.Copy).then_inc(attr_ready, 1)
                for k in range(3):
                    if exists(back(i, s, k + 1)[0]):
                        layer(k, *back(i, s, k + 1))

            rounds(act, RN, step)
            for t in range(RN, RN + 3):
                for k in range(3):
                    if t - k - 1 < RN:
                        layer(k, *divmod(t - k - 1, K))


def edge_messages(nc, g, x, w_up0, w_up1, w_mlp4, w_out0, w_out1, out):
    NM = 2 * 4
    SCALE = MUL ** -0.5 * SILU_2MOM * HID ** -0.5 * (2 * MUL) ** -0.5 / AVG_NEIGHBORS
    with ExitStack() as ctx:
        sb = lambda n, s, d=F32: ctx.enter_context(nc.sbuf_tensor(f"em_{n}", s, d))
        sem = lambda n: nc.alloc_semaphore(f"em_{n}")
        split = [split_weight(nc, ctx, n, w, k, MUL) for n, w, k in
                 (("up0", w_up0, 1), ("up1", w_up1, 1), ("out0", w_out0, 2), ("out1", w_out1, 2))]
        load_split(nc, split)
        up = [(hi[:, 0, :], lo[:, 0, :]) for _, _, hi, lo in split[:2]]
        down = [(hi, lo) for _, _, hi, lo in split[2:]]
        w4 = sb("w4", [HID, D])
        x_in = [sb(f"x{s}", [P, D]) for s in range(K)]
        xT_hi, xT_lo = ([sb(f"{n}{s}", [P, 4, P], F32R) for s in range(2)] for n in ("xT_hi", "xT_lo"))
        hid = [sb(f"hid{s}", [HID, P]) for s in range(2)]
        s_up = [sb(f"s_up{s}", [P, 4, P]) for s in range(2)]
        msg = [sb(f"msg{s}", [P, NM, P]) for s in range(2)]
        dot = [[sb(f"dot{s}{m}", [P, P]) for m in range(3)] for s in range(2)]
        same, carry = [sb(f"same{s}", [P, P]) for s in range(K)], [sb(f"carry{s}", [P, P]) for s in range(K)]
        mT_hi, mT_lo = ([sb(f"{n}{s}", [P, NM, P], F32R) for s in range(2)] for n in ("mT_hi", "mT_lo"))
        sums = [sb(f"sums{s}", [P, D]) for s in range(K)]
        idx = sb("idx", [P, K], I32)
        pb = lambda n, s: ctx.enter_context(nc.psum_tensor(f"em_{n}", s, F32))
        psT, psU, psW, psM = pb("psT", [P, 4, P]), pb("psU", [P, 4, P]), pb("psW", [P, D]), [pb("psM0", [P, 4, P]), pb("psM1", [P, 4, P])]
        ps = [pb(f"ps{s}", [P, 4, P]) for s in range(2)]
        got, stored = [sem(f"got{s}") for s in range(K)], [sem(f"stored{s}") for s in range(K)]
        ready, held, w_in = sem("slot_ready"), sem("held"), sem("w_in")
        turned, high, low, hid_ready, upped, s_ready = (sem(n) for n in ("turned", "high", "low", "hid_ready", "upped", "s_ready"))
        dot0, dot1, dot2, msg_ready, masks_ready = (sem(n) for n in ("dot0", "dot1", "dot2", "msg_ready", "masks_ready"))
        m_done, m_high, m_low, summed, emptied = (sem(n) for n in ("m_done", "m_high", "m_low", "summed", "emptied"))
        block = ctx.enter_context(nc.Block())
        vectors = lambda ap: ap.rearrange("p (v m) -> p m v", m=3)

        @block.sync
        def _(sp):
            sp.dma_start(w4[:, :], w_mlp4).then_inc(w_in, 16)

            def step(i, s):
                t = i * K + s
                sp.wait_ge(emptied, t + 1)
                sp.dma_start(out[bass.ds(t * P, P), :], sums[s][:, :]).then_inc(stored[s], 16)

            rounds(sp, ET, step)
            for s in range(K):
                sp.wait_ge(stored[s], ET // K * 16)

        @block.gpsimd
        def _(pool):
            last_row = pool.to_reg(N - 1)

            def step(i, s):
                t = i * K + s
                if later(i):
                    pool.wait_ge(turned, t - K + 1)
                hold(pool, ready, t + 1, held)
                nc.gpsimd.indirect_dma_start(x_in[s][:, :], None, x, bass.IndirectOffsetOnAxis(idx[:, s:s + 1], 0),
                                             bounds_check=last_row, oob_is_err=False).then_inc(got[s], 16)

            rounds(pool, ET, step)

        @block.tensor
        def _(pe):
            pe.wait_ge(w_in, 16)

            def turn(i, s):
                t = i * K + s
                pe.wait_ge(got[s], i * 16 + 16)
                if not (isinstance(t, int) and t == 0):
                    pe.wait_ge(low, t)
                nc.tensor.transpose(psT[:, 0, :], x_in[s][:, 0:MUL], g.ident[:, :])
                for m in range(3):
                    last = nc.tensor.transpose(psT[:, 1 + m, :], vectors(x_in[s][:, MUL:D])[:, m, :], g.ident[:, :])
                last.then_inc(turned, 1)

            def lift(i, s):
                t, h = i * K + s, s % 2
                pe.wait_ge(low, t + 1)
                pe.wait_ge(hid_ready, t + 1)
                if not (isinstance(t, int) and t == 0):
                    pe.wait_ge(msg_ready, t)
                for m in range(4):
                    w_hi, w_lo = up[min(m, 1)]
                    for n, (a, b) in enumerate(((xT_hi, w_hi), (xT_hi, w_lo), (xT_lo, w_hi))):
                        nc.tensor.matmul(psU[:, m, :], a[h][:, m, :], b, start=n == 0, stop=n == 2)
                nc.tensor.matmul(psW[:, :], hid[h][:, :], w4[:, :], start=True, stop=True).then_inc(upped, 1)

            def gather(i, s):
                t, h = i * K + s, s % 2
                pe.wait_ge(msg_ready, t + 1)
                pe.wait_ge(masks_ready, t + 1)
                if not (isinstance(t, int) and t == 0):
                    pe.wait_ge(m_low, t)
                for c in range(NM):
                    last = nc.tensor.matmul(psM[c // 4][:, c % 4, :], msg[h][:, c, :], same[s][:, :], start=True, stop=True)
                last.then_inc(m_done, 1)

            def project(i, s):
                t, h = i * K + s, s % 2
                pe.wait_ge(m_low, t + 1)
                if exists(back(i, s, 2)[0]):
                    pe.wait_ge(emptied, t - 1)
                alone = isinstance(t, int) and t == 0
                for r in range(4):
                    w_hi, w_lo = down[min(r, 1)]
                    n = 0
                    for a, b in ((mT_hi, w_hi), (mT_hi, w_lo), (mT_lo, w_hi)):
                        for c in range(2):
                            last = nc.tensor.matmul(ps[h][:, r, :], a[h][:, 2 * r + c, :], b[:, c, :], start=n == 0,
                                                    stop=alone and n == 5)
                            n += 1
                    if not alone:
                        if r == 0:
                            pe.wait_ge(emptied, t)
                        before = sums[s - 1][:, 0:MUL] if r == 0 else vectors(sums[s - 1][:, MUL:D])[:, r - 1, :]
                        last = nc.tensor.matmul(ps[h][:, r, :], carry[s][:, :], before, start=False, stop=True)
                last.then_inc(summed, 1)

            def step(i, s):
                turn(i, s)
                for k, f in ((1, lift), (2, gather), (3, project)):
                    if exists(back(i, s, k)[0]):
                        f(*back(i, s, k))

            rounds(pe, ET, step)
            n = ET - 1
            for k, f in ((0, lift), (1, gather), (2, project), (0, gather), (1, project), (0, project)):
                f(*divmod(n - k, K))

        @block.scalar
        def _(act):
            def highs(i, s):
                t, h = i * K + s, s % 2
                if exists(back(i, s, 2)[0]):
                    act.wait_ge(upped, t - 1)
                nc.scalar.activation(hid[h][:, :], g.hid3[:, bass.ds(t * P, P)], ACT.Copy).then_inc(hid_ready, 1)
                act.wait_ge(turned, t + 1)
                nc.scalar.activation(xT_hi[h][:, :, :], psT[:, :, :], ACT.Copy).then_inc(high, 1)

            def lifted(i, s):
                t, h = i * K + s, s % 2
                act.wait_ge(upped, t + 1)
                if exists(back(i, s, 2)[0]):
                    act.wait_ge(msg_ready, t - 1)
                nc.scalar.activation(s_up[h][:, :, :], psU[:, :, :], ACT.Copy, scale=SCALE).then_inc(s_ready, 1)

            def message_highs(i, s):
                t, h = i * K + s, s % 2
                act.wait_ge(m_done, t + 1)
                if exists(back(i, s, 2)[0]):
                    act.wait_ge(summed, t - 1)
                for b in range(2):
                    last = nc.scalar.activation(mT_hi[h][:, 4 * b:4 * b + 4, :], psM[b][:, :, :], ACT.Copy)
                last.then_inc(m_high, 1)

            def empty(i, s):
                t, h = i * K + s, s % 2
                act.wait_ge(summed, t + 1)
                if later(i):
                    act.wait_ge(stored[s], i * 16)
                nc.scalar.activation(sums[s][:, 0:MUL], ps[h][:, 0, :], ACT.Copy)
                nc.scalar.activation(sums[s][:, MUL:D].rearrange("p (v m) -> p v m", m=3),
                                     ps[h][:, 1:4, :].rearrange("p m v -> p v m"), ACT.Copy).then_inc(emptied, 1)

            def step(i, s):
                highs(i, s)
                for k, f in ((1, lifted), (2, message_highs), (3, empty)):
                    if exists(back(i, s, k)[0]):
                        f(*back(i, s, k))

            rounds(act, ET, step)
            n = ET - 1
            for k, f in ((0, lifted), (1, message_highs), (2, empty), (0, message_highs), (1, empty), (0, empty)):
                f(*divmod(n - k, K))

        @block.vector
        def _(dve):
            def stage(t, s):
                nc.vector.tensor_scalar(idx[:, s:s + 1], g.src_row[:, 1, bass.ds(t, 1)], 0.0, None, ALU.add)\
                  .then_inc(ready, 1)

            def lows(i, s):
                t, h = i * K + s, s % 2
                dve.wait_ge(high, t + 1)
                nc.vector.tensor_tensor(xT_lo[h][:, :, :], psT[:, :, :], xT_hi[h][:, :, :].bitcast(F32),
                                        ALU.subtract).then_inc(low, 1)
                if not (isinstance(t, int) and t + K >= ET):
                    dve.wait_ge(got[s], i * 16 + 16)
                    stage(t + K, s)
                if later(i):
                    dve.wait_ge(summed, t - K + 1)
                nc.vector.tensor_scalar(same[s][:, :], g.key_row[:, 1, bass.ds(t * P, P)],
                                        g.rec[1][:, bass.ds(t, 1), 1], None, ALU.is_equal)
                nc.vector.tensor_scalar(carry[s][:, :], g.key_row[:, 1, bass.ds(t * P, P)],
                                        g.prev_last[:, 1, bass.ds(t, 1)], None, ALU.is_equal).then_inc(masks_ready, 1)

            def messages(i, s):
                t, h = i * K + s, s % 2
                y = [g.rec[1][:, bass.ds(t, 1), 2 + m] for m in range(4)]
                sv, w, o = s_up[h], psW, msg[h]
                dve.wait_ge(s_ready, t + 1)
                if exists(back(i, s, 2)[0]):
                    dve.wait_ge(m_done, t - 1)
                    dve.wait_ge(msg_ready, t - 1)
                nc.vector.tensor_scalar(dot[h][0][:, :], sv[:, 1, :], y[1], None, ALU.mult).then_inc(dot0, 1)
                nc.vector.scalar_tensor_tensor(o[:, 0, :], w[:, 0:MUL], y[0], sv[:, 0, :], ALU.mult, ALU.mult)
                dve.wait_ge(dot0, t + 1)
                nc.vector.scalar_tensor_tensor(dot[h][1][:, :], sv[:, 2, :], y[2], dot[h][0][:, :], ALU.mult, ALU.add)\
                  .then_inc(dot1, 1)
                for m in range(3):
                    nc.vector.scalar_tensor_tensor(o[:, 2 + 2 * m, :], w[:, MUL:2 * MUL], y[1 + m], sv[:, 0, :],
                                                   ALU.mult, ALU.mult)
                dve.wait_ge(dot1, t + 1)
                nc.vector.scalar_tensor_tensor(dot[h][2][:, :], sv[:, 3, :], y[3], dot[h][1][:, :], ALU.mult, ALU.add)\
                  .then_inc(dot2, 1)
                nc.vector.scalar_tensor_tensor(o[:, :, :].rearrange("p (a b) v -> p b a v", b=2)[:, 1, 1:4, :],
                                               w[:, 2 * MUL:3 * MUL].unsqueeze(1).to_broadcast([P, 3, MUL]), y[0],
                                               sv[:, 1:4, :], ALU.mult, ALU.mult)
                dve.wait_ge(dot2, t + 1)
                nc.vector.scalar_tensor_tensor(o[:, 1, :], w[:, 3 * MUL:4 * MUL], 3.0 ** -0.5, dot[h][2][:, :],
                                               ALU.mult, ALU.mult).then_inc(msg_ready, 1)

            def message_lows(i, s):
                t, h = i * K + s, s % 2
                dve.wait_ge(m_high, t + 1)
                for b in range(2):
                    last = nc.vector.tensor_tensor(mT_lo[h][:, 4 * b:4 * b + 4, :], psM[b][:, :, :],
                                                   mT_hi[h][:, 4 * b:4 * b + 4, :].bitcast(F32), ALU.subtract)
                last.then_inc(m_low, 1)

            for s in range(K):
                stage(s, s)

            def step(i, s):
                lows(i, s)
                for k, f in ((1, messages), (2, message_lows)):
                    if exists(back(i, s, k)[0]):
                        f(*back(i, s, k))

            rounds(dve, ET, step)
            n = ET - 1
            for k, f in ((0, messages), (1, message_lows), (0, message_lows)):
                f(*divmod(n - k, K))


class Shared:
    pass


def persistent(nc, ctx, g):
    sb = lambda n, s, d=F32: ctx.enter_context(nc.sbuf_tensor(n, s, d))
    dram = lambda n, s: nc.dram_tensor(n, s, F32, kind="Internal").ap()
    g.ident, g.ones, g.ident_bf = sb("ident", [P, P]), sb("ones", [P, P]), sb("ident_bf", [P, P], BF16)
    g.before, g.after = sb("before", [P, P]), sb("after", [P, P])
    g.last_row, g.one_col, g.eps_col = sb("last_row", [P, 1]), sb("one_col", [P, 1]), sb("eps_col", [P, 1])
    g.node_row, g.dis = sb("node_row", [P, 2, NT], I32), sb("dis", [P, NT])
    g.rec = [sb(f"rec{o}", [P, ET, REC]) for o in range(2)]
    g.src_any, g.src_row, g.dst_row = (sb(n, [P, 2, ET], I32) for n in ("src_any", "src_row", "dst_row"))
    g.prev_last = sb("prev_last", [P, 2, ET])
    g.src_tab, g.src_comp = sb("src_tab", [P, ET, 4]), sb("src_comp", [P, 2, ET], I32)
    g.key_row = sb("key_row", [P, 2, EPAD])
    g.att = sb("att", [P, ET, HEADS])
    g.ntab_dram = dram("ntab_dram", [NT * P, 4])
    g.rec_dram = [dram(f"rec_dram{o}", [EPAD, REC]) for o in range(2)]


def prepare(nc, g):
    with ExitStack() as ctx:
        sb = lambda n, s, d=F32: ctx.enter_context(nc.sbuf_tensor(n, s, d))
        g.hot_hi, g.hot_lo = sb("hot_hi", [P, 2, ET, NT], BF16), sb("hot_lo", [P, 2, ET, P], BF16)
        g.keys, g.rec_in = sb("keys", [P, 2, ET]), sb("rec_in", [P, ET, REC])
        g.position, g.ntab = sb("position", [P, 2, ET]), sb("ntab", [NT, P, 4])
        load_edges(nc, g)
        sort_positions(nc, g)
        permute_edges(nc, g)


def graph_network(nc, x, src, dst, edge_attr_4, edge_attr_8, w_up0, w_up1, w_mlp1, w_mlp2, w_mlp3, w_mlp4,
                  w_out0, w_out1, mlp_w1, mlp_b1, mlp_w2, mlp_b2, wq, bq, wk, bk, wv, bv, wo, bo,
                  conv_w1, conv_b1, conv_w2, conv_b2, out):
    g = Shared()
    g.src, g.dst, g.edge_attr_4, g.edge_attr_8 = src, dst, edge_attr_4, edge_attr_8
    table = lambda n, rows: nc.dram_tensor(n, [rows, D], F32, kind="Internal").ap()
    messages, x1_sums, attended, x3_sums, conv_sums, v = (table(n, EPAD) for n in (
        "messages", "x1_sums", "attended", "x3_sums", "conv_sums", "v_edges"))
    x2, x3, hidden = (table(n, N) for n in ("x2", "x3", "conv_hidden"))
    with ExitStack() as ctx:
        persistent(nc, ctx, g)
        stage = nc.cleanup_on_exit
        with stage():
            prepare(nc, g)
        with nc.sbuf_tensor("hid3", [HID, EPAD], F32) as g.hid3:
            with stage():
                radial(nc, g, w_mlp1, w_mlp2, w_mlp3)
            with stage():
                edge_messages(nc, g, x, w_up0, w_up1, w_mlp4, w_out0, w_out1, messages)
        with stage():
            edge_sums(nc, g, "e1", x, x1_sums, comp=messages, comp_order=1)
        with stage():
            node_mlp(nc, g, x, messages, x1_sums, mlp_w1, mlp_b1, mlp_w2, mlp_b2, x2)
        with nc.sbuf_tensor("logits_T", [HEADS, EPAD], F32) as g.logits_T:
            with stage():
                edge_logits(nc, g, x2, (wq, wk, wv), (bq, bk, bv), v)
            with stage():
                edge_softmax(nc, g)
        with stage():
            edge_attend(nc, g, v, wo, attended)
        with stage():
            edge_sums(nc, g, "e3", x2, x3_sums, comp=attended, comp_order=0, bias=bo, by_degree=True)
        with stage():
            node_conv1(nc, g, x2, attended, bo, x3_sums, conv_w1, conv_b1, x3, hidden)
        with stage():
            edge_sums(nc, g, "e4", hidden, conv_sums, normed=False)
        with stage():
            node_conv2(nc, g, x3, hidden, conv_sums, conv_w2, conv_b2, out)


_INS = ['x', 'src', 'dst', 'edge_attr_4', 'edge_attr_8', 'L0_gnn_W_up0', 'L0_gnn_W_up1', 'L0_gnn_W_mlp1',
        'L0_gnn_W_mlp2', 'L0_gnn_W_mlp3', 'L0_gnn_W_mlp4', 'L0_gnn_W_out0', 'L0_gnn_W_out1', 'L1_gnn_W1',
        'L1_gnn_b1', 'L1_gnn_W2', 'L1_gnn_b2', 'L2_gnn_Wq', 'L2_gnn_bq', 'L2_gnn_Wk', 'L2_gnn_bk', 'L2_gnn_Wv',
        'L2_gnn_bv', 'L2_gnn_Wo', 'L2_gnn_bo', 'L3_gnn_W1', 'L3_gnn_b1', 'L3_gnn_W2', 'L3_gnn_b2']
_OUTS = [((10000, 512), 'float32')]


def kernel(**inputs):
    import numpy as _np
    import concourse.bacc as _bacc
    from concourse import mybir as _mybir
    from concourse.bass_utils import run_bass_kernel_spmd as _run

    nc = _bacc.Bacc("TRN2", target_bir_lowering=False, num_devices=1)
    arrays, args = {}, []
    for name in _INS:
        a = _np.ascontiguousarray(inputs[name])
        arrays[f"in_{name}_dram"] = a
        args.append(nc.dram_tensor(f"in_{name}_dram", a.shape, _mybir.dt.from_np(a.dtype), kind="ExternalInput").ap())
    for i, (shape, dtype) in enumerate(_OUTS):
        dt = _mybir.dt.from_np(_np.dtype(dtype))
        args.append(nc.dram_tensor(f"out_{i}_dram", shape, dt, kind="ExternalOutput").ap())
    graph_network(nc, *args)
    r = _run(nc, [arrays], core_ids=[0])
    got = tuple(r.results[0][f"out_{i}_dram"] for i in range(len(_OUTS)))
    return got[0]
```

```python
import concourse.bass as bass
from concourse import mybir
from contextlib import ExitStack

F32 = mybir.dt.float32
F32R = mybir.dt.float32r
BF16 = mybir.dt.bfloat16
I32 = mybir.dt.int32
ALU = mybir.AluOpType
ACT = mybir.ActivationFunctionType
AX = mybir.AxisListType

P = 128
N = 10000
E = 5000
D = 512
KC = D // P
NT = -(-N // P)
NLAST = N - (NT - 1) * P
ET = 40
EP = E // ET
EPAD = ET * P
PAD_NODE = N + 100
TROWS = EPAD + P
REC = 16


def tile_loop(eng, n, step, ahead=2):
    pairs_end = 2 + (n - 2 - ahead) // 2 * 2
    step(0, 0, True, False)
    step(1, 1, True, False)
    with eng.Fori(1, pairs_end // 2) as pair:
        step(pair * 2, 0, False, False)
        step(pair * 2 + 1, 1, False, False)
    for t in range(pairs_end, n):
        step(t, t % 2, False, t == n - 1)


K = 4


def rounds(eng, n, step, peel=2):
    for i in range(peel):
        for s in range(K):
            step(i, s)
    with eng.Fori(peel, n // K - 1) as i:
        for s in range(K):
            step(i, s)
    for t in range((n // K - 1) * K, n):
        step(t // K, t % K)


def skewed(eng, n, stages, k, ahead=0, peel=2):
    def step(i, s):
        for lag, f in stages:
            c, r = divmod(s - lag, k)
            j = i + c if c else i
            if not isinstance(j, int) or 0 <= j * k + r < n:
                f(j, r)

    end = (n - 1 - ahead) // k
    for t in range(-ahead, peel * k):
        step(*divmod(t, k))
    with eng.Fori(peel, end) as i:
        for s in range(k):
            step(i, s)
    for t in range(end * k, n + max(lag for lag, _ in stages)):
        step(*divmod(t, k))


def back(i, s, k):
    return (i, s - k) if s >= k else (i - 1, s - k + K)


def exists(i):
    return not isinstance(i, int) or i >= 0


def later(i):
    return not isinstance(i, int) or i >= 1


def hold(eng, sem, value, held):
    eng.wait_ge(sem, value)
    eng.sem_inc(held, 1)


def load_edges(nc, g):
    with ExitStack() as ctx:
        a4 = ctx.enter_context(nc.sbuf_tensor("a4_in", [P, ET * 4], F32))
        a8 = ctx.enter_context(nc.sbuf_tensor("a8_in", [P, ET * 8], F32))
        his = ctx.enter_context(nc.sbuf_tensor("hi_int", [P, 2, ET], I32))
        los = ctx.enter_context(nc.sbuf_tensor("lo_int", [P, 2, ET], I32))
        hif = ctx.enter_context(nc.sbuf_tensor("hi_f", [P, 2, ET], F32))
        lof = ctx.enter_context(nc.sbuf_tensor("lo_f", [P, 2, ET], F32))
        ids = ctx.enter_context(nc.sbuf_tensor("ids_int", [P, 2, ET], I32))
        iota = g.iota
        sem = lambda n: nc.alloc_semaphore(n)
        filled, loaded, attrs_loaded, made = sem("le_filled"), sem("le_loaded"), sem("le_attrs"), sem("le_made")
        block = ctx.enter_context(nc.Block())

        @block.sync
        def _(sp):
            sp.wait_ge(filled, 1)
            sp.dma_start(ids[0:EP, 0, :], g.src.rearrange("(p t) -> p t", t=ET)).then_inc(loaded, 16)
            sp.dma_start(ids[0:EP, 1, :], g.dst.rearrange("(p t) -> p t", t=ET)).then_inc(loaded, 16)
            sp.dma_start(a4[0:EP, :], g.edge_attr_4.rearrange("(p t) c -> p (t c)", t=ET)).then_inc(attrs_loaded, 16)
            sp.dma_start(a8[0:EP, :], g.edge_attr_8.rearrange("(p t) c -> p (t c)", t=ET)).then_inc(attrs_loaded, 16)

        @block.gpsimd
        def _(pool):
            nc.gpsimd.iota(iota[:, :], [[1, P]], base=0, channel_multiplier=0,
                           allow_small_or_imprecise_dtypes=True).then_inc(made, 1)
            nc.gpsimd.memset(g.ident[:, :], 0.0).then_inc(made, 1)
            nc.gpsimd.memset(g.ones[:, :], 1.0).then_inc(made, 1)
            nc.gpsimd.memset(g.before[:, :], 1.0).then_inc(made, 1)
            pool.wait_ge(made, 4)
            nc.gpsimd.affine_select(out=g.ident[:, :], in_=g.ident[:, :], compare_op=ALU.not_equal, fill=1.0,
                                    base=0, pattern=[[-1, P]], channel_multiplier=1).then_inc(made, 1)
            nc.gpsimd.affine_select(out=g.before[:, :], in_=g.before[:, :], compare_op=ALU.is_gt, fill=0.0,
                                    base=0, pattern=[[1, P]], channel_multiplier=-1).then_inc(made, 1)

        @block.vector
        def _(dve):
            nc.vector.memset(ids[:, :, :], PAD_NODE).then_inc(filled, 1)
            nc.vector.memset(g.rec_in[:, :, :], 0.0).then_inc(filled, 1)
            dve.wait_ge(made, 6)
            nc.vector.tensor_copy(g.ident_bf[:, :], g.ident[:, :])
            nc.vector.tensor_copy(g.last_row[:, :], g.ident[:, P - 1:P])
            nc.vector.tensor_tensor(g.after[:, :], g.ones[:, :], g.before[:, :], ALU.subtract).then_inc(filled, 1)
            dve.wait_ge(filled, 3)
            nc.vector.tensor_tensor(g.after[:, :], g.after[:, :], g.ident[:, :], ALU.subtract)
            dve.wait_ge(loaded, 32)
            nc.vector.tensor_scalar(his[:, :, :], ids[:, :, :], 7, None, ALU.arith_shift_right).then_inc(filled, 1)
            nc.vector.tensor_scalar(los[:, :, :], ids[:, :, :], P - 1, None, ALU.bitwise_and).then_inc(filled, 1)
            nc.vector.tensor_copy(g.keys[:, :, :], ids[:, :, :]).then_inc(filled, 1)
            dve.wait_ge(filled, 6)
            nc.vector.tensor_copy(hif[:, :, :], his[:, :, :]).then_inc(filled, 1)
            nc.vector.tensor_copy(lof[:, :, :], los[:, :, :]).then_inc(filled, 1)
            dve.wait_ge(filled, 8)
            for o in range(2):
                nc.vector.tensor_tensor(g.hot_hi[:, o, :, :], iota[:, 0:NT].unsqueeze(1).to_broadcast([P, ET, NT]),
                                        hif[:, o, :].unsqueeze(2).to_broadcast([P, ET, NT]), ALU.is_equal)
                nc.vector.tensor_tensor(g.hot_lo[:, o, :, :], iota[:, :].unsqueeze(1).to_broadcast([P, ET, P]),
                                        lof[:, o, :].unsqueeze(2).to_broadcast([P, ET, P]), ALU.is_equal)
                nc.vector.tensor_copy(g.rec_in[:, :, o], g.keys[:, o, :])
            dve.wait_ge(attrs_loaded, 32)
            nc.vector.tensor_copy(g.rec_in[0:EP, :, 2:6], a4[0:EP, :].rearrange("p (t c) -> p t c", c=4))
            nc.vector.tensor_copy(g.rec_in[0:EP, :, 6:14], a8[0:EP, :].rearrange("p (t c) -> p t c", c=8))


def sort_positions(nc, g):
    with ExitStack() as ctx:
        sb = lambda n, s, d=F32: ctx.enter_context(nc.sbuf_tensor(n, s, d))
        sem = lambda n: nc.alloc_semaphore(n)
        total, upto = sb("total", [NT, 2, P]), sb("upto", [NT, 2, P])
        row_start, spare = sb("row_start", [NT, 2]), sb("spare", [NT, 2, P])
        running = [sb(f"running{s}", [NT, 2, P]) for s in range(2)]
        hot_T = [sb(f"hot_T{s}", [NT, 2, P]) for s in range(2)]
        key_diag = [sb(f"key_diag{s}", [P, 2, P]) for s in range(2)]
        picked, tied = sb("picked", [P, 2, ET]), sb("tied", [P, 2, ET])
        scrap = [sb(f"scrap{s}", [P, 4, P]) for s in range(2)]
        zeros, ndeg, root = sb("zeros", [NT, P]), sb("ndeg", [NT, P]), sb("root", [NT, 4, P])
        ps_total = ctx.enter_context(nc.psum_tensor("ps_total", [NT, 4, P], F32))
        ps_total2 = ctx.enter_context(nc.psum_tensor("ps_total2", [NT, 4, P], F32))
        ps_hot = [ctx.enter_context(nc.psum_tensor(f"ps_hot{s}", [NT, 4, P], F32)) for s in range(2)]
        ps_key = [ctx.enter_context(nc.psum_tensor(f"ps_key{s}", [P, 4, P], F32)) for s in range(2)]
        ps_pick = [ctx.enter_context(nc.psum_tensor(f"ps_pick{s}", [P, 4, P], F32)) for s in range(2)]
        counted, summed, started, chain = sem("so_counted"), sem("so_summed"), sem("so_started"), sem("so_chain")
        hot_ready, hot_copied, diag_ready = sem("so_hot_ready"), sem("so_hot_copied"), sem("so_diag_ready")
        key_ready, picked_ready, tile_done = sem("so_key_ready"), sem("so_picked_ready"), sem("so_tile_done")
        table_ready, turned, stored = sem("so_table_ready"), sem("so_turned"), sem("so_stored")
        cols_ready, running_ready = sem("so_cols_ready"), sem("so_running_ready")
        zeroed, zeros_stored = sem("so_zeroed"), sem("so_zeros_stored")
        block = ctx.enter_context(nc.Block())

        @block.gpsimd
        def _(pool):
            nc.gpsimd.memset(g.zeros[:, :], 0.0).then_inc(zeroed, 1)

        @block.tensor
        def _(pe):
            for o, ps in ((0, ps_total), (1, ps_total2)):
                nc.tensor.matmul(ps[:, 0, :], g.hot_hi[:, o, 0, :], g.hot_lo[:, o, 0, :], start=True, stop=False)
                with pe.Fori(1, ET - 1) as t:
                    nc.tensor.matmul(ps[:, 0, :], g.hot_hi[:, o, bass.ds(t, 1), :].rearrange("p a b -> p (a b)"),
                                     g.hot_lo[:, o, bass.ds(t, 1), :].rearrange("p a b -> p (a b)"),
                                     start=False, stop=False)
                nc.tensor.matmul(ps[:, 0, :], g.hot_hi[:, o, ET - 1, :], g.hot_lo[:, o, ET - 1, :],
                                 start=False, stop=True).then_inc(counted, 1)
            pe.wait_ge(summed, 1)
            nc.tensor.matmul(ps_total[:, 1, 0:2], g.before[0:NT, 0:NT], upto[:, :, P - 1], start=True,
                             stop=True).then_inc(started, 1)

            def step(t, s, first, last):
                if not first:
                    pe.wait_ge(hot_copied, t - 1)
                    pe.wait_ge(tile_done, t - 1)
                for o in range(2):
                    hot = g.hot_hi[:, o, bass.ds(t, 1), :].rearrange("p a b -> p (a b)")
                    nc.tensor.matmul(ps_hot[s][:, o, :], hot, g.ident_bf[:, :], start=True, stop=True)
                    m = nc.tensor.matmul(ps_key[s][0:NT, 2 + o, :], hot,
                                         g.hot_lo[:, o, bass.ds(t, 1), :].rearrange("p a b -> p (a b)"),
                                         start=True, stop=True)
                m.then_inc(hot_ready, 1)
                pe.wait_ge(diag_ready, t + 1)
                for o in range(2):
                    m = nc.tensor.matmul(ps_key[s][:, o, :], g.ones[:, :], key_diag[s][:, o, :], start=True, stop=True)
                m.then_inc(key_ready, 1)
                pe.wait_ge(hot_copied, t + 1)
                pe.wait_ge(running_ready, t + 1)
                for o in range(2):
                    m = nc.tensor.matmul(ps_pick[s][:, o, :], hot_T[s][:, o, :], running[s][:, o, :],
                                         start=True, stop=True)
                m.then_inc(picked_ready, 1)

            tile_loop(pe, ET, step)
            pe.wait_ge(table_ready, 1)
            for n in range(3):
                m = nc.tensor.transpose(ps_key[0][:, n, 0:NT], g.ntab[:, :, n], g.ident[0:NT, 0:NT])
            m.then_inc(turned, 1)

        @block.scalar
        def _(act):
            def step(t, s, first, last):
                if not first:
                    act.wait_ge(key_ready, t - 1)
                for o in range(2):
                    m = nc.scalar.activation(key_diag[s][:, o, :], g.ident[:, :], ACT.Copy,
                                             scale=g.keys[:, o, bass.ds(t, 1)])
                m.then_inc(diag_ready, 1)
                act.wait_ge(hot_ready, t + 1)
                if not first:
                    act.wait_ge(picked_ready, t - 1)
                nc.scalar.activation(hot_T[s][:, :, :], ps_hot[s][:, 0:2, :], ACT.Copy).then_inc(hot_copied, 1)

            tile_loop(act, ET, step)
            act.wait_ge(cols_ready, 1)
            nc.scalar.activation(ndeg[:, :], total[:, 1, :], ACT.Sqrt, bias=g.one_col[0:NT, :]).then_inc(cols_ready, 1)

        @block.vector
        def _(dve):
            n_chain = [0]

            def link(ins):
                n_chain[0] += 1
                ins.then_inc(chain, 1)
                dve.wait_ge(chain, n_chain[0])

            nc.vector.memset(zeros[:, :], 0.0)
            link(nc.vector.memset(g.one_col[:, :], 1.0))
            dve.wait_ge(counted, 2)
            nc.vector.tensor_copy(total[:, 0, :], ps_total[:, 0, :])
            link(nc.vector.tensor_copy(total[:, 1, :], ps_total2[:, 0, :]))
            for o in range(2):
                m = nc.vector.tensor_tensor_scan(upto[:, o, :], total[:, o, :], zeros[:, :], 0.0, ALU.add, ALU.add)
            m.then_inc(summed, 1)
            dve.wait_ge(started, 1)
            link(nc.vector.tensor_copy(row_start[:, :], ps_total[:, 1, 0:2]))
            for o in range(2):
                link(nc.vector.tensor_scalar(upto[:, o, :], upto[:, o, :], row_start[:, o:o + 1], None, ALU.add))
            nc.vector.tensor_tensor(running[0][:, :, :], upto[:, :, :], total[:, :, :], ALU.subtract)\
              .then_inc(running_ready, 1)
            dve.wait_ge(running_ready, 1)

            def step(t, s, first, last):
                dve.wait_ge(key_ready, t + 1)
                if not first:
                    dve.wait_ge(picked_ready, t)
                elif s == 1:
                    dve.wait_ge(picked_ready, 1)
                nc.vector.tensor_tensor(running[1 - s][:, :, :], running[s][:, :, :], ps_key[s][0:NT, 2:4, :],
                                        ALU.add).then_inc(running_ready, 1)
                if not first:
                    dve.wait_ge(tile_done, t - 1)
                for o in range(2):
                    nc.vector.scalar_tensor_tensor(scrap[s][:, o, :], ps_key[s][:, o, :], g.keys[:, o, bass.ds(t, 1)],
                                                   g.after[:, :], ALU.is_equal, ALU.mult,
                                                   accum_out=tied[:, o, bass.ds(t, 1)])
                dve.wait_ge(picked_ready, t + 1)
                for o in range(2):
                    m = nc.vector.scalar_tensor_tensor(scrap[s][:, 2 + o, :], ps_pick[s][:, o, :], 1.0,
                                                       g.hot_lo[:, o, bass.ds(t, 1), :].rearrange("p a b -> p (a b)"),
                                                       ALU.mult, ALU.mult, accum_out=picked[:, o, bass.ds(t, 1)])
                m.then_inc(tile_done, 1)
                dve.wait_ge(running_ready, t + 2)

            tile_loop(dve, ET, step)
            dve.wait_ge(tile_done, ET)
            nc.vector.tensor_tensor(g.position[:, :, :], picked[:, :, :], tied[:, :, :], ALU.add)
            for o in range(2):
                link(nc.vector.scalar_tensor_tensor(spare[:, o, :], g.iota[0:NT, :], float(EPAD + 1), upto[:, o, :],
                                                    ALU.add, ALU.subtract))
            link(nc.vector.scalar_tensor_tensor(spare[:, :, :], total[:, :, :], 0.5, spare[:, :, :],
                                                ALU.is_lt, ALU.mult))
            link(nc.vector.tensor_tensor(upto[:, :, :], upto[:, :, :], spare[:, :, :], ALU.add))
            for o in range(2):
                nc.vector.tensor_scalar(g.ntab[:, :, o], upto[:, o, :], 1.0, None, ALU.subtract)
            m = nc.vector.memset(g.ntab[:, :, 3], 0.0)
            m.then_inc(cols_ready, 1)
            dve.wait_ge(cols_ready, 2)
            link(nc.vector.reciprocal(root[:, 0, :], ndeg[:, :]))
            link(nc.vector.tensor_tensor(root[:, 1, :], root[:, 0, :], root[:, 0, :], ALU.mult))
            link(nc.vector.scalar_tensor_tensor(root[:, 2, :], total[:, 1, :], 1.0, root[:, 1, :], ALU.add, ALU.mult))
            link(nc.vector.tensor_scalar(root[:, 3, :], root[:, 2, :], -0.5, 1.5, ALU.mult, ALU.add))
            nc.vector.tensor_tensor(g.ntab[:, :, 2], root[:, 0, :], root[:, 3, :], ALU.mult).then_inc(table_ready, 1)
            dve.wait_ge(turned, 1)
            nc.vector.tensor_copy(g.node_row[:, 0, :], ps_key[0][:, 0, 0:NT])
            nc.vector.tensor_copy(g.node_row[:, 1, :], ps_key[0][:, 1, 0:NT])
            nc.vector.tensor_copy(g.dis[:, :], ps_key[0][:, 2, 0:NT])

        @block.sync
        def _(sp):
            sp.wait_ge(zeroed, 1)
            for table in g.summed_tables:
                sp.dma_start(table[EPAD:TROWS, :], g.zeros[:, :]).then_inc(zeros_stored, 16)
            sp.wait_ge(zeros_stored, 16 * len(g.summed_tables))
            sp.wait_ge(table_ready, 1)
            sp.dma_start(g.ntab_dram.rearrange("(h l) c -> h l c", l=P), g.ntab[:, :, :]).then_inc(stored, 16)
            sp.wait_ge(stored, 16)


def scatter_tile(nc, g, o, rec_out, pos_out, s, done):
    nc.gpsimd.indirect_dma_start(g.rec_dram[o], bass.IndirectOffsetOnAxis(pos_out[:, s:s + 1], 0),
                                 rec_out[:, s, :], None, bounds_check=g.last_edge, oob_is_err=False).then_inc(done, 16)


def stage_tile(nc, g, o, rec_out, pos_out, t, s, staged):
    nc.vector.tensor_scalar(rec_out[:, s, :], g.rec_in[:, bass.ds(t, 1), :].rearrange("p a b -> p (a b)"),
                            0.0, None, ALU.add)
    nc.vector.tensor_scalar(pos_out[:, s:s + 1], g.position[:, o, bass.ds(t, 1)], 0.0, None, ALU.add)\
      .then_inc(staged, 1)


def sorted_ids(nc, g, o, dve, done):
    nc.vector.tensor_copy(g.src_any[:, o, :], g.rec[o][:, :, 0])
    nc.vector.tensor_scalar(g.src_row[:, o, :], g.rec[o][:, :, 0], float(N - 1), None, ALU.min)
    nc.vector.tensor_scalar(g.dst_row[:, o, :], g.rec[o][:, :, 1], float(N - 1), None, ALU.min)
    nc.vector.memset(g.prev_last[:, o, 0:1], -1.0)
    nc.vector.tensor_scalar(g.prev_last[:, o, 1:ET], g.rec[o][:, 0:ET - 1, o], 1.0,
                            g.last_row[:, 0:1], ALU.add, ALU.mult).then_inc(done, 1)
    dve.wait_ge(done, 1)
    nc.vector.tensor_scalar(g.prev_last[:, o, 1:ET], g.prev_last[:, o, 1:ET], 1.0, None, ALU.subtract).then_inc(done, 1)


def sort_by_dst(nc, g):
    S = 8
    with ExitStack() as ctx:
        sb = lambda n, s, d=F32: ctx.enter_context(nc.sbuf_tensor(f"sd_{n}", s, d))
        sem = lambda n: nc.alloc_semaphore(f"sd_{n}")
        rec_out, pos_out = sb("rec_out", [P, S, REC]), sb("pos_out", [P, S], I32)
        scattered = [sem(f"scattered{s}") for s in range(S)]
        staged, held, reloaded, ids_ready = sem("staged"), sem("held"), sem("reloaded"), sem("ids_ready")
        block = ctx.enter_context(nc.Block())

        @block.gpsimd
        def _(pool):
            g.last_edge = pool.to_reg(EPAD - 1)

            def scatter(i, s):
                hold(pool, staged, i * S + s + 1, held)
                scatter_tile(nc, g, 1, rec_out, pos_out, s, scattered[s])

            skewed(pool, ET, [(0, scatter)], S)

        @block.vector
        def _(dve):
            def stage(i, s):
                if later(i):
                    dve.wait_ge(scattered[s], i * 16)
                stage_tile(nc, g, 1, rec_out, pos_out, i * S + s, s, staged)

            skewed(dve, ET, [(0, stage)], S)
            nc.vector.memset(g.eps_col[:, :], 1e-5)
            dve.wait_ge(reloaded, 16)
            sorted_ids(nc, g, 1, dve, ids_ready)

        @block.sync
        def _(sp):
            for s in range(S):
                sp.wait_ge(scattered[s], ET // S * 16)
            sp.dma_start(g.rec[1][:, :, :], g.rec_dram[1].rearrange("(t p) c -> p t c", p=P)).then_inc(reloaded, 16)


def load_split(nc, weights):
    with ExitStack() as ctx:
        names = [w[0] for w in weights]
        full = [ctx.enter_context(nc.sbuf_tensor(f"full_{n}", list(hi.shape), F32)) for n, _, hi, _ in weights]
        loaded = [nc.alloc_semaphore(f"ls_loaded_{n}") for n in names]
        high = nc.alloc_semaphore(f"ls_high_{names[0]}")
        low = nc.alloc_semaphore(f"ls_low_{names[0]}")
        block = ctx.enter_context(nc.Block())

        @block.sync
        def _(sp):
            for (_, src, _, _), f, sem in zip(weights, full, loaded):
                sp.dma_start(f[:, :, :], src).then_inc(sem, 16)

        @block.scalar
        def _(act):
            for (_, _, hi, _), f, sem in zip(weights, full, loaded):
                act.wait_ge(sem, 16)
                nc.scalar.activation(hi[:, :, :], f[:, :, :], ACT.Copy).then_inc(high, 1)

        @block.vector
        def _(dve):
            for k, ((_, _, hi, lo), f, sem) in enumerate(zip(weights, full, loaded)):
                dve.wait_ge(sem, 16)
                dve.wait_ge(high, k + 1)
                nc.vector.tensor_tensor(lo[:, :, :], f[:, :, :], hi[:, :, :].bitcast(F32), ALU.subtract)\
                  .then_inc(low, 1)


def split_weight(nc, ctx, name, src, k, n):
    hi = ctx.enter_context(nc.sbuf_tensor(f"{name}_hi", [P, k, n], F32R))
    lo = ctx.enter_context(nc.sbuf_tensor(f"{name}_lo", [P, k, n], F32R))
    return (name, src.rearrange("(k p) n -> p k n", p=P), hi, lo)


def edge_sums(nc, g, tag, rows, out, comp=None, comp_order=0, by_degree=False, normed=True):
    S, B = 6, 3
    with ExitStack() as ctx:
        sb = lambda n, s, d=F32: ctx.enter_context(nc.sbuf_tensor(f"{tag}_{n}", s, d))
        sem = lambda n: nc.alloc_semaphore(f"{tag}_{n}")
        x = [sb(f"x{s}", [P, D]) for s in range(S)]
        same = [sb(f"same{s}", [P, P]) for s in range(S)]
        carry = [sb(f"carry{s}", [P, P]) for s in range(S)]
        sums = [sb(f"sums{s}", [P, D]) for s in range(S)]
        row_idx = sb("row_idx", [P, S], I32)
        ps = [ctx.enter_context(nc.psum_tensor(f"{tag}_ps{s}", [P, D], F32)) for s in range(B)]
        m, lag = x, 2
        if normed:
            lag = 6
            comp_idx = sb("comp_idx", [P, S], I32)
            m = [sb(f"m{s}", [P, D]) for s in range(S)]
            stats, mv = sb("stats", [P, S, 6]), sb("mv", [P, S, 2])
            std, rstd, shift, rdis = (sb(n, [P, S]) for n in ("std", "rstd", "shift", "rdis"))
        got_x, got_c = [sem(f"got_x{s}") for s in range(S)], [sem(f"got_c{s}") for s in range(S)]
        stored = [sem(f"stored{s}") for s in range(S)]
        ready, comp_ready, held = sem("rows_ready"), sem("comp_ready"), sem("held")
        measured, var_ready, std_ready = sem("measured"), sem("var_ready"), sem("std_ready")
        inverted, coef_ready, m_ready, masks_ready = sem("inverted"), sem("coef_ready"), sem("m_ready"), sem("masks_ready")
        summed, emptied, scaled = sem("summed"), sem("emptied"), sem("scaled")
        block = ctx.enter_context(nc.Block())

        @block.gpsimd
        def _(pool):
            last_row, last_sum = pool.to_reg(N - 1), pool.to_reg(TROWS - 1)

            def gather(i, s):
                t = i * S + s
                if later(i):
                    pool.wait_ge(m_ready if normed else summed, t - S + 1)
                hold(pool, ready, t + 1, held)
                nc.gpsimd.indirect_dma_start(x[s][:, :], None, rows, bass.IndirectOffsetOnAxis(row_idx[:, s:s + 1], 0),
                                             bounds_check=last_row, oob_is_err=False).then_inc(got_x[s], 16)

            def add_sums(i, s):
                pool.wait_ge(comp_ready, i * S + s + 1)
                hold(pool, got_x[s], i * 16 + 16, held)
                nc.gpsimd.indirect_dma_start(x[s][:, :], None, comp, bass.IndirectOffsetOnAxis(comp_idx[:, s:s + 1], 0),
                                             bounds_check=last_sum, compute_op=ALU.add).then_inc(got_c[s], 16)

            skewed(pool, ET, [(0, gather), (2, add_sums)] if normed else [(0, gather)], S)

        @block.vector
        def _(dve):
            def stage(i, s):
                t = i * S + s
                if later(i):
                    dve.wait_ge(got_x[s], i * 16)
                nc.vector.tensor_scalar(row_idx[:, s:s + 1], g.src_row[:, 1, bass.ds(t, 1)], 0.0, None, ALU.add)\
                  .then_inc(ready, 1)
                if normed:
                    if later(i):
                        dve.wait_ge(got_c[s], i * 16)
                    nc.vector.tensor_scalar(comp_idx[:, s:s + 1], g.src_comp[:, comp_order, bass.ds(t, 1)],
                                            0.0, None, ALU.add).then_inc(comp_ready, 1)

            def measure(i, s):
                t = i * S + s
                dve.wait_ge(got_c[s], i * 16 + 16)
                nc.vector.bn_stats(stats[:, s, :], x[s][:, :]).then_inc(measured, 1)

            def aggregate(i, s):
                hold(dve, measured, i * S + s + 1, held)
                nc.vector.bn_aggr(mv[:, s, :], stats[:, s, :]).then_inc(var_ready, 1)

            def masks(i, s):
                t = i * S + s
                if later(i):
                    dve.wait_ge(summed, t - S + 1)
                nc.vector.tensor_scalar(same[s][:, :], g.key_row[:, 1, bass.ds(t * P, P)],
                                        g.rec[1][:, bass.ds(t, 1), 1], None, ALU.is_equal)
                nc.vector.tensor_scalar(carry[s][:, :], g.key_row[:, 1, bass.ds(t * P, P)],
                                        g.prev_last[:, 1, bass.ds(t, 1)], None, ALU.is_equal).then_inc(masks_ready, 1)

            def coefs(i, s):
                t = i * S + s
                dve.wait_ge(std_ready, t + 1)
                nc.vector.reciprocal(rstd[:, s:s + 1], std[:, s:s + 1]).then_inc(inverted, 1)
                dve.wait_ge(inverted, t + 1)
                if by_degree:
                    nc.vector.tensor_scalar(rdis[:, s:s + 1], rstd[:, s:s + 1], g.src_tab[:, bass.ds(t, 1), 2],
                                            None, ALU.mult).then_inc(scaled, 1)
                    dve.wait_ge(scaled, t + 1)
                r = rdis if by_degree else rstd
                nc.vector.tensor_scalar(shift[:, s:s + 1], mv[:, s, 0:1], r[:, s:s + 1], -1.0,
                                        ALU.mult, ALU.mult).then_inc(coef_ready, 1)

            skewed(dve, ET, [(-1, stage), (4, measure), (lag - 1, masks), (4, aggregate), (5, coefs)] if normed else
                   [(-1, stage), (lag - 1, masks)], S, ahead=1)

        @block.scalar
        def _(act):
            def root(i, s):
                act.wait_ge(var_ready, i * S + s + 1)
                nc.scalar.activation(std[:, s:s + 1], mv[:, s, 1:2], ACT.Sqrt, bias=g.eps_col[:, :]).then_inc(std_ready, 1)

            def apply(i, s):
                t = i * S + s
                act.wait_ge(coef_ready, t + 1)
                if later(i):
                    act.wait_ge(summed, t - S + 1)
                nc.scalar.activation(m[s][:, :], x[s][:, :], ACT.Identity, bias=shift[:, s:s + 1],
                                     scale=(rdis if by_degree else rstd)[:, s:s + 1]).then_inc(m_ready, 1)

            def empty(i, s):
                act.wait_ge(summed, i * S + s + 1)
                if later(i):
                    act.wait_ge(stored[s], i * 16)
                nc.scalar.activation(sums[s][:, :], ps[s % B][:, :], ACT.Copy).then_inc(emptied, 1)

            skewed(act, ET, [(5, apply), (6, empty), (4, root)] if normed else [(lag, empty)], S)

        @block.tensor
        def _(pe):
            def total(i, s):
                t = i * S + s
                pe.wait_ge(masks_ready, t + 1)
                if normed:
                    pe.wait_ge(m_ready, t + 1)
                else:
                    pe.wait_ge(got_x[s], i * 16 + 16)
                alone = isinstance(t, int) and t == 0
                if not (isinstance(t, int) and t < B):
                    pe.wait_ge(emptied, t - B + 1)
                last = nc.tensor.matmul(ps[s % B][:, :], same[s][:, :], m[s][:, :], start=True, stop=alone)
                if not alone:
                    pe.wait_ge(emptied, t)
                    last = nc.tensor.matmul(ps[s % B][:, :], carry[s][:, :], sums[s - 1][:, :], start=False, stop=True)
                last.then_inc(summed, 1)

            skewed(pe, ET, [(lag, total)], S)

        @block.sync
        def _(sp):
            def store(i, s):
                t = i * S + s
                sp.wait_ge(emptied, t + 1)
                sp.dma_start(out[bass.ds(t * P, P), :], sums[s][:, :]).then_inc(stored[s], 16)

            skewed(sp, ET, [(lag, store)], S)
            for s in range(S):
                sp.wait_ge(stored[s], len(range(s, ET, S)) * 16)


BIG = 3.0e38
HEADS = 8
DK = D // HEADS


def edge_logits(nc, g, x, weights, biases, v_dram):
    with ExitStack() as ctx:
        sb = lambda n, s, d=F32: ctx.enter_context(nc.sbuf_tensor(f"el_{n}", s, d))
        pb = lambda n, s: ctx.enter_context(nc.psum_tensor(f"el_{n}", s, F32))
        sem = lambda n: nc.alloc_semaphore(f"el_{n}")
        split = [split_weight(nc, ctx, n, w, KC, D) for n, w in zip(("wq", "wk", "wv"), weights)]
        load_split(nc, split)
        (_, _, wq_hi, wq_lo), (_, _, wk_hi, wk_lo), (_, _, wv_hi, wv_lo) = split
        xs, xd = [sb(f"xs{s}", [P, D]) for s in range(K)], [sb(f"xd{s}", [P, D]) for s in range(K)]
        xT_hi = [[sb(f"xT_hi{w}{s}", [P, KC, P], F32R) for s in range(2)] for w in range(2)]
        xT_lo = [[sb(f"xT_lo{w}{s}", [P, KC, P], F32R) for s in range(2)] for w in range(2)]
        q, k, prod = [sb(f"q{s}", [P, D]) for s in range(2)], [sb(f"k{s}", [P, D]) for s in range(2)], [sb(f"qk{s}", [P, D]) for s in range(2)]
        v = [sb(f"v{s}", [P, D]) for s in range(K)]
        bias = [sb(f"bias{n}", [P, D]) for n in range(3)]
        dots, logit = sb("dots", [P, K, HEADS]), sb("logit", [P, K, HEADS])
        idx = sb("idx", [P, 2, K], I32)
        psT = [pb(f"psT{w}", [P, KC, P]) for w in range(2)]
        psq, psk, psv, psL = [pb(f"psq{s}", [P, D]) for s in range(2)], [pb(f"psk{s}", [P, D]) for s in range(2)], pb("psv", [P, D]), pb("psL", [HEADS, P])
        got = [[sem(f"got{w}{s}") for s in range(K)] for w in range(2)]
        ready, held, bias_in = sem("slot_ready"), sem("held"), sem("bias_in")
        turned, high, low = sem("turned"), sem("high"), sem("low")
        q_done, k_done, v_done = sem("q_done"), sem("k_done"), sem("v_done")
        q_out, k_out, v_out, multiplied, reduced = sem("q_out"), sem("k_out"), sem("v_out"), sem("multiplied"), sem("reduced")
        logit_ready, logit_turned, logit_kept = sem("logit_ready"), sem("logit_turned"), sem("logit_kept")
        stored = [sem(f"stored{s}") for s in range(K)]
        block = ctx.enter_context(nc.Block())

        @block.gpsimd
        def _(pool):
            last_row = pool.to_reg(N - 1)

            def step(i, s):
                t = i * K + s
                if later(i):
                    pool.wait_ge(turned, t - K + 1)
                hold(pool, ready, t + 1, held)
                for w, x_w in enumerate((xs, xd)):
                    nc.gpsimd.indirect_dma_start(x_w[s][:, :], None, x,
                                                 bass.IndirectOffsetOnAxis(idx[:, w, s:s + 1], 0),
                                                 bounds_check=last_row, oob_is_err=False).then_inc(got[w][s], 16)

            rounds(pool, ET, step)

        @block.tensor
        def _(pe):
            def project(i, s):
                t, h = i * K + s, s % 2
                pe.wait_ge(low, t + 1)
                for ps, w, (hi, lo), done, out in ((psq[h], 0, (wq_hi, wq_lo), q_done, q_out),
                                                   (psk[h], 1, (wk_hi, wk_lo), k_done, k_out),
                                                   (psv, 1, (wv_hi, wv_lo), v_done, v_out)):
                    if ps is psv:
                        if exists(back(i, s, 1)[0]):
                            pe.wait_ge(out, t)
                    elif exists(back(i, s, 2)[0]):
                        pe.wait_ge(out, t - 1)
                    n = 0
                    for a, b in ((xT_hi, hi), (xT_hi, lo), (xT_lo, hi)):
                        for c in range(KC):
                            last = nc.tensor.matmul(ps[:, :], a[w][h][:, c, :], b[:, c, :], start=n == 0,
                                                    stop=n == 3 * KC - 1)
                            n += 1
                    last.then_inc(done, 1)

            def turn_logits(i, s):
                t = i * K + s
                pe.wait_ge(logit_ready, t + 1)
                if not (isinstance(t, int) and t == 0):
                    pe.wait_ge(logit_kept, t)
                nc.tensor.transpose(psL[:, :], logit[:, s, :], g.ident[:, :]).then_inc(logit_turned, 1)

            def step(i, s):
                t = i * K + s
                for w, x_w in enumerate((xs, xd)):
                    pe.wait_ge(got[w][s], i * 16 + 16)
                if not (isinstance(t, int) and t == 0):
                    pe.wait_ge(low, t)
                for w, x_w in enumerate((xs, xd)):
                    for c in range(KC):
                        last = nc.tensor.transpose(psT[w][:, c, :], x_w[s][:, c * P:(c + 1) * P], g.ident[:, :])
                last.then_inc(turned, 1)
                if exists(back(i, s, 1)[0]):
                    project(*back(i, s, 1))
                if exists(back(i, s, 2)[0]):
                    turn_logits(*back(i, s, 2))

            rounds(pe, ET, step)
            project(ET // K - 1, K - 1)
            turn_logits(ET // K - 1, K - 2)
            turn_logits(ET // K - 1, K - 1)

        @block.scalar
        def _(act):
            def keep_logits(i, s):
                t = i * K + s
                act.wait_ge(logit_turned, t + 1)
                nc.scalar.activation(g.logits_T[:, bass.ds(t * P, P)], psL[:, :], ACT.Copy).then_inc(logit_kept, 1)

            def step(i, s):
                t = i * K + s
                act.wait_ge(turned, t + 1)
                if exists(back(i, s, 2)[0]):
                    act.wait_ge(v_done, t - 1)
                for w in range(2):
                    last = nc.scalar.activation(xT_hi[w][s % 2][:, :, :], psT[w][:, :, :], ACT.Copy)
                last.then_inc(high, 1)
                if exists(back(i, s, 3)[0]):
                    keep_logits(*back(i, s, 3))

            rounds(act, ET, step)
            for b in range(3, 0, -1):
                keep_logits(ET // K - 1, K - b)

        @block.vector
        def _(dve):
            def stage(t, s):
                nc.vector.tensor_scalar(idx[:, 0, s:s + 1], g.src_row[:, 0, bass.ds(t, 1)], 0.0, None, ALU.add)
                nc.vector.tensor_scalar(idx[:, 1, s:s + 1], g.dst_row[:, 0, bass.ds(t, 1)], 0.0, None, ALU.add)\
                  .then_inc(ready, 1)

            for s in range(K):
                stage(s, s)
            dve.wait_ge(bias_in, 48)

            def finish(i, s):
                t, h = i * K + s, s % 2
                dve.wait_ge(q_done, t + 1)
                if exists(back(i, s, 2)[0]):
                    dve.wait_ge(multiplied, t - 1)
                nc.vector.tensor_tensor(q[h][:, :], psq[h][:, :], bias[0][:, :], ALU.add).then_inc(q_out, 1)
                dve.wait_ge(k_done, t + 1)
                nc.vector.tensor_tensor(k[h][:, :], psk[h][:, :], bias[1][:, :], ALU.add).then_inc(k_out, 1)
                dve.wait_ge(k_out, t + 1)
                dve.wait_ge(q_out, t + 1)
                if exists(back(i, s, 2)[0]):
                    dve.wait_ge(reduced, t - 1)
                nc.vector.tensor_tensor(prod[h][:, :], q[h][:, :], k[h][:, :], ALU.mult).then_inc(multiplied, 1)
                dve.wait_ge(v_done, t + 1)
                if later(i):
                    dve.wait_ge(stored[s], i * 16)
                nc.vector.tensor_tensor(v[s][:, :], psv[:, :], bias[2][:, :], ALU.add).then_inc(v_out, 1)
                dve.wait_ge(multiplied, t + 1)
                if later(i):
                    dve.wait_ge(logit_ready, t - K + 1)
                nc.vector.tensor_reduce(dots[:, s, :], prod[h][:, :].rearrange("p (h d) -> p h d", h=HEADS),
                                        AX.X, ALU.add).then_inc(reduced, 1)
                dve.wait_ge(reduced, t + 1)
                if later(i):
                    dve.wait_ge(logit_turned, t - K + 1)
                nc.vector.scalar_tensor_tensor(logit[:, s, :], dots[:, s, :], float(DK) ** -0.5,
                                               g.rec[0][:, bass.ds(t, 1), 6:14].rearrange("p a b -> p (a b)"),
                                               ALU.mult, ALU.add).then_inc(logit_ready, 1)

            def step(i, s):
                t = i * K + s
                dve.wait_ge(high, t + 1)
                for w in range(2):
                    last = nc.vector.tensor_tensor(xT_lo[w][s % 2][:, :, :], psT[w][:, :, :],
                                                   xT_hi[w][s % 2][:, :, :].bitcast(F32), ALU.subtract)
                last.then_inc(low, 1)
                if not (isinstance(t, int) and t + K >= ET):
                    dve.wait_ge(got[0][s], i * 16 + 16)
                    dve.wait_ge(got[1][s], i * 16 + 16)
                    stage(t + K, s)
                if exists(back(i, s, 1)[0]):
                    finish(*back(i, s, 1))

            rounds(dve, ET, step)
            finish(ET // K - 1, K - 1)

        @block.sync
        def _(sp):
            for b, src in zip(bias, biases):
                sp.dma_start(b[:, :], src.rearrange("(a n) -> a n", a=1).to_broadcast([P, D])).then_inc(bias_in, 16)

            def step(i, s):
                t = i * K + s
                sp.wait_ge(v_out, t + 1)
                sp.dma_start(v_dram[bass.ds(t * P, P), :], v[s][:, :]).then_inc(stored[s], 16)

            rounds(sp, ET, step)
            for s in range(K):
                sp.wait_ge(stored[s], ET // K * 16)


def edge_softmax(nc, g):
    with ExitStack() as ctx:
        sb = lambda n, s, d=F32: ctx.enter_context(nc.sbuf_tensor(f"es_{n}", s, d))
        sem = lambda n: nc.alloc_semaphore(f"es_{n}")
        joined, gap = sb("joined", [HEADS, EPAD + 1]), sb("gap", [HEADS, EPAD + 1])
        upto, top = sb("upto", [HEADS, EPAD]), sb("top", [HEADS, EPAD])
        p, inverse = sb("p", [HEADS, EPAD]), sb("inverse", [P, ET, HEADS])
        psP, psS = (ctx.enter_context(nc.psum_tensor(f"es_{n}", [P, D // HEADS, HEADS], F32))[:, 0:ET, :] for n in ("psP", "psS"))
        chain, centred, expd, att_ready, turned = sem("chain"), sem("centred"), sem("expd"), sem("att_ready"), sem("turned")
        block = ctx.enter_context(nc.Block())
        backwards = lambda ap: ap[:, ::-1]

        @block.vector
        def _(dve):
            n_chain = [0]

            def link(ins):
                n_chain[0] += 1
                ins.then_inc(chain, 1)
                dve.wait_ge(chain, n_chain[0])

            nc.vector.memset(joined[:, 0:1], 0.0)
            nc.vector.memset(joined[:, EPAD:EPAD + 1], 0.0)
            link(nc.vector.tensor_tensor(joined[:, 1:EPAD], g.key_row[0:HEADS, 0, 1:EPAD],
                                         g.key_row[0:HEADS, 0, 0:EPAD - 1], ALU.is_equal))
            link(nc.vector.tensor_scalar(gap[:, :], joined[:, :], 1.0, BIG, ALU.subtract, ALU.mult))
            link(nc.vector.tensor_tensor_scan(upto[:, :], gap[:, 0:EPAD], g.logits_T[:, :], -BIG, ALU.add, ALU.max))
            link(nc.vector.tensor_tensor_scan(backwards(top), backwards(gap[:, 1:EPAD + 1]), backwards(upto),
                                              -BIG, ALU.add, ALU.max))
            nc.vector.tensor_tensor(p[:, :], g.logits_T[:, :], top[:, :], ALU.subtract).then_inc(centred, 1)
            dve.wait_ge(expd, 1)
            link(nc.vector.tensor_tensor_scan(upto[:, :], joined[:, 0:EPAD], p[:, :], 0.0, ALU.mult, ALU.add))
            nc.vector.tensor_tensor_scan(backwards(top), backwards(gap[:, 1:EPAD + 1]), backwards(upto),
                                         -BIG, ALU.add, ALU.max).then_inc(att_ready, 1)
            dve.wait_ge(turned, 1)
            link(nc.vector.reciprocal(inverse[:, :, :], psS[:, :, :]))
            nc.vector.tensor_tensor(g.att[:, :, :], psP[:, :, :], inverse[:, :, :], ALU.mult)

        @block.scalar
        def _(act):
            act.wait_ge(centred, 1)
            nc.scalar.activation(p[:, :], p[:, :], ACT.Exp).then_inc(expd, 1)

        @block.tensor
        def _(pe):
            pe.wait_ge(att_ready, 1)
            for t in range(ET):
                nc.tensor.transpose(psP[:, t, :], p[:, t * P:(t + 1) * P], g.ident[0:HEADS, 0:HEADS])
                last = nc.tensor.transpose(psS[:, t, :], top[:, t * P:(t + 1) * P], g.ident[0:HEADS, 0:HEADS])
            last.then_inc(turned, 1)


def edge_attend(nc, g, v_dram, wo, bo, out):
    with ExitStack() as ctx:
        sb = lambda n, s, d=F32: ctx.enter_context(nc.sbuf_tensor(f"ea_{n}", s, d))
        sem = lambda n: nc.alloc_semaphore(f"ea_{n}")
        split = split_weight(nc, ctx, "wo", wo, KC, D)
        load_split(nc, [split])
        _, _, wo_hi, wo_lo = split
        v, av = [sb(f"v{s}", [P, D]) for s in range(K)], [sb(f"av{s}", [P, D]) for s in range(K)]
        same, carry = [sb(f"same{s}", [P, P]) for s in range(K)], [sb(f"carry{s}", [P, P]) for s in range(K)]
        y_hi, y_lo = [sb(f"y_hi{s}", [P, KC, P], F32R) for s in range(2)], [sb(f"y_lo{s}", [P, KC, P], F32R) for s in range(2)]
        sums, biased = [sb(f"sums{s}", [P, D]) for s in range(K)], [sb(f"biased{s}", [P, D]) for s in range(K)]
        bias_row = sb("bias_row", [P, D])
        psY = [ctx.enter_context(nc.psum_tensor(f"ea_psY{s}", [P, KC, P], F32)) for s in range(2)]
        ps = [ctx.enter_context(nc.psum_tensor(f"ea_ps{s}", [P, D], F32)) for s in range(K)]
        loaded, stored = [sem(f"loaded{s}") for s in range(K)], [sem(f"stored{s}") for s in range(K)]
        weighed, masks_ready, y_done, high, low = sem("weighed"), sem("masks_ready"), sem("y_done"), sem("high"), sem("low")
        summed, emptied = sem("summed"), sem("emptied")
        bias_in, rows_stored, biased_ready = sem("bias_in"), sem("rows_stored"), sem("biased_ready")
        block = ctx.enter_context(nc.Block())

        @block.gpsimd
        def _(pool):
            pool.wait_ge(bias_in, 16)

            def step(i, s):
                pool.wait_ge(emptied, i * K + s + 1)
                if later(i):
                    pool.wait_ge(stored[s], i * 16)
                nc.gpsimd.tensor_tensor(biased[s][:, :], sums[s][:, :], bias_row[:, :], ALU.add).then_inc(biased_ready, 1)

            rounds(pool, ET, step)

        @block.sync
        def _(sp):
            sp.dma_start(bias_row[:, :], bo.rearrange("(a n) -> a n", a=1).to_broadcast([P, D])).then_inc(bias_in, 16)

            def load(i, s):
                if later(i):
                    sp.wait_ge(weighed, i * K + s - K + 1)
                sp.dma_start(v[s][:, :], v_dram[bass.ds((i * K + s) * P, P), :]).then_inc(loaded[s], 16)

            def store(i, s):
                sp.wait_ge(biased_ready, i * K + s + 1)
                sp.dma_start(out[bass.ds((i * K + s) * P, P), :], biased[s][:, :]).then_inc(stored[s], 16)

            for s in range(K - 1):
                load(0, s)
            sp.wait_ge(bias_in, 16)
            sp.dma_start(out[EPAD:TROWS, :], bias_row[:, :]).then_inc(rows_stored, 16)

            def step(i, s):
                t = i * K + s
                if not (isinstance(t, int) and t + K - 1 >= ET):
                    load(*((i, K - 1) if s == 0 else (i + 1, s - 1)))
                if exists(back(i, s, 2)[0]):
                    store(*back(i, s, 2))

            rounds(sp, ET, step)
            store(ET // K - 1, K - 2)
            store(ET // K - 1, K - 1)
            sp.wait_ge(rows_stored, 16)
            for s in range(K):
                sp.wait_ge(stored[s], ET // K * 16)

        @block.vector
        def _(dve):
            def lows(i, s):
                dve.wait_ge(high, i * K + s + 1)
                nc.vector.tensor_tensor(y_lo[s % 2][:, :, :], psY[s % 2][:, :, :], y_hi[s % 2][:, :, :].bitcast(F32),
                                        ALU.subtract).then_inc(low, 1)

            def step(i, s):
                t = i * K + s
                dve.wait_ge(loaded[s], i * 16 + 16)
                if later(i):
                    dve.wait_ge(summed, t - K + 1)
                nc.vector.tensor_tensor(av[s][:, :].rearrange("p (h d) -> p h d", h=HEADS),
                                        v[s][:, :].rearrange("p (h d) -> p h d", h=HEADS),
                                        g.att[:, bass.ds(t, 1), :].rearrange("p a b -> p (a b)").unsqueeze(2)
                                        .to_broadcast([P, HEADS, DK]), ALU.mult).then_inc(weighed, 1)
                nc.vector.tensor_scalar(same[s][:, :], g.key_row[:, 0, bass.ds(t * P, P)],
                                        g.rec[0][:, bass.ds(t, 1), 0], None, ALU.is_equal)
                nc.vector.tensor_scalar(carry[s][:, :], g.key_row[:, 0, bass.ds(t * P, P)],
                                        g.prev_last[:, 0, bass.ds(t, 1)], None, ALU.is_equal).then_inc(masks_ready, 1)
                if exists(back(i, s, 1)[0]):
                    lows(*back(i, s, 1))

            rounds(dve, ET, step)
            lows(ET // K - 1, K - 1)

        @block.scalar
        def _(act):
            def empty(i, s):
                act.wait_ge(summed, i * K + s + 1)
                if later(i):
                    act.wait_ge(biased_ready, i * K + s - K + 1)
                nc.scalar.activation(sums[s][:, :], ps[s][:, :], ACT.Copy).then_inc(emptied, 1)

            def step(i, s):
                t = i * K + s
                act.wait_ge(y_done, t + 1)
                if exists(back(i, s, 2)[0]):
                    act.wait_ge(summed, t - 1)
                nc.scalar.activation(y_hi[s % 2][:, :, :], psY[s % 2][:, :, :], ACT.Copy).then_inc(high, 1)
                if exists(back(i, s, 1)[0]):
                    empty(*back(i, s, 1))

            rounds(act, ET, step)
            empty(ET // K - 1, K - 1)

        @block.tensor
        def _(pe):
            def project(i, s):
                t, h = i * K + s, s % 2
                pe.wait_ge(low, t + 1)
                if later(i):
                    pe.wait_ge(emptied, t - K + 1)
                alone = isinstance(t, int) and t == 0
                n = 0
                for a, b in ((y_hi, wo_hi), (y_hi, wo_lo), (y_lo, wo_hi)):
                    for c in range(KC):
                        last = nc.tensor.matmul(ps[s][:, :], a[h][:, c, :], b[:, c, :], start=n == 0,
                                                stop=alone and n == 3 * KC - 1)
                        n += 1
                if not alone:
                    pe.wait_ge(emptied, t)
                    last = nc.tensor.matmul(ps[s][:, :], carry[s][:, :], sums[s - 1][:, :], start=False, stop=True)
                last.then_inc(summed, 1)

            def step(i, s):
                t, h = i * K + s, s % 2
                pe.wait_ge(masks_ready, t + 1)
                if exists(back(i, s, 2)[0]):
                    pe.wait_ge(low, t - 1)
                for c in range(KC):
                    last = nc.tensor.matmul(psY[h][:, c, :], av[s][:, c * P:(c + 1) * P], same[s][:, :],
                                            start=True, stop=True)
                last.then_inc(y_done, 1)
                if exists(back(i, s, 1)[0]):
                    project(*back(i, s, 1))

            rounds(pe, ET, step)
            project(ET // K - 1, K - 1)


G4 = 4
NG = -(-NT // G4)
S8, B4 = 8, 4


def bias_rows(src):
    return src.rearrange("(a n) -> a n", a=1).to_broadcast([P, D])


def tile_rows(t):
    return NLAST if isinstance(t, int) and t == NT - 1 else P


def node_mlp(nc, g, x, comp_a, comp_b, w1, b1, w2, b2, out):
    with ExitStack() as ctx:
        sb = lambda n, s, d=F32: ctx.enter_context(nc.sbuf_tensor(f"nm_{n}", s, d))
        sem = lambda n: nc.alloc_semaphore(f"nm_{n}")
        split = [split_weight(nc, ctx, n, w, KC, D) for n, w in (("w1", w1), ("w2", w2))]
        load_split(nc, split)
        (_, _, w1_hi, w1_lo), (_, _, w2_hi, w2_lo) = split
        xb, x1 = ([[sb(f"{n}_{h}{r}", [P, D]) for r in range(G4)] for h in range(2)] for n in ("x", "x1"))
        u, ypre, y = ([sb(f"{n}{r}", [P, D]) for r in range(G4)] for n in ("u", "ypre", "y"))
        uT_hi, uT_lo = ([sb(f"{n}{h}", [P, KC, D], F32R) for h in range(2)] for n in ("uT_hi", "uT_lo"))
        hT = [sb(f"hT{m}", [P, D]) for m in range(KC)]
        hT_hi, hT_lo = sb("hT_hi", [P, KC, D], F32R), sb("hT_lo", [P, KC, D], F32R)
        b1_col, b2_row = sb("b1_col", [P, KC]), sb("b2_row", [P, D])
        idx = sb("idx", [P, 2, 2, G4], I32)
        st, mv = [sb(f"st{w}", [P, G4, 6]) for w in range(2)], [sb(f"mv{w}", [P, G4, 2]) for w in range(2)]
        std, rstd, shift = ([sb(f"{n}{w}", [P, G4]) for w in range(2)] for n in ("std", "rstd", "shift"))
        psT = [ctx.enter_context(nc.psum_tensor(f"nm_psT{s}", [P, KC, P], F32)) for s in range(2)]
        ps1 = [ctx.enter_context(nc.psum_tensor(f"nm_ps1{s}", [P, D], F32)) for s in range(KC)]
        ps2 = [ctx.enter_context(nc.psum_tensor(f"nm_ps2{s}", [P, D], F32)) for s in range(2)]
        got_x, got_a, got_c = ([[sem(f"{n}{h}{r}") for r in range(G4)] for h in range(2)] for n in ("got_x", "got_a", "got_c"))
        stored = [sem(f"stored{r}") for r in range(G4)]
        a_ready, c_ready, held, bias_in = sem("a_ready"), sem("c_ready"), sem("held"), sem("bias_in")
        measured, var_ready, std_ready, inverted, coef_ready = (sem(n) for n in (
            "measured", "var_ready", "std_ready", "inverted", "coef_ready"))
        y_added, y_measured, y_var_ready, y_std_ready, y_inverted, y_coef_ready = (sem(n) for n in (
            "y_added", "y_measured", "y_var_ready", "y_std_ready", "y_inverted", "y_coef_ready"))
        x1_ready, u_ready, x1_biased, turned, high, low = (sem(n) for n in (
            "x1_ready", "u_ready", "x1_biased", "turned", "high", "low"))
        h_done, h_ready, h_high, h_low, y_done, y_ready = (sem(n) for n in (
            "h_done", "h_ready", "h_high", "h_low", "y_done", "y_ready"))
        block = ctx.enter_context(nc.Block())

        def tiles(q):
            return range(NT - (NG - 1) * G4 if isinstance(q, int) and q == NG - 1 else G4)

        def width(q):
            return len(tiles(q)) * P

        def past(q, n):
            return not isinstance(q, int) or q >= n

        def each(f):
            def stage(i, h):
                for r in tiles(i * 2 + h):
                    f(i, h, r)
            return stage

        def tile(r, f):
            return lambda i, h: f(i, h, r) if r in tiles(i * 2 + h) else None

        def chunk(m, f):
            return lambda i, h: f(i, h, m)

        @block.sync
        def _(sp):
            with nc.allow_non_contiguous_dma(reason="a bias onto the partitions, once"):
                sp.dma_start(b1_col[:, :], b1.rearrange("(m p) -> p m", p=P)).then_inc(bias_in, 16)
            sp.dma_start(b2_row[:, :], bias_rows(b2)).then_inc(bias_in, 16)

            def load(i, h, r):
                t = (i * 2 + h) * G4 + r
                if past(i * 2 + h, 2):
                    sp.wait_ge(x1_ready, t - 2 * G4 + 1)
                    sp.wait_ge(u_ready, t - 2 * G4 + 1)
                n = tile_rows(t)
                sp.dma_start(xb[h][r][0:n, :], x[bass.ds(t * P, n), :]).then_inc(got_x[h][r], 16)

            def store(i, h, r):
                t = (i * 2 + h) * G4 + r
                sp.wait_ge(y_ready, t + 1)
                n = tile_rows(t)
                sp.dma_start(out[bass.ds(t * P, n), :], y[r][0:n, :]).then_inc(stored[r], 16)

            skewed(sp, NG, [(-3, each(load)), (1, each(store))], 2, ahead=3)
            for r in range(G4):
                sp.wait_ge(stored[r], 16 * (NG if r in tiles(NG - 1) else NG - 1))

        @block.gpsimd
        def _(pool):
            last_sum = pool.to_reg(TROWS - 1)
            pool.wait_ge(bias_in, 32)

            def add_a(i, h, r):
                if r == 0:
                    pool.wait_ge(a_ready, i * 2 + h + 1)
                hold(pool, got_x[h][r], i * 16 + 16, held)
                nc.gpsimd.indirect_dma_start(xb[h][r][:, :], None, comp_a,
                                             bass.IndirectOffsetOnAxis(idx[:, 0, h, r:r + 1], 0),
                                             bounds_check=last_sum, compute_op=ALU.add).then_inc(got_a[h][r], 16)

            def add_bias(i, h, r):
                pool.wait_ge(x1_ready, (i * 2 + h) * G4 + r + 1)
                nc.gpsimd.tensor_tensor(x1[h][r][:, :], x1[h][r][:, :], b2_row[:, :], ALU.add).then_inc(x1_biased, 1)

            def add_c(i, h, r):
                if r == 0:
                    pool.wait_ge(c_ready, i * 2 + h + 1)
                hold(pool, u_ready, (i * 2 + h) * G4 + r + 1, held)
                nc.gpsimd.indirect_dma_start(u[r][:, :], None, comp_b,
                                             bass.IndirectOffsetOnAxis(idx[:, 1, h, r:r + 1], 0),
                                             bounds_check=last_sum, compute_op=ALU.add).then_inc(got_c[h][r], 16)

            skewed(pool, NG, [(-3, each(add_a)), (-1, each(add_bias)), (-2, each(add_c))], 2, ahead=3)

        @block.tensor
        def _(pe):
            def turn(i, h, r):
                t = (i * 2 + h) * G4 + r
                pe.wait_ge(got_c[h][r], i * 16 + 16)
                if not (isinstance(t, int) and t < 2):
                    pe.wait_ge(low, t - 1)
                for k in range(KC):
                    last = nc.tensor.transpose(psT[r % 2][:, k, :], u[r][:, k * P:(k + 1) * P], g.ident[:, :])
                last.then_inc(turned, 1)

            def up(i, h, m):
                q = i * 2 + h
                w = width(q)
                if m == 0:
                    pe.wait_ge(low, q * G4 + len(tiles(q)))
                if past(q, 1):
                    pe.wait_ge(h_low, q * KC + m - KC + 1)
                n = 0
                for wt, ut in ((w1_hi, uT_hi[h]), (w1_lo, uT_hi[h]), (w1_hi, uT_lo[h])):
                    for k in range(KC):
                        last = nc.tensor.matmul(ps1[m][:, 0:w], wt[:, k, m * P:(m + 1) * P], ut[:, k, 0:w],
                                                start=n == 0, stop=n == 3 * KC - 1)
                        n += 1
                last.then_inc(h_done, 1)

            def down(i, h, r):
                q = i * 2 + h
                t = q * G4 + r
                if not (isinstance(t, int) and t < 2):
                    pe.wait_ge(y_added, t - 1)
                n = 0
                for k in range(KC):
                    if r == 0:
                        pe.wait_ge(h_low, q * KC + k + 1)
                    for ht, wt in ((hT_hi, w2_hi), (hT_hi, w2_lo), (hT_lo, w2_hi)):
                        last = nc.tensor.matmul(ps2[r % 2][:, :], ht[:, k, r * P:(r + 1) * P], wt[:, k, :],
                                                start=n == 0, stop=n == 3 * KC - 1)
                        n += 1
                last.then_inc(y_done, 1)

            stages = [(0, chunk(0, up))]
            for m in range(1, KC):
                stages += [(0, chunk(m, up)), (-1, tile(m - 1, turn))]
            skewed(pe, NG, stages + [(-1, tile(G4 - 1, turn)), (0, each(down))], 2, ahead=1)

        @block.scalar
        def _(act):
            act.wait_ge(bias_in, 32)

            def hidden(i, h, m):
                q = i * 2 + h
                w = width(q)
                act.wait_ge(h_done, q * KC + m + 1)
                if past(q, 1):
                    act.wait_ge(h_low, q * KC + m - KC + 1)
                    act.wait_ge(y_done, q * G4)
                nc.scalar.activation(hT[m][:, 0:w], ps1[m][:, 0:w], ACT.Relu, bias=b1_col[:, m:m + 1])\
                  .then_inc(h_ready, 1)
                act.wait_ge(h_ready, q * KC + m + 1)
                nc.scalar.activation(hT_hi[:, m, 0:w], hT[m][:, 0:w], ACT.Copy).then_inc(h_high, 1)

            def highs(i, h, r):
                q = i * 2 + h
                act.wait_ge(turned, q * G4 + r + 1)
                if past(q, 2):
                    act.wait_ge(h_done, (q - 1) * KC)
                nc.scalar.activation(uT_hi[h][:, :, r * P:(r + 1) * P], psT[r % 2][:, :, :], ACT.Copy).then_inc(high, 1)

            def y_root(i, h, r):
                act.wait_ge(y_var_ready, (i * 2 + h) * G4 + r + 1)
                nc.scalar.activation(std[1][:, r:r + 1], mv[1][:, r, 1:2], ACT.Sqrt, bias=g.eps_col[:, :])\
                  .then_inc(y_std_ready, 1)

            def root(i, h, r):
                act.wait_ge(var_ready, (i * 2 + h) * G4 + r + 1)
                nc.scalar.activation(std[0][:, r:r + 1], mv[0][:, r, 1:2], ACT.Sqrt, bias=g.eps_col[:, :])\
                  .then_inc(std_ready, 1)

            def apply(i, h, r):
                q = i * 2 + h
                t = q * G4 + r
                act.wait_ge(coef_ready, t + 1)
                if past(q, 2):
                    act.wait_ge(y_added, t - 2 * G4 + 1)
                nc.scalar.activation(x1[h][r][:, :], xb[h][r][:, :], ACT.Identity, bias=shift[0][:, r:r + 1],
                                     scale=rstd[0][:, r:r + 1]).then_inc(x1_ready, 1)

            def y_apply(i, h, r):
                q = i * 2 + h
                act.wait_ge(y_coef_ready, q * G4 + r + 1)
                if past(q, 1):
                    act.wait_ge(stored[r], q * 16)
                nc.scalar.activation(y[r][:, :], ypre[r][:, :], ACT.Identity, bias=shift[1][:, r:r + 1],
                                     scale=rstd[1][:, r:r + 1]).then_inc(y_ready, 1)

            stages = [(0, chunk(0, hidden)), (1, tile(G4 - 1, y_apply)), (-1, tile(G4 - 1, apply))]
            for m in range(1, KC):
                stages += [(0, chunk(m, hidden)), (-2, tile(m - 1, root)), (-1, tile(m - 1, highs))]
            stages += [(-1, tile(G4 - 1, highs)), (-2, tile(G4 - 1, root))]
            for r in range(G4):
                stages += [(0, tile(r, y_root))]
                if r > 0:
                    stages += [(-2, tile(r - 1, apply)), (0, tile(r - 1, y_apply))]
            skewed(act, NG, stages, 2, ahead=2)

        @block.vector
        def _(dve):
            def stage(k, ready):
                def stage_group(i, h):
                    n = len(tiles(i * 2 + h))
                    nc.vector.tensor_scalar(idx[:, k, h, 0:n], g.node_row[:, 1, bass.ds((i * 2 + h) * G4, n)], 0.0,
                                            None, ALU.add).then_inc(ready, 1)
                return stage_group

            def measure(i, h, r):
                t = (i * 2 + h) * G4 + r
                dve.wait_ge(got_a[h][r], i * 16 + 16)
                nc.vector.bn_stats(st[0][:, r, :], xb[h][r][:, :]).then_inc(measured, 1)
                hold(dve, measured, t + 1, held)
                nc.vector.bn_aggr(mv[0][:, r, :], st[0][:, r, :]).then_inc(var_ready, 1)

            def coefs(w, std_sem, inv_sem, coef_sem):
                def tile_coefs(i, h, r):
                    t = (i * 2 + h) * G4 + r
                    dve.wait_ge(std_sem, t + 1)
                    nc.vector.reciprocal(rstd[w][:, r:r + 1], std[w][:, r:r + 1]).then_inc(inv_sem, 1)
                    dve.wait_ge(inv_sem, t + 1)
                    nc.vector.tensor_scalar(shift[w][:, r:r + 1], mv[w][:, r, 0:1], rstd[w][:, r:r + 1], -1.0,
                                            ALU.mult, ALU.mult).then_inc(coef_sem, 1)
                return tile_coefs

            def lows(i, h, r):
                dve.wait_ge(high, (i * 2 + h) * G4 + r + 1)
                nc.vector.tensor_tensor(uT_lo[h][:, :, r * P:(r + 1) * P], psT[r % 2][:, :, :],
                                        uT_hi[h][:, :, r * P:(r + 1) * P].bitcast(F32), ALU.subtract).then_inc(low, 1)

            def hidden(i, h, m):
                q = i * 2 + h
                w = width(q)
                dve.wait_ge(h_high, q * KC + m + 1)
                nc.vector.tensor_tensor(hT_lo[:, m, 0:w], hT[m][:, 0:w], hT_hi[:, m, 0:w].bitcast(F32),
                                        ALU.subtract).then_inc(h_low, 1)

            def finish(i, h, r):
                q = i * 2 + h
                t = q * G4 + r
                dve.wait_ge(y_done, t + 1)
                dve.wait_ge(x1_biased, t + 1)
                if past(q, 1):
                    dve.wait_ge(y_ready, t - G4 + 1)
                nc.vector.tensor_tensor(ypre[r][:, :], ps2[r % 2][:, :], x1[h][r][:, :], ALU.add).then_inc(y_added, 1)
                dve.wait_ge(y_added, t + 1)
                nc.vector.bn_stats(st[1][:, r, :], ypre[r][:, :]).then_inc(y_measured, 1)
                hold(dve, y_measured, t + 1, held)
                nc.vector.bn_aggr(mv[1][:, r, :], st[1][:, r, :]).then_inc(y_var_ready, 1)

            def copy_u(i, h, r):
                q = i * 2 + h
                dve.wait_ge(coef_ready, q * G4 + r + 1)
                if past(q, 1):
                    dve.wait_ge(turned, q * G4 + r - G4 + 1)
                nc.vector.tensor_scalar(u[r][:, :], xb[h][r][:, :], rstd[0][:, r:r + 1], shift[0][:, r:r + 1],
                                        ALU.mult, ALU.add).then_inc(u_ready, 1)

            x_coefs = coefs(0, std_ready, inverted, coef_ready)
            y_coefs = coefs(1, y_std_ready, y_inverted, y_coef_ready)
            stages = [(-3, stage(0, a_ready)), (-2, stage(1, c_ready))]
            for m in range(KC):
                stages += [(0, chunk(m, hidden)), (-2, tile(m, measure))]
                if m > 0:
                    stages += [(-1, tile(m - 1, lows)), (-2, tile(m - 1, x_coefs))]
            stages += [(-1, tile(G4 - 1, lows)), (-2, tile(G4 - 1, x_coefs))]
            for r in range(G4):
                stages += [(0, tile(r, finish)), (-2, tile(r, copy_u))]
                if r > 0:
                    stages += [(0, tile(r - 1, y_coefs))]
            stages += [(0, tile(G4 - 1, y_coefs))]
            skewed(dve, NG, stages, 2, ahead=3)


def node_conv1(nc, g, x2, comp_a, comp_b, w, b, x3_out, g_out):
    S, B = S8, B4
    with ExitStack() as ctx:
        sb = lambda n, s, d=F32: ctx.enter_context(nc.sbuf_tensor(f"n3_{n}", s, d))
        sem = lambda n: nc.alloc_semaphore(f"n3_{n}")
        split = split_weight(nc, ctx, "conv1_w", w, KC, D)
        load_split(nc, [split])
        _, _, w_hi, w_lo = split
        xb, x3, v, z, gz = ([sb(f"{n}{s}", [P, D]) for s in range(S)] for n in ("x", "x3", "v", "z", "gz"))
        vT_hi, vT_lo = ([sb(f"{n}{s}", [P, KC, P], F32R) for s in range(2)] for n in ("vT_hi", "vT_lo"))
        b_row = sb("b_row", [P, D])
        idx = sb("idx", [P, 2, S], I32)
        stats, mv = sb("stats", [P, S, 6]), sb("mv", [P, S, 2])
        std, rstd, shift = sb("std", [P, S]), sb("rstd", [P, S]), sb("shift", [P, S])
        psT = [ctx.enter_context(nc.psum_tensor(f"n3_psT{s}", [P, KC, P], F32)) for s in range(B)]
        ps = [ctx.enter_context(nc.psum_tensor(f"n3_ps{s}", [P, D], F32)) for s in range(B)]
        got_x, got_a, got_c, x3_stored, g_stored = ([sem(f"{n}{s}") for s in range(S)] for n in
                                                    ("got_x", "got_a", "got_c", "x3_stored", "g_stored"))
        a_ready, c_ready, held, bias_in = (sem(n) for n in ("a_ready", "c_ready", "held", "bias_in"))
        measured, var_ready, std_ready, inverted, coef_ready, x3_ready = (sem(n) for n in (
            "measured", "var_ready", "std_ready", "inverted", "coef_ready", "x3_ready"))
        v_ready, turned, high, low, z_done, z_ready, g_ready, act_held = (sem(n) for n in (
            "v_ready", "turned", "high", "low", "z_done", "z_ready", "g_ready", "act_held"))
        block = ctx.enter_context(nc.Block())

        @block.sync
        def _(sp):
            sp.dma_start(b_row[:, :], bias_rows(b)).then_inc(bias_in, 16)

            def load(i, s):
                t = i * S + s
                if later(i):
                    sp.wait_ge(x3_ready, t - S + 1)
                n = tile_rows(t)
                sp.dma_start(xb[s][0:n, :], x2[bass.ds(t * P, n), :]).then_inc(got_x[s], 16)

            def store_x3(i, s):
                t = i * S + s
                n = tile_rows(t)
                sp.wait_ge(x3_ready, t + 1)
                sp.dma_start(x3_out[bass.ds(t * P, n), :], x3[s][0:n, :]).then_inc(x3_stored[s], 16)

            def store_g(i, s):
                t = i * S + s
                n = tile_rows(t)
                sp.wait_ge(g_ready, t + 1)
                sp.dma_start(g_out[bass.ds(t * P, n), :], gz[s][0:n, :]).then_inc(g_stored[s], 16)

            skewed(sp, NT, [(-2, load), (5, store_x3), (11, store_g)], S, ahead=2, peel=3)
            for s in range(S):
                sp.wait_ge(x3_stored[s], 16 * len(range(s, NT, S)))
                sp.wait_ge(g_stored[s], 16 * len(range(s, NT, S)))

        @block.gpsimd
        def _(pool):
            last_sum = pool.to_reg(TROWS - 1)

            def add_a(i, s):
                pool.wait_ge(a_ready, i * S + s + 1)
                hold(pool, got_x[s], i * 16 + 16, held)
                nc.gpsimd.indirect_dma_start(xb[s][:, :], None, comp_a, bass.IndirectOffsetOnAxis(idx[:, 0, s:s + 1], 0),
                                             bounds_check=last_sum, compute_op=ALU.add).then_inc(got_a[s], 16)

            def add_c(i, s):
                pool.wait_ge(c_ready, i * S + s + 1)
                hold(pool, v_ready, i * S + s + 1, held)
                nc.gpsimd.indirect_dma_start(v[s][:, :], None, comp_b, bass.IndirectOffsetOnAxis(idx[:, 1, s:s + 1], 0),
                                             bounds_check=last_sum, compute_op=ALU.add).then_inc(got_c[s], 16)

            skewed(pool, NT, [(0, add_a), (5, add_c)], S, peel=3)

        @block.tensor
        def _(pe):
            def turn(i, s):
                t = i * S + s
                pe.wait_ge(got_c[s], i * 16 + 16)
                if not (isinstance(t, int) and t < B):
                    pe.wait_ge(low, t - B + 1)
                for k in range(KC):
                    last = nc.tensor.transpose(psT[s % B][:, k, :], v[s][:, k * P:(k + 1) * P], g.ident[:, :])
                last.then_inc(turned, 1)

            def project(i, s):
                t, h = i * S + s, s % 2
                pe.wait_ge(low, t + 1)
                if not (isinstance(t, int) and t < B):
                    pe.wait_ge(z_ready, t - B + 1)
                n = 0
                for vt, wt in ((vT_hi, w_hi), (vT_hi, w_lo), (vT_lo, w_hi)):
                    for k in range(KC):
                        last = nc.tensor.matmul(ps[s % B][:, :], vt[h][:, k, :], wt[:, k, :], start=n == 0,
                                                stop=n == 3 * KC - 1)
                        n += 1
                last.then_inc(z_done, 1)

            skewed(pe, NT, [(7, turn), (8, project)], S, peel=3)

        @block.scalar
        def _(act):
            def root(i, s):
                act.wait_ge(var_ready, i * S + s + 1)
                nc.scalar.activation(std[:, s:s + 1], mv[:, s, 1:2], ACT.Sqrt, bias=g.eps_col[:, :]).then_inc(std_ready, 1)

            def apply(i, s):
                t = i * S + s
                act.wait_ge(coef_ready, t + 1)
                if later(i):
                    act.wait_ge(x3_stored[s], i * 16)
                    act.wait_ge(v_ready, t - S + 1)
                nc.scalar.activation(x3[s][:, :], xb[s][:, :], ACT.Identity, bias=shift[:, s:s + 1],
                                     scale=rstd[:, s:s + 1]).then_inc(x3_ready, 1)
                act.wait_ge(x3_ready, t + 1)
                if later(i):
                    act.wait_ge(turned, t - S + 1)
                nc.scalar.activation(v[s][:, :], x3[s][:, :], ACT.Copy, scale=g.dis[:, bass.ds(t, 1)]).then_inc(v_ready, 1)

            def highs(i, s):
                t = i * S + s
                act.wait_ge(turned, t + 1)
                if not (isinstance(t, int) and t < 2):
                    act.wait_ge(z_done, t - 1)
                nc.scalar.activation(vT_hi[s % 2][:, :, :], psT[s % B][:, :, :], ACT.Copy).then_inc(high, 1)

            def relu(i, s):
                t = i * S + s
                act.wait_ge(z_ready, t + 1)
                if later(i):
                    hold(act, g_stored[s], i * 16, act_held)
                nc.scalar.activation(gz[s][:, :], z[s][:, :], ACT.Relu, scale=g.dis[:, bass.ds(t, 1)]).then_inc(g_ready, 1)

            skewed(act, NT, [(7, highs), (10, relu), (4, apply), (2, root)], S, peel=3)

        @block.vector
        def _(dve):
            def stage_a(i, s):
                nc.vector.tensor_scalar(idx[:, 0, s:s + 1], g.node_row[:, 0, bass.ds(i * S + s, 1)], 0.0, None, ALU.add)\
                  .then_inc(a_ready, 1)

            def stage_c(i, s):
                nc.vector.tensor_scalar(idx[:, 1, s:s + 1], g.node_row[:, 1, bass.ds(i * S + s, 1)], 0.0, None, ALU.add)\
                  .then_inc(c_ready, 1)

            def measure(i, s):
                dve.wait_ge(got_a[s], i * 16 + 16)
                nc.vector.bn_stats(stats[:, s, :], xb[s][:, :]).then_inc(measured, 1)

            def aggregate(i, s):
                hold(dve, measured, i * S + s + 1, held)
                nc.vector.bn_aggr(mv[:, s, :], stats[:, s, :]).then_inc(var_ready, 1)

            def coefs(i, s):
                t = i * S + s
                dve.wait_ge(std_ready, t + 1)
                nc.vector.reciprocal(rstd[:, s:s + 1], std[:, s:s + 1]).then_inc(inverted, 1)
                dve.wait_ge(inverted, t + 1)
                nc.vector.tensor_scalar(shift[:, s:s + 1], mv[:, s, 0:1], rstd[:, s:s + 1], -1.0,
                                        ALU.mult, ALU.mult).then_inc(coef_ready, 1)

            def lows(i, s):
                dve.wait_ge(high, i * S + s + 1)
                nc.vector.tensor_tensor(vT_lo[s % 2][:, :, :], psT[s % B][:, :, :], vT_hi[s % 2][:, :, :].bitcast(F32),
                                        ALU.subtract).then_inc(low, 1)

            def out(i, s):
                t = i * S + s
                dve.wait_ge(z_done, t + 1)
                if later(i):
                    dve.wait_ge(g_ready, t - S + 1)
                nc.vector.scalar_tensor_tensor(z[s][:, :], ps[s % B][:, :], g.dis[:, bass.ds(t, 1)], b_row[:, :],
                                               ALU.mult, ALU.add).then_inc(z_ready, 1)

            dve.wait_ge(bias_in, 16)
            skewed(dve, NT, [(-1, stage_a), (7, lows), (9, out), (3, coefs), (1, measure), (4, stage_c), (1, aggregate)],
                   S, ahead=1, peel=3)


def node_conv2(nc, g, x3_in, g_in, comp, w, b, out):
    S, B = S8, B4
    with ExitStack() as ctx:
        sb = lambda n, s, d=F32: ctx.enter_context(nc.sbuf_tensor(f"n4_{n}", s, d))
        sem = lambda n: nc.alloc_semaphore(f"n4_{n}")
        split = split_weight(nc, ctx, "conv2_w", w, KC, D)
        load_split(nc, [split])
        _, _, w_hi, w_lo = split
        x3, v, pre, y = ([sb(f"{n}{s}", [P, D]) for s in range(S)] for n in ("x3", "v", "pre", "y"))
        vT_hi, vT_lo = ([sb(f"{n}{s}", [P, KC, P], F32R) for s in range(2)] for n in ("vT_hi", "vT_lo"))
        b_row = sb("b_row", [P, D])
        idx = sb("idx", [P, S], I32)
        stats, mv = sb("stats", [P, S, 6]), sb("mv", [P, S, 2])
        std, rstd, shift = sb("std", [P, S]), sb("rstd", [P, S]), sb("shift", [P, S])
        psT = [ctx.enter_context(nc.psum_tensor(f"n4_psT{s}", [P, KC, P], F32)) for s in range(B)]
        ps = [ctx.enter_context(nc.psum_tensor(f"n4_ps{s}", [P, D], F32)) for s in range(B)]
        got_x, got_g, got_c, stored = ([sem(f"{n}{s}") for s in range(S)] for n in ("got_x", "got_g", "got_c", "stored"))
        c_ready, held, bias_in, x3_biased = (sem(n) for n in ("c_ready", "held", "bias_in", "x3_biased"))
        turned, high, low, z_done = (sem(n) for n in ("turned", "high", "low", "z_done"))
        added, measured, var_ready, std_ready, inverted, coef_ready, y_ready = (sem(n) for n in (
            "added", "measured", "var_ready", "std_ready", "inverted", "coef_ready", "y_ready"))
        block = ctx.enter_context(nc.Block())

        @block.sync
        def _(sp):
            sp.dma_start(b_row[:, :], bias_rows(b)).then_inc(bias_in, 16)

            def load_g(i, s):
                t = i * S + s
                n = tile_rows(t)
                if later(i):
                    sp.wait_ge(turned, t - S + 1)
                sp.dma_start(v[s][0:n, :], g_in[bass.ds(t * P, n), :]).then_inc(got_g[s], 16)

            def load_x3(i, s):
                t = i * S + s
                n = tile_rows(t)
                if later(i):
                    sp.wait_ge(added, t - S + 1)
                sp.dma_start(x3[s][0:n, :], x3_in[bass.ds(t * P, n), :]).then_inc(got_x[s], 16)

            def store(i, s):
                t = i * S + s
                n = tile_rows(t)
                sp.wait_ge(y_ready, t + 1)
                sp.dma_start(out[bass.ds(t * P, n), :], y[s][0:n, :]).then_inc(stored[s], 16)

            skewed(sp, NT, [(-3, load_g), (-1, load_x3), (7, store)], S, ahead=3)
            for s in range(S):
                sp.wait_ge(stored[s], 16 * len(range(s, NT, S)))

        @block.gpsimd
        def _(pool):
            last_sum = pool.to_reg(TROWS - 1)
            pool.wait_ge(bias_in, 16)

            def add_sums(i, s):
                pool.wait_ge(c_ready, i * S + s + 1)
                hold(pool, got_g[s], i * 16 + 16, held)
                nc.gpsimd.indirect_dma_start(v[s][:, :], None, comp, bass.IndirectOffsetOnAxis(idx[:, s:s + 1], 0),
                                             bounds_check=last_sum, compute_op=ALU.add).then_inc(got_c[s], 16)

            def add_bias(i, s):
                pool.wait_ge(got_x[s], i * 16 + 16)
                nc.gpsimd.tensor_tensor(x3[s][:, :], x3[s][:, :], b_row[:, :], ALU.add).then_inc(x3_biased, 1)

            skewed(pool, NT, [(-1, add_sums), (1, add_bias)], S, ahead=1)

        @block.tensor
        def _(pe):
            def turn(i, s):
                t = i * S + s
                pe.wait_ge(got_c[s], i * 16 + 16)
                if not (isinstance(t, int) and t < B):
                    pe.wait_ge(low, t - B + 1)
                for k in range(KC):
                    last = nc.tensor.transpose(psT[s % B][:, k, :], v[s][:, k * P:(k + 1) * P], g.ident[:, :])
                last.then_inc(turned, 1)

            def project(i, s):
                t, h = i * S + s, s % 2
                pe.wait_ge(low, t + 1)
                if not (isinstance(t, int) and t < B):
                    pe.wait_ge(added, t - B + 1)
                n = 0
                for vt, wt in ((vT_hi, w_hi), (vT_hi, w_lo), (vT_lo, w_hi)):
                    for k in range(KC):
                        last = nc.tensor.matmul(ps[s % B][:, :], vt[h][:, k, :], wt[:, k, :], start=n == 0,
                                                stop=n == 3 * KC - 1)
                        n += 1
                last.then_inc(z_done, 1)

            skewed(pe, NT, [(1, turn), (2, project)], S)

        @block.scalar
        def _(act):
            def highs(i, s):
                t = i * S + s
                act.wait_ge(turned, t + 1)
                if not (isinstance(t, int) and t < 2):
                    act.wait_ge(z_done, t - 1)
                nc.scalar.activation(vT_hi[s % 2][:, :, :], psT[s % B][:, :, :], ACT.Copy).then_inc(high, 1)

            def root(i, s):
                act.wait_ge(var_ready, i * S + s + 1)
                nc.scalar.activation(std[:, s:s + 1], mv[:, s, 1:2], ACT.Sqrt, bias=g.eps_col[:, :]).then_inc(std_ready, 1)

            def apply(i, s):
                act.wait_ge(coef_ready, i * S + s + 1)
                if later(i):
                    act.wait_ge(stored[s], i * 16)
                nc.scalar.activation(y[s][:, :], pre[s][:, :], ACT.Identity, bias=shift[:, s:s + 1],
                                     scale=rstd[:, s:s + 1]).then_inc(y_ready, 1)

            skewed(act, NT, [(1, highs), (6, apply), (4, root)], S)

        @block.vector
        def _(dve):
            def stage(i, s):
                if later(i):
                    dve.wait_ge(got_c[s], i * 16)
                nc.vector.tensor_scalar(idx[:, s:s + 1], g.node_row[:, 1, bass.ds(i * S + s, 1)], 0.0, None, ALU.add)\
                  .then_inc(c_ready, 1)

            def coefs(i, s):
                t = i * S + s
                dve.wait_ge(std_ready, t + 1)
                nc.vector.reciprocal(rstd[:, s:s + 1], std[:, s:s + 1]).then_inc(inverted, 1)
                dve.wait_ge(inverted, t + 1)
                nc.vector.tensor_scalar(shift[:, s:s + 1], mv[:, s, 0:1], rstd[:, s:s + 1], -1.0,
                                        ALU.mult, ALU.mult).then_inc(coef_ready, 1)

            def lows(i, s):
                dve.wait_ge(high, i * S + s + 1)
                nc.vector.tensor_tensor(vT_lo[s % 2][:, :, :], psT[s % B][:, :, :], vT_hi[s % 2][:, :, :].bitcast(F32),
                                        ALU.subtract).then_inc(low, 1)

            def out_pre(i, s):
                t = i * S + s
                dve.wait_ge(z_done, t + 1)
                dve.wait_ge(x3_biased, t + 1)
                if later(i):
                    dve.wait_ge(y_ready, t - S + 1)
                nc.vector.scalar_tensor_tensor(pre[s][:, :], ps[s % B][:, :], g.dis[:, bass.ds(t, 1)], x3[s][:, :],
                                               ALU.mult, ALU.add).then_inc(added, 1)
                dve.wait_ge(added, t + 1)
                nc.vector.bn_stats(stats[:, s, :], pre[s][:, :]).then_inc(measured, 1)
                hold(dve, measured, t + 1, held)
                nc.vector.bn_aggr(mv[:, s, :], stats[:, s, :]).then_inc(var_ready, 1)

            skewed(dve, NT, [(-3, stage), (1, lows), (3, out_pre), (5, coefs)], S, ahead=3)


MUL = 128
HID = 64
RB = 8
SILU_2MOM = 1.679177
AVG_NEIGHBORS = 10.0
RW = 256
RN = EPAD // RW


def radial(nc, g, w1, w2, w3):
    S = 8
    G = 4
    NK = ET // G
    with ExitStack() as ctx:
        sb = lambda n, s, d=F32: ctx.enter_context(nc.sbuf_tensor(f"ra_{n}", s, d))
        sem = lambda n: nc.alloc_semaphore(f"ra_{n}")
        wt = [sb("w1", [RB, HID]), sb("w2", [HID, HID]), sb("w3", [HID, HID])]
        attr = [sb(f"attr{h}", [P, RW // P, RB]) for h in range(2)]
        attr_T = [sb(f"attr_T{h}", [RB, RW]) for h in range(2)]
        hid = [[sb(f"hid{k}{h}", [HID, RW]) for h in range(2)] for k in range(2)]
        key_diag = [sb(f"key_diag{s}", [P, G, P]) for s in range(2)]
        rec_out, pos_out = sb("rec_out", [P, S, REC]), sb("pos_out", [P, S], I32)
        tab_slot, tab_idx = sb("tab_slot", [P, S, 4]), sb("tab_idx", [P, S], I32)
        bank = [ctx.enter_context(nc.psum_tensor(f"ra_bank{h}", [P, G * P], F32)) for h in range(2)]
        psA = [b[0:RB, 0:RW] for b in bank]
        psH = [[ctx.enter_context(nc.psum_tensor(f"ra_ps{k}{h}", [HID, RW], F32)) for h in range(2)] for k in range(3)]
        w_in, staged, turned, attr_ready = sem("w_in"), sem("staged"), sem("turned"), sem("attr_ready")
        held, act_held, pool_held = sem("held"), sem("act_held"), sem("pool_held")
        done, ready = [sem(f"done{k}") for k in range(3)], [sem(f"ready{k}") for k in range(3)]
        diag_ready, row_ready, row_copied = sem("diag_ready"), sem("row_ready"), sem("row_copied")
        rec_staged, tab_staged, tab_kept = sem("rec_staged"), sem("tab_staged"), sem("tab_kept")
        reloaded, ids_ready = sem("reloaded"), sem("ids_ready")
        scattered, tab_got = [sem(f"scattered{s}") for s in range(S)], [sem(f"tab_got{s}") for s in range(S)]
        block = ctx.enter_context(nc.Block())

        @block.sync
        def _(sp):
            for t, src in zip(wt, (w1, w2, w3)):
                sp.dma_start(t[:, :], src).then_inc(w_in, 16)
            for s in range(S):
                sp.wait_ge(scattered[s], ET // S * 16)
            sp.dma_start(g.rec[0][:, :, :], g.rec_dram[0].rearrange("(t p) c -> p t c", p=P)).then_inc(reloaded, 16)

        @block.gpsimd
        def _(pool):
            g.last_edge, last_node = pool.to_reg(EPAD - 1), pool.to_reg(NT * P - 1)

            def scatter(i, s):
                hold(pool, rec_staged, i * S + s + 1, pool_held)
                scatter_tile(nc, g, 0, rec_out, pos_out, s, scattered[s])

            skewed(pool, ET, [(0, scatter)], S)

            def look_up(i, s):
                hold(pool, tab_staged, i * S + s + 1, pool_held)
                nc.gpsimd.indirect_dma_start(
                    tab_slot[:, s, :], None, g.ntab_dram, bass.IndirectOffsetOnAxis(tab_idx[:, s:s + 1], 0),
                    bounds_check=last_node, oob_is_err=False).then_inc(tab_got[s], 16)

            skewed(pool, ET, [(0, look_up)], S)

        @block.vector
        def _(dve):
            def stage(i, s):
                if later(i):
                    dve.wait_ge(scattered[s], i * 16)
                stage_tile(nc, g, 0, rec_out, pos_out, i * S + s, s, rec_staged)

            skewed(dve, ET, [(0, stage)], S)

            def stage_look_up(i, s):
                nc.vector.tensor_scalar(tab_idx[:, s:s + 1], g.src_any[:, 1, bass.ds(i * S + s, 1)],
                                        0.0, None, ALU.add).then_inc(tab_staged, 1)

            def keep(i, s):
                dve.wait_ge(tab_got[s], i * 16 + 16)
                nc.vector.tensor_scalar(g.src_tab[:, bass.ds(i * S + s, 1), :].rearrange("p a b -> p (a b)"),
                                        tab_slot[:, s, :], 0.0, None, ALU.add).then_inc(tab_kept, 1)

            skewed(dve, ET, [(7, keep), (0, stage_look_up)], S)
            dve.wait_ge(tab_kept, ET)
            nc.vector.tensor_copy(g.src_comp[:, :, :], g.src_tab[:, :, 0:2].rearrange("p t o -> p o t"))
            dve.wait_ge(reloaded, 16)
            sorted_ids(nc, g, 0, dve, ids_ready)

        @block.tensor
        def _(pe):
            pe.wait_ge(w_in, 48)

            def layer(k):
                def run(i, s):
                    t, h = i * K + s, s % 2
                    if not (isinstance(t, int) and t < 2):
                        pe.wait_ge(ready[k], t - 1)
                    hold(pe, attr_ready if k == 0 else ready[k - 1], t + 1, held)
                    src = attr_T[h] if k == 0 else hid[k - 1][h]
                    nc.tensor.matmul(psH[k][h][:, :], wt[k][:, :], src[:, :], start=True, stop=True).then_inc(done[k], 1)
                return run

            def turn(i, s):
                t, h = i * K + s, s % 2
                pe.wait_ge(staged, t + 1)
                if not (isinstance(t, int) and t < 2):
                    pe.wait_ge(attr_ready, t - 1)
                for j in range(RW // P):
                    m = nc.tensor.transpose(psA[h][:, j * P:(j + 1) * P], attr[h][:, j, :], g.ident[:, :])
                m.then_inc(turned, 1)

            skewed(pe, RN, [(0, turn), (1, layer(0)), (2, layer(1)), (3, layer(2))], K)
            pe.wait_ge(attr_ready, RN)
            for n in range(2):
                def spread(i, s, n=n):
                    u = i * 2 + s + n * NK
                    pe.wait_ge(diag_ready, u + 1)
                    if not (isinstance(u, int) and u < 2):
                        pe.wait_ge(row_copied, u - 1)
                    nc.tensor.matmul(bank[s][:, :], g.ones[:, :], key_diag[s][:, :, :].rearrange("p g e -> p (g e)"),
                                     start=True, stop=True).then_inc(row_ready, 1)

                skewed(pe, NK, [(0, spread)], 2, peel=1)

        @block.scalar
        def _(act):
            def stage(i, s):
                t, h = i * K + s, s % 2
                if not (isinstance(t, int) and t < 2):
                    hold(act, turned, t - 1, act_held)
                nc.scalar.activation(attr[h][:, :, :], g.rec[1][:, bass.ds(t * (RW // P), RW // P), 6:14], ACT.Copy)\
                   .then_inc(staged, 1)

            def copy_attr(i, s):
                t, h = i * K + s, s % 2
                act.wait_ge(turned, t + 1)
                if not (isinstance(t, int) and t < 2):
                    act.wait_ge(done[0], t - 1)
                nc.scalar.activation(attr_T[h][:, :], psA[h][:, :], ACT.Copy).then_inc(attr_ready, 1)

            def layer(k):
                def run(i, s):
                    t, h = i * K + s, s % 2
                    act.wait_ge(done[k], t + 1)
                    if k < 2 and not (isinstance(t, int) and t < 2):
                        act.wait_ge(done[k + 1], t - 1)
                    out = hid[k][h][:, :] if k < 2 else g.hid3[:, bass.ds(t * RW, RW)]
                    scale = RB ** -0.5 if k == 0 else SILU_2MOM * HID ** -0.5
                    nc.scalar.activation(out, psH[k][h][:, :], ACT.Silu, scale=scale).then_inc(ready[k], 1)
                return run

            skewed(act, RN, [(-1, stage), (0, copy_attr), (1, layer(0)), (2, layer(1)), (3, layer(2))], K, ahead=1)
            for n, o in enumerate((1, 0)):
                def diagonals(i, s, n=n, o=o):
                    t = i * 2 + s
                    u = t + n * NK
                    if not (isinstance(u, int) and u < 2):
                        hold(act, row_ready, u - 1, act_held)
                    for j in range(G):
                        last = nc.scalar.activation(key_diag[s][:, j, :], g.ident[:, :], ACT.Copy,
                                                    scale=g.rec[o][:, bass.ds(t * G + j, 1), o])
                    last.then_inc(diag_ready, 1)

                def keep(i, s, n=n, o=o):
                    t = i * 2 + s
                    hold(act, row_ready, t + n * NK + 1, act_held)
                    nc.scalar.activation(g.key_row[:, o, bass.ds(t * G * P, G * P)], bank[s][:, :], ACT.Copy)\
                       .then_inc(row_copied, 1)

                if o == 0:
                    act.wait_ge(reloaded, 16)
                skewed(act, NK, [(0, diagonals), (1, keep)], 2, peel=1)


def edge_messages(nc, g, x, w_up0, w_up1, w_mlp4, w_out0, w_out1, out):
    NM = 2 * 4
    SCALE = MUL ** -0.5 * SILU_2MOM * HID ** -0.5 * (2 * MUL) ** -0.5 / AVG_NEIGHBORS
    with ExitStack() as ctx:
        sb = lambda n, s, d=F32: ctx.enter_context(nc.sbuf_tensor(f"em_{n}", s, d))
        sem = lambda n: nc.alloc_semaphore(f"em_{n}")
        split = [split_weight(nc, ctx, n, w, k, MUL) for n, w, k in
                 (("up0", w_up0, 1), ("up1", w_up1, 1), ("out0", w_out0, 2), ("out1", w_out1, 2))]
        load_split(nc, split)
        up = [(hi[:, 0, :], lo[:, 0, :]) for _, _, hi, lo in split[:2]]
        down = [(hi, lo) for _, _, hi, lo in split[2:]]
        w4 = sb("w4", [HID, D])
        x_in = [sb(f"x{s}", [P, D]) for s in range(K)]
        xT_hi, xT_lo = ([sb(f"{n}{s}", [P, 4, P], F32R) for s in range(2)] for n in ("xT_hi", "xT_lo"))
        hid = [sb(f"hid{s}", [HID, P]) for s in range(2)]
        s_up = [sb(f"s_up{s}", [P, 4, P]) for s in range(2)]
        msg = [sb(f"msg{s}", [P, NM, P]) for s in range(2)]
        dot = [[sb(f"dot{s}{m}", [P, P]) for m in range(3)] for s in range(2)]
        same, carry = [sb(f"same{s}", [P, P]) for s in range(K)], [sb(f"carry{s}", [P, P]) for s in range(K)]
        mT_hi, mT_lo = ([sb(f"{n}{s}", [P, NM, P], F32R) for s in range(2)] for n in ("mT_hi", "mT_lo"))
        sums = [sb(f"sums{s}", [P, D]) for s in range(K)]
        idx = sb("idx", [P, K], I32)
        pb = lambda n, s: ctx.enter_context(nc.psum_tensor(f"em_{n}", s, F32))
        psT, psU, psW, psM = pb("psT", [P, 4, P]), pb("psU", [P, 4, P]), pb("psW", [P, D]), [pb("psM0", [P, 4, P]), pb("psM1", [P, 4, P])]
        ps = [pb(f"ps{s}", [P, 4, P]) for s in range(2)]
        got, stored = [sem(f"got{s}") for s in range(K)], [sem(f"stored{s}") for s in range(K)]
        ready, held, w_in = sem("slot_ready"), sem("held"), sem("w_in")
        turned, high, low, hid_ready, upped, s_ready = (sem(n) for n in ("turned", "high", "low", "hid_ready", "upped", "s_ready"))
        dot0, dot1, dot2, msg_ready, masks_ready = (sem(n) for n in ("dot0", "dot1", "dot2", "msg_ready", "masks_ready"))
        m_done, m_high, m_low, summed, emptied = (sem(n) for n in ("m_done", "m_high", "m_low", "summed", "emptied"))
        block = ctx.enter_context(nc.Block())
        vectors = lambda ap: ap.rearrange("p (v m) -> p m v", m=3)

        @block.sync
        def _(sp):
            sp.dma_start(w4[:, :], w_mlp4).then_inc(w_in, 16)

            def step(i, s):
                t = i * K + s
                sp.wait_ge(emptied, t + 1)
                sp.dma_start(out[bass.ds(t * P, P), :], sums[s][:, :]).then_inc(stored[s], 16)

            rounds(sp, ET, step)
            for s in range(K):
                sp.wait_ge(stored[s], ET // K * 16)

        @block.gpsimd
        def _(pool):
            last_row = pool.to_reg(N - 1)

            def step(i, s):
                t = i * K + s
                if later(i):
                    pool.wait_ge(turned, t - K + 1)
                hold(pool, ready, t + 1, held)
                nc.gpsimd.indirect_dma_start(x_in[s][:, :], None, x, bass.IndirectOffsetOnAxis(idx[:, s:s + 1], 0),
                                             bounds_check=last_row, oob_is_err=False).then_inc(got[s], 16)

            rounds(pool, ET, step)

        @block.tensor
        def _(pe):
            pe.wait_ge(w_in, 16)

            def turn(i, s):
                t = i * K + s
                pe.wait_ge(got[s], i * 16 + 16)
                if not (isinstance(t, int) and t == 0):
                    pe.wait_ge(low, t)
                nc.tensor.transpose(psT[:, 0, :], x_in[s][:, 0:MUL], g.ident[:, :])
                for m in range(3):
                    last = nc.tensor.transpose(psT[:, 1 + m, :], vectors(x_in[s][:, MUL:D])[:, m, :], g.ident[:, :])
                last.then_inc(turned, 1)

            def lift(i, s):
                t, h = i * K + s, s % 2
                pe.wait_ge(low, t + 1)
                pe.wait_ge(hid_ready, t + 1)
                if not (isinstance(t, int) and t == 0):
                    pe.wait_ge(msg_ready, t)
                for m in range(4):
                    w_hi, w_lo = up[min(m, 1)]
                    for n, (a, b) in enumerate(((xT_hi, w_hi), (xT_hi, w_lo), (xT_lo, w_hi))):
                        nc.tensor.matmul(psU[:, m, :], a[h][:, m, :], b, start=n == 0, stop=n == 2)
                nc.tensor.matmul(psW[:, :], hid[h][:, :], w4[:, :], start=True, stop=True).then_inc(upped, 1)

            def gather(i, s):
                t, h = i * K + s, s % 2
                pe.wait_ge(msg_ready, t + 1)
                pe.wait_ge(masks_ready, t + 1)
                if not (isinstance(t, int) and t == 0):
                    pe.wait_ge(m_low, t)
                for c in range(NM):
                    last = nc.tensor.matmul(psM[c // 4][:, c % 4, :], msg[h][:, c, :], same[s][:, :], start=True, stop=True)
                last.then_inc(m_done, 1)

            def project(i, s):
                t, h = i * K + s, s % 2
                pe.wait_ge(m_low, t + 1)
                if exists(back(i, s, 2)[0]):
                    pe.wait_ge(emptied, t - 1)
                alone = isinstance(t, int) and t == 0
                for r in range(4):
                    w_hi, w_lo = down[min(r, 1)]
                    n = 0
                    for a, b in ((mT_hi, w_hi), (mT_hi, w_lo), (mT_lo, w_hi)):
                        for c in range(2):
                            last = nc.tensor.matmul(ps[h][:, r, :], a[h][:, 2 * r + c, :], b[:, c, :], start=n == 0,
                                                    stop=alone and n == 5)
                            n += 1
                    if not alone:
                        if r == 0:
                            pe.wait_ge(emptied, t)
                        before = sums[s - 1][:, 0:MUL] if r == 0 else vectors(sums[s - 1][:, MUL:D])[:, r - 1, :]
                        last = nc.tensor.matmul(ps[h][:, r, :], carry[s][:, :], before, start=False, stop=True)
                last.then_inc(summed, 1)

            def step(i, s):
                turn(i, s)
                for k, f in ((1, lift), (2, gather), (3, project)):
                    if exists(back(i, s, k)[0]):
                        f(*back(i, s, k))

            rounds(pe, ET, step)
            n = ET - 1
            for k, f in ((0, lift), (1, gather), (2, project), (0, gather), (1, project), (0, project)):
                f(*divmod(n - k, K))

        @block.scalar
        def _(act):
            def highs(i, s):
                t, h = i * K + s, s % 2
                if exists(back(i, s, 2)[0]):
                    act.wait_ge(upped, t - 1)
                nc.scalar.activation(hid[h][:, :], g.hid3[:, bass.ds(t * P, P)], ACT.Copy).then_inc(hid_ready, 1)
                act.wait_ge(turned, t + 1)
                nc.scalar.activation(xT_hi[h][:, :, :], psT[:, :, :], ACT.Copy).then_inc(high, 1)

            def lifted(i, s):
                t, h = i * K + s, s % 2
                act.wait_ge(upped, t + 1)
                if exists(back(i, s, 2)[0]):
                    act.wait_ge(msg_ready, t - 1)
                nc.scalar.activation(s_up[h][:, :, :], psU[:, :, :], ACT.Copy, scale=SCALE).then_inc(s_ready, 1)

            def message_highs(i, s):
                t, h = i * K + s, s % 2
                act.wait_ge(m_done, t + 1)
                if exists(back(i, s, 2)[0]):
                    act.wait_ge(summed, t - 1)
                for b in range(2):
                    last = nc.scalar.activation(mT_hi[h][:, 4 * b:4 * b + 4, :], psM[b][:, :, :], ACT.Copy)
                last.then_inc(m_high, 1)

            def empty(i, s):
                t, h = i * K + s, s % 2
                act.wait_ge(summed, t + 1)
                if later(i):
                    act.wait_ge(stored[s], i * 16)
                nc.scalar.activation(sums[s][:, 0:MUL], ps[h][:, 0, :], ACT.Copy)
                nc.scalar.activation(sums[s][:, MUL:D].rearrange("p (v m) -> p v m", m=3),
                                     ps[h][:, 1:4, :].rearrange("p m v -> p v m"), ACT.Copy).then_inc(emptied, 1)

            def step(i, s):
                highs(i, s)
                for k, f in ((1, lifted), (2, message_highs), (3, empty)):
                    if exists(back(i, s, k)[0]):
                        f(*back(i, s, k))

            rounds(act, ET, step)
            n = ET - 1
            for k, f in ((0, lifted), (1, message_highs), (2, empty), (0, message_highs), (1, empty), (0, empty)):
                f(*divmod(n - k, K))

        @block.vector
        def _(dve):
            def stage(t, s):
                nc.vector.tensor_scalar(idx[:, s:s + 1], g.src_row[:, 1, bass.ds(t, 1)], 0.0, None, ALU.add)\
                  .then_inc(ready, 1)

            def lows(i, s):
                t, h = i * K + s, s % 2
                dve.wait_ge(high, t + 1)
                nc.vector.tensor_tensor(xT_lo[h][:, :, :], psT[:, :, :], xT_hi[h][:, :, :].bitcast(F32),
                                        ALU.subtract).then_inc(low, 1)
                if not (isinstance(t, int) and t + K >= ET):
                    dve.wait_ge(got[s], i * 16 + 16)
                    stage(t + K, s)
                if later(i):
                    dve.wait_ge(summed, t - K + 1)
                nc.vector.tensor_scalar(same[s][:, :], g.key_row[:, 1, bass.ds(t * P, P)],
                                        g.rec[1][:, bass.ds(t, 1), 1], None, ALU.is_equal)
                nc.vector.tensor_scalar(carry[s][:, :], g.key_row[:, 1, bass.ds(t * P, P)],
                                        g.prev_last[:, 1, bass.ds(t, 1)], None, ALU.is_equal).then_inc(masks_ready, 1)

            def messages(i, s):
                t, h = i * K + s, s % 2
                y = [g.rec[1][:, bass.ds(t, 1), 2 + m] for m in range(4)]
                sv, w, o = s_up[h], psW, msg[h]
                dve.wait_ge(s_ready, t + 1)
                if exists(back(i, s, 2)[0]):
                    dve.wait_ge(m_done, t - 1)
                    dve.wait_ge(msg_ready, t - 1)
                nc.vector.tensor_scalar(dot[h][0][:, :], sv[:, 1, :], y[1], None, ALU.mult).then_inc(dot0, 1)
                nc.vector.scalar_tensor_tensor(o[:, 0, :], w[:, 0:MUL], y[0], sv[:, 0, :], ALU.mult, ALU.mult)
                dve.wait_ge(dot0, t + 1)
                nc.vector.scalar_tensor_tensor(dot[h][1][:, :], sv[:, 2, :], y[2], dot[h][0][:, :], ALU.mult, ALU.add)\
                  .then_inc(dot1, 1)
                for m in range(3):
                    nc.vector.scalar_tensor_tensor(o[:, 2 + 2 * m, :], w[:, MUL:2 * MUL], y[1 + m], sv[:, 0, :],
                                                   ALU.mult, ALU.mult)
                dve.wait_ge(dot1, t + 1)
                nc.vector.scalar_tensor_tensor(dot[h][2][:, :], sv[:, 3, :], y[3], dot[h][1][:, :], ALU.mult, ALU.add)\
                  .then_inc(dot2, 1)
                nc.vector.scalar_tensor_tensor(o[:, :, :].rearrange("p (a b) v -> p b a v", b=2)[:, 1, 1:4, :],
                                               w[:, 2 * MUL:3 * MUL].unsqueeze(1).to_broadcast([P, 3, MUL]), y[0],
                                               sv[:, 1:4, :], ALU.mult, ALU.mult)
                dve.wait_ge(dot2, t + 1)
                nc.vector.scalar_tensor_tensor(o[:, 1, :], w[:, 3 * MUL:4 * MUL], 3.0 ** -0.5, dot[h][2][:, :],
                                               ALU.mult, ALU.mult).then_inc(msg_ready, 1)

            def message_lows(i, s):
                t, h = i * K + s, s % 2
                dve.wait_ge(m_high, t + 1)
                for b in range(2):
                    last = nc.vector.tensor_tensor(mT_lo[h][:, 4 * b:4 * b + 4, :], psM[b][:, :, :],
                                                   mT_hi[h][:, 4 * b:4 * b + 4, :].bitcast(F32), ALU.subtract)
                last.then_inc(m_low, 1)

            for s in range(K):
                stage(s, s)

            def step(i, s):
                lows(i, s)
                for k, f in ((1, messages), (2, message_lows)):
                    if exists(back(i, s, k)[0]):
                        f(*back(i, s, k))

            rounds(dve, ET, step)
            n = ET - 1
            for k, f in ((0, messages), (1, message_lows), (0, message_lows)):
                f(*divmod(n - k, K))


class Shared:
    pass


def persistent(nc, ctx, g):
    sb = lambda n, s, d=F32: ctx.enter_context(nc.sbuf_tensor(n, s, d))
    dram = lambda n, s: nc.dram_tensor(n, s, F32, kind="Internal").ap()
    g.ident, g.ones, g.ident_bf = sb("ident", [P, P]), sb("ones", [P, P]), sb("ident_bf", [P, P], BF16)
    g.before, g.after = sb("before", [P, P]), sb("after", [P, P])
    g.last_row, g.one_col, g.eps_col = sb("last_row", [P, 1]), sb("one_col", [P, 1]), sb("eps_col", [P, 1])
    g.zeros = sb("zero_rows", [P, D])
    g.node_row, g.dis = sb("node_row", [P, 2, NT], I32), sb("dis", [P, NT])
    g.rec = [sb(f"rec{o}", [P, ET, REC]) for o in range(2)]
    g.src_any, g.src_row, g.dst_row = (sb(n, [P, 2, ET], I32) for n in ("src_any", "src_row", "dst_row"))
    g.prev_last = sb("prev_last", [P, 2, ET])
    g.src_tab, g.src_comp = sb("src_tab", [P, ET, 4]), sb("src_comp", [P, 2, ET], I32)
    g.key_row = sb("key_row", [P, 2, EPAD])
    g.att = sb("att", [P, ET, HEADS])
    g.ntab_dram = dram("ntab_dram", [NT * P, 4])
    g.rec_dram = [dram(f"rec_dram{o}", [EPAD, REC]) for o in range(2)]


def prepare(nc, g):
    with ExitStack() as ctx:
        sb = lambda n, s, d=F32: ctx.enter_context(nc.sbuf_tensor(n, s, d))
        g.hot_hi, g.hot_lo = sb("hot_hi", [P, 2, ET, NT], BF16), sb("hot_lo", [P, 2, ET, P], BF16)
        g.keys, g.ntab = sb("keys", [P, 2, ET]), sb("ntab", [NT, P, 4])
        g.iota = sb("iota_row", [P, P])
        load_edges(nc, g)
        sort_positions(nc, g)
        sort_by_dst(nc, g)


def graph_network(nc, x, src, dst, edge_attr_4, edge_attr_8, w_up0, w_up1, w_mlp1, w_mlp2, w_mlp3, w_mlp4,
                  w_out0, w_out1, mlp_w1, mlp_b1, mlp_w2, mlp_b2, wq, bq, wk, bk, wv, bv, wo, bo,
                  conv_w1, conv_b1, conv_w2, conv_b2, out):
    g = Shared()
    g.src, g.dst, g.edge_attr_4, g.edge_attr_8 = src, dst, edge_attr_4, edge_attr_8
    table = lambda n, rows: nc.dram_tensor(n, [rows, D], F32, kind="Internal").ap()
    messages, x1_sums, attended, x3_sums, conv_sums, v = (table(n, TROWS) for n in (
        "messages", "x1_sums", "attended", "x3_sums", "conv_sums", "v_edges"))
    g.summed_tables = (messages, x1_sums, x3_sums, conv_sums)
    x2, x3, hidden = (table(n, N) for n in ("x2", "x3", "conv_hidden"))
    with ExitStack() as ctx:
        persistent(nc, ctx, g)
        stage = nc.cleanup_on_exit
        with nc.sbuf_tensor("rec_in", [P, ET, REC], F32) as g.rec_in, nc.sbuf_tensor("position", [P, 2, ET], F32) as g.position, \
             nc.sbuf_tensor("hid3", [HID, EPAD], F32) as g.hid3:
            with stage():
                prepare(nc, g)
            with stage():
                radial(nc, g, w_mlp1, w_mlp2, w_mlp3)
            with stage():
                edge_messages(nc, g, x, w_up0, w_up1, w_mlp4, w_out0, w_out1, messages)
        with stage():
            edge_sums(nc, g, "e1", x, x1_sums, comp=messages, comp_order=1)
        with stage():
            node_mlp(nc, g, x, messages, x1_sums, mlp_w1, mlp_b1, mlp_w2, mlp_b2, x2)
        with nc.sbuf_tensor("logits_T", [HEADS, EPAD], F32) as g.logits_T:
            with stage():
                edge_logits(nc, g, x2, (wq, wk, wv), (bq, bk, bv), v)
            with stage():
                edge_softmax(nc, g)
        with stage():
            edge_attend(nc, g, v, wo, bo, attended)
        with stage():
            edge_sums(nc, g, "e3", x2, x3_sums, comp=attended, comp_order=0, by_degree=True)
        with stage():
            node_conv1(nc, g, x2, attended, x3_sums, conv_w1, conv_b1, x3, hidden)
        with stage():
            edge_sums(nc, g, "e4", hidden, conv_sums, normed=False)
        with stage():
            node_conv2(nc, g, x3, hidden, conv_sums, conv_w2, conv_b2, out)


_INS = ['x', 'src', 'dst', 'edge_attr_4', 'edge_attr_8', 'L0_gnn_W_up0', 'L0_gnn_W_up1', 'L0_gnn_W_mlp1',
        'L0_gnn_W_mlp2', 'L0_gnn_W_mlp3', 'L0_gnn_W_mlp4', 'L0_gnn_W_out0', 'L0_gnn_W_out1', 'L1_gnn_W1',
        'L1_gnn_b1', 'L1_gnn_W2', 'L1_gnn_b2', 'L2_gnn_Wq', 'L2_gnn_bq', 'L2_gnn_Wk', 'L2_gnn_bk', 'L2_gnn_Wv',
        'L2_gnn_bv', 'L2_gnn_Wo', 'L2_gnn_bo', 'L3_gnn_W1', 'L3_gnn_b1', 'L3_gnn_W2', 'L3_gnn_b2']
_OUTS = [((10000, 512), 'float32')]


def kernel(**inputs):
    import numpy as _np
    import concourse.bacc as _bacc
    from concourse import mybir as _mybir
    from concourse.bass_utils import run_bass_kernel_spmd as _run

    nc = _bacc.Bacc("TRN2", target_bir_lowering=False, num_devices=1)
    arrays, args = {}, []
    for name in _INS:
        a = _np.ascontiguousarray(inputs[name])
        arrays[f"in_{name}_dram"] = a
        args.append(nc.dram_tensor(f"in_{name}_dram", a.shape, _mybir.dt.from_np(a.dtype), kind="ExternalInput").ap())
    for i, (shape, dtype) in enumerate(_OUTS):
        dt = _mybir.dt.from_np(_np.dtype(dtype))
        args.append(nc.dram_tensor(f"out_{i}_dram", shape, dt, kind="ExternalOutput").ap())
    graph_network(nc, *args)
    r = _run(nc, [arrays], core_ids=[0])
    got = tuple(r.results[0][f"out_{i}_dram"] for i in range(len(_OUTS)))
    return got[0]
```

```python
import concourse.bass as bass
from concourse import mybir
from contextlib import ExitStack

F32 = mybir.dt.float32
F32R = mybir.dt.float32r
BF16 = mybir.dt.bfloat16
I32 = mybir.dt.int32
ALU = mybir.AluOpType
ACT = mybir.ActivationFunctionType
AX = mybir.AxisListType

P = 128
N = 10000
E = 5000
D = 512
KC = D // P
NT = -(-N // P)
NLAST = N - (NT - 1) * P
ET = 40
EP = E // ET
EPAD = ET * P
PAD_NODE = N + 100
TROWS = EPAD + P
REC = 16


K = 4


def rounds(eng, n, step, peel=2):
    for i in range(peel):
        for s in range(K):
            step(i, s)
    with eng.Fori(peel, n // K - 1) as i:
        for s in range(K):
            step(i, s)
    for t in range((n // K - 1) * K, n):
        step(t // K, t % K)


def skewed(eng, n, stages, k, ahead=0, peel=2):
    def step(i, s):
        for lag, f in stages:
            c, r = divmod(s - lag, k)
            j = i + c if c else i
            if not isinstance(j, int) or 0 <= j * k + r < n:
                f(j, r)

    end = (n - 1 - ahead) // k
    for t in range(-ahead, peel * k):
        step(*divmod(t, k))
    with eng.Fori(peel, end) as i:
        for s in range(k):
            step(i, s)
    for t in range(end * k, n + max(lag for lag, _ in stages)):
        step(*divmod(t, k))


def back(i, s, k):
    return (i, s - k) if s >= k else (i - 1, s - k + K)


def exists(i):
    return not isinstance(i, int) or i >= 0


def later(i):
    return not isinstance(i, int) or i >= 1


def hold(eng, sem, value, held):
    eng.wait_ge(sem, value)
    eng.sem_inc(held, 1)


def load_edges(nc, g):
    with ExitStack() as ctx:
        a4 = ctx.enter_context(nc.sbuf_tensor("a4_in", [P, ET * 4], F32))
        a8 = ctx.enter_context(nc.sbuf_tensor("a8_in", [P, ET * 8], F32))
        his = ctx.enter_context(nc.sbuf_tensor("hi_int", [P, 2, ET], I32))
        los = ctx.enter_context(nc.sbuf_tensor("lo_int", [P, 2, ET], I32))
        hif = ctx.enter_context(nc.sbuf_tensor("hi_f", [P, 2, ET], F32))
        lof = ctx.enter_context(nc.sbuf_tensor("lo_f", [P, 2, ET], F32))
        ids = ctx.enter_context(nc.sbuf_tensor("ids_int", [P, 2, ET], I32))
        iota = g.iota
        sem = lambda n: nc.alloc_semaphore(n)
        filled, loaded, attrs_loaded, made = sem("le_filled"), sem("le_loaded"), sem("le_attrs"), sem("le_made")
        block = ctx.enter_context(nc.Block())

        @block.sync
        def _(sp):
            sp.wait_ge(filled, 1)
            sp.dma_start(ids[0:EP, 0, :], g.src.rearrange("(p t) -> p t", t=ET)).then_inc(loaded, 16)
            sp.dma_start(ids[0:EP, 1, :], g.dst.rearrange("(p t) -> p t", t=ET)).then_inc(loaded, 16)
            sp.dma_start(a4[0:EP, :], g.edge_attr_4.rearrange("(p t) c -> p (t c)", t=ET)).then_inc(attrs_loaded, 16)
            sp.dma_start(a8[0:EP, :], g.edge_attr_8.rearrange("(p t) c -> p (t c)", t=ET)).then_inc(attrs_loaded, 16)

        @block.gpsimd
        def _(pool):
            nc.gpsimd.iota(iota[:, :], [[1, P]], base=0, channel_multiplier=0,
                           allow_small_or_imprecise_dtypes=True).then_inc(made, 1)
            nc.gpsimd.memset(g.ident[:, :], 0.0).then_inc(made, 1)
            nc.gpsimd.memset(g.ones[:, :], 1.0).then_inc(made, 1)
            nc.gpsimd.memset(g.before[:, :], 1.0).then_inc(made, 1)
            pool.wait_ge(made, 4)
            nc.gpsimd.affine_select(out=g.ident[:, :], in_=g.ident[:, :], compare_op=ALU.not_equal, fill=1.0,
                                    base=0, pattern=[[-1, P]], channel_multiplier=1).then_inc(made, 1)
            nc.gpsimd.affine_select(out=g.before[:, :], in_=g.before[:, :], compare_op=ALU.is_gt, fill=0.0,
                                    base=0, pattern=[[1, P]], channel_multiplier=-1).then_inc(made, 1)

        @block.vector
        def _(dve):
            nc.vector.memset(ids[:, :, :], PAD_NODE).then_inc(filled, 1)
            nc.vector.memset(g.rec_in[:, :, :], 0.0).then_inc(filled, 1)
            dve.wait_ge(made, 6)
            nc.vector.tensor_copy(g.ident_bf[:, :], g.ident[:, :])
            nc.vector.tensor_copy(g.last_row[:, :], g.ident[:, P - 1:P])
            nc.vector.tensor_tensor(g.after[:, :], g.ones[:, :], g.before[:, :], ALU.subtract).then_inc(filled, 1)
            dve.wait_ge(filled, 3)
            nc.vector.tensor_tensor(g.after[:, :], g.after[:, :], g.ident[:, :], ALU.subtract)
            dve.wait_ge(loaded, 32)
            nc.vector.tensor_scalar(his[:, :, :], ids[:, :, :], 7, None, ALU.arith_shift_right).then_inc(filled, 1)
            nc.vector.tensor_scalar(los[:, :, :], ids[:, :, :], P - 1, None, ALU.bitwise_and).then_inc(filled, 1)
            nc.vector.tensor_copy(g.keys[:, :, :], ids[:, :, :]).then_inc(filled, 1)
            dve.wait_ge(filled, 6)
            nc.vector.tensor_copy(hif[:, :, :], his[:, :, :]).then_inc(filled, 1)
            nc.vector.tensor_copy(lof[:, :, :], los[:, :, :]).then_inc(filled, 1)
            dve.wait_ge(filled, 8)
            for o in range(2):
                nc.vector.tensor_tensor(g.hot_hi[:, o, :, :], iota[:, 0:NT].unsqueeze(1).to_broadcast([P, ET, NT]),
                                        hif[:, o, :].unsqueeze(2).to_broadcast([P, ET, NT]), ALU.is_equal)
                nc.vector.tensor_tensor(g.hot_lo[:, o, :, :], iota[:, :].unsqueeze(1).to_broadcast([P, ET, P]),
                                        lof[:, o, :].unsqueeze(2).to_broadcast([P, ET, P]), ALU.is_equal)
                nc.vector.tensor_copy(g.rec_in[:, :, o], g.keys[:, o, :])
            dve.wait_ge(attrs_loaded, 32)
            nc.vector.tensor_copy(g.rec_in[0:EP, :, 2:6], a4[0:EP, :].rearrange("p (t c) -> p t c", c=4))
            nc.vector.tensor_copy(g.rec_in[0:EP, :, 6:14], a8[0:EP, :].rearrange("p (t c) -> p t c", c=8))


def scatter_tile(nc, g, o, rec_out, pos_out, s, done):
    nc.gpsimd.indirect_dma_start(g.rec_dram[o], bass.IndirectOffsetOnAxis(pos_out[:, s:s + 1], 0),
                                 rec_out[:, s, :], None, bounds_check=g.last_edge, oob_is_err=False).then_inc(done, 16)


def stage_tile(nc, g, o, rec_out, pos_out, t, s, staged):
    nc.vector.tensor_scalar(rec_out[:, s, :], g.rec_in[:, bass.ds(t, 1), :].rearrange("p a b -> p (a b)"),
                            0.0, None, ALU.add)
    nc.vector.tensor_scalar(pos_out[:, s:s + 1], g.position[:, o, bass.ds(t, 1)], 0.0, None, ALU.add)\
      .then_inc(staged, 1)


def sorted_ids(nc, g, o, dve, done):
    nc.vector.tensor_copy(g.src_any[:, o, :], g.rec[o][:, :, 0])
    nc.vector.tensor_scalar(g.src_row[:, o, :], g.rec[o][:, :, 0], float(N - 1), None, ALU.min)
    nc.vector.tensor_scalar(g.dst_row[:, o, :], g.rec[o][:, :, 1], float(N - 1), None, ALU.min)
    nc.vector.memset(g.prev_last[:, o, 0:1], -1.0)
    nc.vector.tensor_scalar(g.prev_last[:, o, 1:ET], g.rec[o][:, 0:ET - 1, o], 1.0,
                            g.last_row[:, 0:1], ALU.add, ALU.mult).then_inc(done, 1)
    dve.wait_ge(done, 1)
    nc.vector.tensor_scalar(g.prev_last[:, o, 1:ET], g.prev_last[:, o, 1:ET], 1.0, None, ALU.subtract).then_inc(done, 1)


def sort_positions(nc, g):
    with ExitStack() as ctx:
        sb = lambda n, s, d=F32: ctx.enter_context(nc.sbuf_tensor(n, s, d))
        sem = lambda n: nc.alloc_semaphore(n)
        total, upto = sb("total", [NT, 2, P]), sb("upto", [NT, 2, P])
        row_start, spare = sb("row_start", [NT, 2]), sb("spare", [NT, 2, P])
        running = [sb(f"running{s}", [NT, 2, P]) for s in range(2)]
        hot_T = [sb(f"hot_T{s}", [NT, 2, P]) for s in range(2)]
        key_diag = [sb(f"key_diag{s}", [P, 2, P]) for s in range(2)]
        picked, tied = sb("picked", [P, 2, ET]), sb("tied", [P, 2, ET])
        scrap = [sb(f"scrap{s}", [P, 4, P]) for s in range(2)]
        zeros, ndeg, root = sb("zeros", [NT, P]), sb("ndeg", [NT, P]), sb("root", [NT, 4, P])
        ps_total = ctx.enter_context(nc.psum_tensor("ps_total", [NT, 4, P], F32))
        ps_total2 = ctx.enter_context(nc.psum_tensor("ps_total2", [NT, 4, P], F32))
        ps_hot = [ctx.enter_context(nc.psum_tensor(f"ps_hot{s}", [NT, 4, P], F32)) for s in range(2)]
        ps_key = [ctx.enter_context(nc.psum_tensor(f"ps_key{s}", [P, 4, P], F32)) for s in range(2)]
        ps_pick = [ctx.enter_context(nc.psum_tensor(f"ps_pick{s}", [P, 4, P], F32)) for s in range(2)]
        counted, summed, started, chain = sem("so_counted"), sem("so_summed"), sem("so_started"), sem("so_chain")
        hot_ready, hot_copied, diag_ready = sem("so_hot_ready"), sem("so_hot_copied"), sem("so_diag_ready")
        key_ready, picked_ready, tile_done = sem("so_key_ready"), sem("so_picked_ready"), sem("so_tile_done")
        table_ready, turned, stored = sem("so_table_ready"), sem("so_turned"), sem("so_stored")
        cols_ready, running_ready = sem("so_cols_ready"), sem("so_running_ready")
        zeroed, zeros_stored = sem("so_zeroed"), sem("so_zeros_stored")
        rec_out, pos_out = sb("rec_out", [P, K, REC]), sb("pos_out", [P, K], I32)
        scattered = [sem(f"so_scattered{s}") for s in range(K)]
        placed, held, reloaded, ids_ready = sem("so_placed"), sem("so_held"), sem("so_reloaded"), sem("so_ids_ready")
        held_dve = sem("so_held_dve")
        block = ctx.enter_context(nc.Block())

        def by_tile(step):
            return lambda i, s: step(i * K + s, s % 2, isinstance(i, int) and i * K + s < 2)

        @block.gpsimd
        def _(pool):
            nc.gpsimd.memset(g.zeros[:, :], 0.0).then_inc(zeroed, 1)
            g.last_edge = pool.to_reg(EPAD - 1)

            def scatter(i, s):
                hold(pool, placed, i * K + s + 1, held)
                scatter_tile(nc, g, 1, rec_out, pos_out, s, scattered[s])

            skewed(pool, ET, [(1, scatter)], K)

        @block.tensor
        def _(pe):
            for o, ps in ((0, ps_total), (1, ps_total2)):
                nc.tensor.matmul(ps[:, 0, :], g.hot_hi[:, o, 0, :], g.hot_lo[:, o, 0, :], start=True, stop=False)
                with pe.Fori(0, 2) as i:
                    for n in range((ET - 2) // 2):
                        t = i * ((ET - 2) // 2) + n + 1
                        nc.tensor.matmul(ps[:, 0, :], g.hot_hi[:, o, bass.ds(t, 1), :].rearrange("p a b -> p (a b)"),
                                         g.hot_lo[:, o, bass.ds(t, 1), :].rearrange("p a b -> p (a b)"),
                                         start=False, stop=False)
                nc.tensor.matmul(ps[:, 0, :], g.hot_hi[:, o, ET - 1, :], g.hot_lo[:, o, ET - 1, :],
                                 start=False, stop=True).then_inc(counted, 1)
            pe.wait_ge(summed, 1)
            nc.tensor.matmul(ps_total[:, 1, 0:2], g.before[0:NT, 0:NT], upto[:, :, P - 1], start=True,
                             stop=True).then_inc(started, 1)

            def step(t, s, first):
                if not first:
                    pe.wait_ge(hot_copied, t - 1)
                    pe.wait_ge(tile_done, t - 1)
                for o in range(2):
                    hot = g.hot_hi[:, o, bass.ds(t, 1), :].rearrange("p a b -> p (a b)")
                    nc.tensor.matmul(ps_hot[s][:, o, :], hot, g.ident_bf[:, :], start=True, stop=True)
                    m = nc.tensor.matmul(ps_key[s][0:NT, 2 + o, :], hot,
                                         g.hot_lo[:, o, bass.ds(t, 1), :].rearrange("p a b -> p (a b)"),
                                         start=True, stop=True)
                m.then_inc(hot_ready, 1)
                pe.wait_ge(diag_ready, t + 1)
                for o in range(2):
                    m = nc.tensor.matmul(ps_key[s][:, o, :], g.ones[:, :], key_diag[s][:, o, :], start=True, stop=True)
                m.then_inc(key_ready, 1)
                pe.wait_ge(hot_copied, t + 1)
                pe.wait_ge(running_ready, t + 1)
                for o in range(2):
                    m = nc.tensor.matmul(ps_pick[s][:, o, :], hot_T[s][:, o, :], running[s][:, o, :],
                                         start=True, stop=True)
                m.then_inc(picked_ready, 1)

            skewed(pe, ET, [(0, by_tile(step))], K)
            pe.wait_ge(table_ready, 1)
            for n in range(3):
                m = nc.tensor.transpose(ps_key[0][:, n, 0:NT], g.ntab[:, :, n], g.ident[0:NT, 0:NT])
            m.then_inc(turned, 1)

        @block.scalar
        def _(act):
            def step(t, s, first):
                if not first:
                    act.wait_ge(key_ready, t - 1)
                for o in range(2):
                    m = nc.scalar.activation(key_diag[s][:, o, :], g.ident[:, :], ACT.Copy,
                                             scale=g.keys[:, o, bass.ds(t, 1)])
                m.then_inc(diag_ready, 1)
                act.wait_ge(hot_ready, t + 1)
                if not first:
                    act.wait_ge(picked_ready, t - 1)
                nc.scalar.activation(hot_T[s][:, :, :], ps_hot[s][:, 0:2, :], ACT.Copy).then_inc(hot_copied, 1)

            skewed(act, ET, [(0, by_tile(step))], K)
            act.wait_ge(cols_ready, 1)
            nc.scalar.activation(ndeg[:, :], total[:, 1, :], ACT.Sqrt, bias=g.one_col[0:NT, :]).then_inc(cols_ready, 1)

        @block.vector
        def _(dve):
            n_chain = [0]

            def link(ins):
                n_chain[0] += 1
                ins.then_inc(chain, 1)
                dve.wait_ge(chain, n_chain[0])

            nc.vector.memset(zeros[:, :], 0.0)
            link(nc.vector.memset(g.one_col[:, :], 1.0))
            dve.wait_ge(counted, 2)
            nc.vector.tensor_copy(total[:, 0, :], ps_total[:, 0, :])
            link(nc.vector.tensor_copy(total[:, 1, :], ps_total2[:, 0, :]))
            for o in range(2):
                m = nc.vector.tensor_tensor_scan(upto[:, o, :], total[:, o, :], zeros[:, :], 0.0, ALU.add, ALU.add)
            m.then_inc(summed, 1)
            dve.wait_ge(started, 1)
            link(nc.vector.tensor_copy(row_start[:, :], ps_total[:, 1, 0:2]))
            for o in range(2):
                link(nc.vector.tensor_scalar(upto[:, o, :], upto[:, o, :], row_start[:, o:o + 1], None, ALU.add))
            nc.vector.tensor_tensor(running[0][:, :, :], upto[:, :, :], total[:, :, :], ALU.subtract)\
              .then_inc(running_ready, 1)
            dve.wait_ge(running_ready, 1)

            def step(t, s, first):
                dve.wait_ge(key_ready, t + 1)
                if not first:
                    dve.wait_ge(picked_ready, t)
                elif s == 1:
                    dve.wait_ge(picked_ready, 1)
                nc.vector.tensor_tensor(running[1 - s][:, :, :], running[s][:, :, :], ps_key[s][0:NT, 2:4, :],
                                        ALU.add).then_inc(running_ready, 1)
                if not first:
                    dve.wait_ge(tile_done, t - 1)
                for o in range(2):
                    nc.vector.scalar_tensor_tensor(scrap[s][:, o, :], ps_key[s][:, o, :], g.keys[:, o, bass.ds(t, 1)],
                                                   g.after[:, :], ALU.is_equal, ALU.mult,
                                                   accum_out=tied[:, o, bass.ds(t, 1)])
                dve.wait_ge(picked_ready, t + 1)
                for o in range(2):
                    m = nc.vector.scalar_tensor_tensor(scrap[s][:, 2 + o, :], ps_pick[s][:, o, :], 1.0,
                                                       g.hot_lo[:, o, bass.ds(t, 1), :].rearrange("p a b -> p (a b)"),
                                                       ALU.mult, ALU.mult, accum_out=picked[:, o, bass.ds(t, 1)])
                m.then_inc(tile_done, 1)
                dve.wait_ge(running_ready, t + 2)

            def place(i, s):
                t = i * K + s
                if later(i):
                    dve.wait_ge(scattered[s], i * 16)
                nc.vector.tensor_scalar(rec_out[:, s, :], g.rec_in[:, bass.ds(t, 1), :].rearrange("p a b -> p (a b)"),
                                        0.0, None, ALU.add)
                hold(dve, tile_done, t + 1, held_dve)
                nc.vector.tensor_tensor(pos_out[:, s:s + 1], picked[:, 1, bass.ds(t, 1)], tied[:, 1, bass.ds(t, 1)],
                                        ALU.add).then_inc(placed, 1)

            skewed(dve, ET, [(0, by_tile(step)), (1, place)], K)
            dve.wait_ge(tile_done, ET)
            nc.vector.tensor_tensor(g.position[:, :, :], picked[:, :, :], tied[:, :, :], ALU.add)
            for o in range(2):
                link(nc.vector.scalar_tensor_tensor(spare[:, o, :], g.iota[0:NT, :], float(EPAD + 1), upto[:, o, :],
                                                    ALU.add, ALU.subtract))
            link(nc.vector.scalar_tensor_tensor(spare[:, :, :], total[:, :, :], 0.5, spare[:, :, :],
                                                ALU.is_lt, ALU.mult))
            link(nc.vector.tensor_tensor(upto[:, :, :], upto[:, :, :], spare[:, :, :], ALU.add))
            for o in range(2):
                nc.vector.tensor_scalar(g.ntab[:, :, o], upto[:, o, :], 1.0, None, ALU.subtract)
            m = nc.vector.memset(g.ntab[:, :, 3], 0.0)
            m.then_inc(cols_ready, 1)
            dve.wait_ge(cols_ready, 2)
            link(nc.vector.reciprocal(root[:, 0, :], ndeg[:, :]))
            link(nc.vector.tensor_tensor(root[:, 1, :], root[:, 0, :], root[:, 0, :], ALU.mult))
            link(nc.vector.scalar_tensor_tensor(root[:, 2, :], total[:, 1, :], 1.0, root[:, 1, :], ALU.add, ALU.mult))
            link(nc.vector.tensor_scalar(root[:, 3, :], root[:, 2, :], -0.5, 1.5, ALU.mult, ALU.add))
            nc.vector.tensor_tensor(g.ntab[:, :, 2], root[:, 0, :], root[:, 3, :], ALU.mult).then_inc(table_ready, 1)
            dve.wait_ge(turned, 1)
            nc.vector.tensor_copy(g.node_row[:, 0, :], ps_key[0][:, 0, 0:NT])
            nc.vector.tensor_copy(g.node_row[:, 1, :], ps_key[0][:, 1, 0:NT])
            nc.vector.tensor_copy(g.dis[:, :], ps_key[0][:, 2, 0:NT])
            nc.vector.memset(g.eps_col[:, :], 1e-5)
            dve.wait_ge(reloaded, 16)
            sorted_ids(nc, g, 1, dve, ids_ready)

        @block.sync
        def _(sp):
            sp.wait_ge(zeroed, 1)
            for table in g.summed_tables:
                sp.dma_start(table[EPAD:TROWS, :], g.zeros[:, :]).then_inc(zeros_stored, 16)
            for s in range(K):
                sp.wait_ge(scattered[s], ET // K * 16)
            sp.dma_start(g.rec[1][:, :, :], g.rec_dram[1].rearrange("(t p) c -> p t c", p=P)).then_inc(reloaded, 16)
            sp.wait_ge(zeros_stored, 16 * len(g.summed_tables))
            sp.wait_ge(table_ready, 1)
            sp.dma_start(g.ntab_dram.rearrange("(h l) c -> h l c", l=P), g.ntab[:, :, :]).then_inc(stored, 16)
            sp.wait_ge(stored, 16)


class Weights:

    def __init__(self, nc, ctx, weights):
        self.nc, self.weights = nc, weights
        name = weights[0][0]
        self.full = [ctx.enter_context(nc.sbuf_tensor(f"full_{n}", list(hi.shape), F32))[:, :, :] for n, _, hi, _ in weights]
        self.loaded = [nc.alloc_semaphore(f"w_loaded_{n}") for n, _, _, _ in weights]
        self.high, self.low = nc.alloc_semaphore(f"w_high_{name}"), nc.alloc_semaphore(f"w_low_{name}")

    def load(self, sp):
        for (_, src, _, _), f, loaded in zip(self.weights, self.full, self.loaded):
            sp.dma_start(f, src).then_inc(loaded, 16)

    def highs(self, act):
        for (_, _, hi, _), f, loaded in zip(self.weights, self.full, self.loaded):
            act.wait_ge(loaded, 16)
            self.nc.scalar.activation(hi[:, :, :], f, ACT.Copy).then_inc(self.high, 1)

    def lows(self, dve):
        for k, ((_, _, hi, lo), f, loaded) in enumerate(zip(self.weights, self.full, self.loaded)):
            dve.wait_ge(loaded, 16)
            dve.wait_ge(self.high, k + 1)
            self.nc.vector.tensor_tensor(lo[:, :, :], f, hi[:, :, :].bitcast(F32), ALU.subtract).then_inc(self.low, 1)


def split_weight(nc, ctx, name, src, k, n):
    hi = ctx.enter_context(nc.sbuf_tensor(f"{name}_hi", [P, k, n], F32R))
    lo = ctx.enter_context(nc.sbuf_tensor(f"{name}_lo", [P, k, n], F32R))
    return (name, src.rearrange("(k p) n -> p k n", p=P), hi, lo)


def edge_sums(nc, g, tag, rows, out, comp=None, comp_order=0, by_degree=False, normed=True, in_order=False, then=None):
    S, B = 8, 4
    HALF = D // 2
    with ExitStack() as ctx:
        sb = lambda n, s, d=F32: ctx.enter_context(nc.sbuf_tensor(f"{tag}_{n}", s, d))
        sem = lambda n: nc.alloc_semaphore(f"{tag}_{n}")
        x = [sb(f"x{s}", [P, D]) for s in range(S)]
        carry = [sb(f"carry{s}", [P, P]) for s in range(S)]
        sums = [sb(f"sums{s}", [P, D]) for s in range(S)]
        row_idx = sb("row_idx", [P, S], I32)
        ps = [[ctx.enter_context(nc.psum_tensor(f"{tag}_ps{c}{s}", [P, D], F32)) for s in range(B)] for c in range(2)]
        half = [slice(c * HALF, (c + 1) * HALF) for c in range(2)]
        lag = 4
        if not normed:
            same = [sb(f"same_parts{s}", [P, P], F32R) for s in range(S)]
            x_hi, x_lo = ([sb(f"{n}{s}", [P, D], F32R) for s in range(S)] for n in ("x_hi", "x_lo"))
        if normed:
            lag = 8
            comp_idx = sb("comp_idx", [P, S], I32)
            same = [sb(f"same{s}", [P, P]) for s in range(S)]
            m = [sb(f"m{s}", [P, D]) for s in range(S)]
            stats, mv = sb("stats", [P, S, 6]), sb("mv", [P, S, 2])
            std, rstd, shift, rdis = (sb(n, [P, S]) for n in ("std", "rstd", "shift", "rdis"))
        got_x, got_c = [sem(f"got_x{s}") for s in range(S)], [sem(f"got_c{s}") for s in range(S)]
        stored = [sem(f"stored{s}") for s in range(S)]
        ready, comp_ready, held = sem("rows_ready"), sem("comp_ready"), sem("held")
        measured, var_ready, std_ready = sem("measured"), sem("var_ready"), sem("std_ready")
        inverted, coef_ready, m_ready, masks_ready = sem("inverted"), sem("coef_ready"), sem("m_ready"), sem("masks_ready")
        half_summed, half_emptied = ([sem(f"{n}{c}") for c in range(2)] for n in ("summed", "emptied"))
        summed, emptied, scaled = half_summed[1], half_emptied[1], sem("scaled")
        high, low = sem("high"), sem("low")
        weights = Weights(nc, ctx, then)
        block = ctx.enter_context(nc.Block())

        @block.gpsimd
        def _(pool):
            last_row, last_sum = pool.to_reg(N - 1), pool.to_reg(TROWS - 1)

            def gather(i, s):
                t = i * S + s
                if later(i):
                    pool.wait_ge(m_ready if normed else low, t - S + 1)
                hold(pool, ready, t + 1, held)
                nc.gpsimd.indirect_dma_start(x[s][:, :], None, rows, bass.IndirectOffsetOnAxis(row_idx[:, s:s + 1], 0),
                                             bounds_check=last_row, oob_is_err=False).then_inc(got_x[s], 16)

            def add_sums(i, s):
                pool.wait_ge(comp_ready, i * S + s + 1)
                hold(pool, got_x[s], i * 16 + 16, held)
                nc.gpsimd.indirect_dma_start(x[s][:, :], None, comp, bass.IndirectOffsetOnAxis(comp_idx[:, s:s + 1], 0),
                                             bounds_check=last_sum, compute_op=ALU.add).then_inc(got_c[s], 16)

            skewed(pool, ET, ([] if in_order else [(0, gather)]) + ([(2, add_sums)] if normed else []), S)

        @block.vector
        def _(dve):
            def stage(i, s):
                t = i * S + s
                if not in_order:
                    if later(i):
                        dve.wait_ge(got_x[s], i * 16)
                    nc.vector.tensor_scalar(row_idx[:, s:s + 1], g.src_row[:, 1, bass.ds(t, 1)], 0.0, None, ALU.add)\
                      .then_inc(ready, 1)
                if normed:
                    if later(i):
                        dve.wait_ge(got_c[s], i * 16)
                    nc.vector.tensor_scalar(comp_idx[:, s:s + 1], g.src_comp[:, comp_order, bass.ds(t, 1)],
                                            0.0, None, ALU.add).then_inc(comp_ready, 1)

            def measure(i, s):
                t = i * S + s
                dve.wait_ge(got_c[s], i * 16 + 16)
                nc.vector.bn_stats(stats[:, s, :], x[s][:, :]).then_inc(measured, 1)

            def aggregate(i, s):
                hold(dve, measured, i * S + s + 1, held)
                nc.vector.bn_aggr(mv[:, s, :], stats[:, s, :]).then_inc(var_ready, 1)

            def lows(i, s):
                dve.wait_ge(high, i * S + s + 1)
                nc.vector.tensor_tensor(x_lo[s][:, :], x[s][:, :], x_hi[s][:, :].bitcast(F32), ALU.subtract).then_inc(low, 1)

            def masks(i, s):
                t = i * S + s
                if later(i):
                    dve.wait_ge(summed, t - S + 1)
                nc.vector.tensor_scalar(same[s][:, :], g.key_row[:, 1, bass.ds(t * P, P)],
                                        g.rec[1][:, bass.ds(t, 1), 1], None, ALU.is_equal)
                nc.vector.tensor_scalar(carry[s][:, :], g.key_row[:, 1, bass.ds(t * P, P)],
                                        g.prev_last[:, 1, bass.ds(t, 1)], None, ALU.is_equal).then_inc(masks_ready, 1)

            def coefs(i, s):
                t = i * S + s
                dve.wait_ge(std_ready, t + 1)
                nc.vector.reciprocal(rstd[:, s:s + 1], std[:, s:s + 1]).then_inc(inverted, 1)
                dve.wait_ge(inverted, t + 1)
                if by_degree:
                    nc.vector.tensor_scalar(rdis[:, s:s + 1], rstd[:, s:s + 1], g.src_tab[:, bass.ds(t, 1), 2],
                                            None, ALU.mult).then_inc(scaled, 1)
                    dve.wait_ge(scaled, t + 1)
                r = rdis if by_degree else rstd
                nc.vector.tensor_scalar(shift[:, s:s + 1], mv[:, s, 0:1], r[:, s:s + 1], -1.0,
                                        ALU.mult, ALU.mult).then_inc(coef_ready, 1)

            skewed(dve, ET, [(-1, stage), (6, coefs), (4, measure), (lag - 1, masks), (4, aggregate)] if normed else
                   [(-1, stage), (lag - 1, masks), (3, lows)], S, ahead=1)
            weights.lows(dve)

        @block.scalar
        def _(act):
            def root(i, s):
                act.wait_ge(var_ready, i * S + s + 1)
                nc.scalar.activation(std[:, s:s + 1], mv[:, s, 1:2], ACT.Sqrt, bias=g.eps_col[:, :]).then_inc(std_ready, 1)

            def apply(i, s):
                t = i * S + s
                act.wait_ge(coef_ready, t + 1)
                if later(i):
                    act.wait_ge(summed, t - S + 1)
                nc.scalar.activation(m[s][:, :], x[s][:, :], ACT.Identity, bias=shift[:, s:s + 1],
                                     scale=(rdis if by_degree else rstd)[:, s:s + 1]).then_inc(m_ready, 1)

            def empty(i, s):
                for c in range(2):
                    if c == 0 and later(i):
                        act.wait_ge(stored[s], i * 16)
                    act.wait_ge(half_summed[c], i * S + s + 1)
                    nc.scalar.activation(sums[s][:, half[c]], ps[c][s % B][:, 0:HALF], ACT.Copy).then_inc(half_emptied[c], 1)

            def highs(i, s):
                t = i * S + s
                act.wait_ge(got_x[s], i * 16 + 16)
                if later(i):
                    act.wait_ge(summed, t - S + 1)
                nc.scalar.activation(x_hi[s][:, :], x[s][:, :], ACT.Copy).then_inc(high, 1)

            def split(i, s):
                if isinstance(i, int) and i * S + s == 1:
                    weights.highs(act)

            skewed(act, ET, [(7, apply), (5, root), (8, empty), (6, split)] if normed else
                   [(2, highs), (lag, empty), (6, split)], S)

        @block.tensor
        def _(pe):
            def total(i, s):
                t = i * S + s
                pe.wait_ge(masks_ready, t + 1)
                if normed:
                    pe.wait_ge(m_ready, t + 1)
                else:
                    pe.wait_ge(low, t + 1)
                alone = isinstance(t, int) and t == 0
                if not (isinstance(t, int) and t < B):
                    pe.wait_ge(emptied, t - B + 1)
                parts = [m[s]] if normed else [x_hi[s], x_lo[s]]
                last = [None, None]
                for c in range(2):
                    for n, part in enumerate(parts):
                        last[c] = nc.tensor.matmul(ps[c][s % B][:, 0:HALF], same[s][:, :], part[:, half[c]], start=n == 0,
                                                   stop=alone and part is parts[-1])
                for c in range(2):
                    if not alone:
                        pe.wait_ge(half_emptied[c], t)
                        last[c] = nc.tensor.matmul(ps[c][s % B][:, 0:HALF], carry[s][:, :], sums[s - 1][:, half[c]],
                                                   start=False, stop=True)
                    last[c].then_inc(half_summed[c], 1)

            skewed(pe, ET, [(lag, total)], S)

        @block.sync
        def _(sp):
            def store(i, s):
                t = i * S + s
                sp.wait_ge(emptied, t + 1)
                sp.dma_start(out[bass.ds(t * P, P), :], sums[s][:, :]).then_inc(stored[s], 16)

            def load(i, s):
                t = i * S + s
                if later(i):
                    sp.wait_ge(m_ready, t - S + 1)
                sp.dma_start(x[s][:, :], rows[bass.ds(t * P, P), :]).then_inc(got_x[s], 16)

            def load_weights(i, s):
                if isinstance(i, int) and i * S + s == S - 1:
                    weights.load(sp)

            skewed(sp, ET, ([(0, load)] if in_order else []) + [(0, load_weights), (lag, store)], S)
            for s in range(S):
                sp.wait_ge(stored[s], len(range(s, ET, S)) * 16)


BIG = 3.0e38
HEADS = 8
DK = D // HEADS


def edge_logits(nc, g, x, weights, biases, v_dram):
    with ExitStack() as ctx:
        sb = lambda n, s, d=F32: ctx.enter_context(nc.sbuf_tensor(f"el_{n}", s, d))
        pb = lambda n, s: ctx.enter_context(nc.psum_tensor(f"el_{n}", s, F32))
        sem = lambda n: nc.alloc_semaphore(f"el_{n}")
        split = [split_weight(nc, ctx, n, w, KC, D) for n, w in zip(("wq", "wk", "wv"), weights)]
        w_parts = Weights(nc, ctx, split)
        (_, _, wq_hi, wq_lo), (_, _, wk_hi, wk_lo), (_, _, wv_hi, wv_lo) = split
        xs, xd = [sb(f"xs{s}", [P, D]) for s in range(K)], [sb(f"xd{s}", [P, D]) for s in range(K)]
        xT_hi = [[sb(f"xT_hi{w}{s}", [P, KC, P], F32R) for s in range(2)] for w in range(2)]
        xT_lo = [[sb(f"xT_lo{w}{s}", [P, KC, P], F32R) for s in range(2)] for w in range(2)]
        q, k, prod = [sb(f"q{s}", [P, D]) for s in range(2)], [sb(f"k{s}", [P, D]) for s in range(2)], [sb(f"qk{s}", [P, D]) for s in range(2)]
        v = [sb(f"v{s}", [P, D]) for s in range(K)]
        bias = [sb(f"bias{n}", [P, D]) for n in range(3)]
        dots, logit = sb("dots", [P, K, HEADS]), sb("logit", [P, K, HEADS])
        idx = sb("idx", [P, 2, K], I32)
        psT = [pb(f"psT{w}", [P, KC, P]) for w in range(2)]
        psq, psk, psv, psL = [pb(f"psq{s}", [P, D]) for s in range(2)], [pb(f"psk{s}", [P, D]) for s in range(2)], pb("psv", [P, D]), pb("psL", [HEADS, P])
        got = [[sem(f"got{w}{s}") for s in range(K)] for w in range(2)]
        ready, held, bias_in = sem("slot_ready"), sem("held"), sem("bias_in")
        turned, high, low = sem("turned"), sem("high"), sem("low")
        q_done, k_done, v_done = sem("q_done"), sem("k_done"), sem("v_done")
        q_out, k_out, v_out, multiplied, reduced = sem("q_out"), sem("k_out"), sem("v_out"), sem("multiplied"), sem("reduced")
        logit_ready, logit_turned, logit_kept = sem("logit_ready"), sem("logit_turned"), sem("logit_kept")
        stored = [sem(f"stored{s}") for s in range(K)]
        block = ctx.enter_context(nc.Block())

        @block.gpsimd
        def _(pool):
            last_row = pool.to_reg(N - 1)

            def step(i, s):
                t = i * K + s
                if later(i):
                    pool.wait_ge(turned, t - K + 1)
                hold(pool, ready, t + 1, held)
                for w, x_w in enumerate((xs, xd)):
                    nc.gpsimd.indirect_dma_start(x_w[s][:, :], None, x,
                                                 bass.IndirectOffsetOnAxis(idx[:, w, s:s + 1], 0),
                                                 bounds_check=last_row, oob_is_err=False).then_inc(got[w][s], 16)

            rounds(pool, ET, step)

        @block.tensor
        def _(pe):
            def project(i, s):
                t, h = i * K + s, s % 2
                pe.wait_ge(low, t + 1)
                for ps, w, (hi, lo), done, out in ((psq[h], 0, (wq_hi, wq_lo), q_done, q_out),
                                                   (psk[h], 1, (wk_hi, wk_lo), k_done, k_out),
                                                   (psv, 1, (wv_hi, wv_lo), v_done, v_out)):
                    if isinstance(t, int) and t == 0:
                        pe.wait_ge(w_parts.low, 3 if ps is psv else 1 + w)
                    if ps is psv:
                        if exists(back(i, s, 1)[0]):
                            pe.wait_ge(out, t)
                    elif exists(back(i, s, 2)[0]):
                        pe.wait_ge(out, t - 1)
                    n = 0
                    for a, b in ((xT_hi, hi), (xT_hi, lo), (xT_lo, hi)):
                        for c in range(KC):
                            last = nc.tensor.matmul(ps[:, :], a[w][h][:, c, :], b[:, c, :], start=n == 0,
                                                    stop=n == 3 * KC - 1)
                            n += 1
                    last.then_inc(done, 1)

            def turn_logits(i, s):
                t = i * K + s
                pe.wait_ge(logit_ready, t + 1)
                if not (isinstance(t, int) and t == 0):
                    pe.wait_ge(logit_kept, t)
                nc.tensor.transpose(psL[:, :], logit[:, s, :], g.ident[:, :]).then_inc(logit_turned, 1)

            def step(i, s):
                t = i * K + s
                for w, x_w in enumerate((xs, xd)):
                    pe.wait_ge(got[w][s], i * 16 + 16)
                if not (isinstance(t, int) and t == 0):
                    pe.wait_ge(low, t)
                for w, x_w in enumerate((xs, xd)):
                    for c in range(KC):
                        last = nc.tensor.transpose(psT[w][:, c, :], x_w[s][:, c * P:(c + 1) * P], g.ident[:, :])
                last.then_inc(turned, 1)
                if exists(back(i, s, 1)[0]):
                    project(*back(i, s, 1))
                if exists(back(i, s, 2)[0]):
                    turn_logits(*back(i, s, 2))

            rounds(pe, ET, step)
            project(ET // K - 1, K - 1)
            turn_logits(ET // K - 1, K - 2)
            turn_logits(ET // K - 1, K - 1)

        @block.scalar
        def _(act):
            def keep_logits(i, s):
                t = i * K + s
                act.wait_ge(logit_turned, t + 1)
                nc.scalar.activation(g.logits_T[:, bass.ds(t * P, P)], psL[:, :], ACT.Copy).then_inc(logit_kept, 1)

            def step(i, s):
                t = i * K + s
                act.wait_ge(turned, t + 1)
                if exists(back(i, s, 2)[0]):
                    act.wait_ge(v_done, t - 1)
                for w in range(2):
                    last = nc.scalar.activation(xT_hi[w][s % 2][:, :, :], psT[w][:, :, :], ACT.Copy)
                last.then_inc(high, 1)
                if exists(back(i, s, 3)[0]):
                    keep_logits(*back(i, s, 3))

            w_parts.highs(act)
            rounds(act, ET, step)
            for b in range(3, 0, -1):
                keep_logits(ET // K - 1, K - b)

        @block.vector
        def _(dve):
            def stage(t, s):
                nc.vector.tensor_scalar(idx[:, 0, s:s + 1], g.src_row[:, 0, bass.ds(t, 1)], 0.0, None, ALU.add)
                nc.vector.tensor_scalar(idx[:, 1, s:s + 1], g.dst_row[:, 0, bass.ds(t, 1)], 0.0, None, ALU.add)\
                  .then_inc(ready, 1)

            for s in range(K):
                stage(s, s)
            w_parts.lows(dve)
            dve.wait_ge(bias_in, 48)

            def finish(i, s):
                t, h = i * K + s, s % 2
                dve.wait_ge(q_done, t + 1)
                if exists(back(i, s, 2)[0]):
                    dve.wait_ge(multiplied, t - 1)
                nc.vector.tensor_tensor(q[h][:, :], psq[h][:, :], bias[0][:, :], ALU.add).then_inc(q_out, 1)
                dve.wait_ge(k_done, t + 1)
                nc.vector.tensor_tensor(k[h][:, :], psk[h][:, :], bias[1][:, :], ALU.add).then_inc(k_out, 1)
                dve.wait_ge(k_out, t + 1)
                dve.wait_ge(q_out, t + 1)
                if exists(back(i, s, 2)[0]):
                    dve.wait_ge(reduced, t - 1)
                nc.vector.tensor_tensor(prod[h][:, :], q[h][:, :], k[h][:, :], ALU.mult).then_inc(multiplied, 1)
                dve.wait_ge(v_done, t + 1)
                if later(i):
                    dve.wait_ge(stored[s], i * 16)
                nc.vector.tensor_tensor(v[s][:, :], psv[:, :], bias[2][:, :], ALU.add).then_inc(v_out, 1)
                dve.wait_ge(multiplied, t + 1)
                if later(i):
                    dve.wait_ge(logit_ready, t - K + 1)
                nc.vector.tensor_reduce(dots[:, s, :], prod[h][:, :].rearrange("p (h d) -> p h d", h=HEADS),
                                        AX.X, ALU.add).then_inc(reduced, 1)
                dve.wait_ge(reduced, t + 1)
                if later(i):
                    dve.wait_ge(logit_turned, t - K + 1)
                nc.vector.scalar_tensor_tensor(logit[:, s, :], dots[:, s, :], float(DK) ** -0.5,
                                               g.rec[0][:, bass.ds(t, 1), 6:14].rearrange("p a b -> p (a b)"),
                                               ALU.mult, ALU.add).then_inc(logit_ready, 1)

            def step(i, s):
                t = i * K + s
                dve.wait_ge(high, t + 1)
                for w in range(2):
                    last = nc.vector.tensor_tensor(xT_lo[w][s % 2][:, :, :], psT[w][:, :, :],
                                                   xT_hi[w][s % 2][:, :, :].bitcast(F32), ALU.subtract)
                last.then_inc(low, 1)
                if not (isinstance(t, int) and t + K >= ET):
                    dve.wait_ge(got[0][s], i * 16 + 16)
                    dve.wait_ge(got[1][s], i * 16 + 16)
                    stage(t + K, s)
                if exists(back(i, s, 1)[0]):
                    finish(*back(i, s, 1))

            rounds(dve, ET, step)
            finish(ET // K - 1, K - 1)

        @block.sync
        def _(sp):
            w_parts.load(sp)
            for b, src in zip(bias, biases):
                sp.dma_start(b[:, :], src.rearrange("(a n) -> a n", a=1).to_broadcast([P, D])).then_inc(bias_in, 16)

            def step(i, s):
                t = i * K + s
                sp.wait_ge(v_out, t + 1)
                sp.dma_start(v_dram[bass.ds(t * P, P), :], v[s][:, :]).then_inc(stored[s], 16)

            rounds(sp, ET, step)
            for s in range(K):
                sp.wait_ge(stored[s], ET // K * 16)


def edge_softmax(nc, g, then):
    with ExitStack() as ctx:
        sb = lambda n, s, d=F32: ctx.enter_context(nc.sbuf_tensor(f"es_{n}", s, d))
        sem = lambda n: nc.alloc_semaphore(f"es_{n}")
        joined, gap = sb("joined", [HEADS, EPAD + 1]), sb("gap", [HEADS, EPAD + 1])
        upto, top = sb("upto", [HEADS, EPAD]), sb("top", [HEADS, EPAD])
        p, inverse = sb("p", [HEADS, EPAD]), sb("inverse", [P, ET, HEADS])
        psP, psS = (ctx.enter_context(nc.psum_tensor(f"es_{n}", [P, D // HEADS, HEADS], F32))[:, 0:ET, :] for n in ("psP", "psS"))
        weights = Weights(nc, ctx, then)
        chain, centred, expd, att_ready, turned = sem("chain"), sem("centred"), sem("expd"), sem("att_ready"), sem("turned")
        block = ctx.enter_context(nc.Block())
        backwards = lambda ap: ap[:, ::-1]

        @block.sync
        def _(sp):
            weights.load(sp)

        @block.vector
        def _(dve):
            n_chain = [0]

            def link(ins):
                n_chain[0] += 1
                ins.then_inc(chain, 1)
                dve.wait_ge(chain, n_chain[0])

            nc.vector.memset(joined[:, 0:1], 0.0)
            nc.vector.memset(joined[:, EPAD:EPAD + 1], 0.0)
            link(nc.vector.tensor_tensor(joined[:, 1:EPAD], g.key_row[0:HEADS, 0, 1:EPAD],
                                         g.key_row[0:HEADS, 0, 0:EPAD - 1], ALU.is_equal))
            link(nc.vector.tensor_scalar(gap[:, :], joined[:, :], 1.0, BIG, ALU.subtract, ALU.mult))
            link(nc.vector.tensor_tensor_scan(upto[:, :], gap[:, 0:EPAD], g.logits_T[:, :], -BIG, ALU.add, ALU.max))
            link(nc.vector.tensor_tensor_scan(backwards(top), backwards(gap[:, 1:EPAD + 1]), backwards(upto),
                                              -BIG, ALU.add, ALU.max))
            nc.vector.tensor_tensor(p[:, :], g.logits_T[:, :], top[:, :], ALU.subtract).then_inc(centred, 1)
            dve.wait_ge(expd, 1)
            link(nc.vector.tensor_tensor_scan(upto[:, :], joined[:, 0:EPAD], p[:, :], 0.0, ALU.mult, ALU.add))
            nc.vector.tensor_tensor_scan(backwards(top), backwards(gap[:, 1:EPAD + 1]), backwards(upto),
                                         -BIG, ALU.add, ALU.max).then_inc(att_ready, 1)
            dve.wait_ge(turned, 1)
            link(nc.vector.reciprocal(inverse[:, :, :], psS[:, :, :]))
            nc.vector.tensor_tensor(g.att[:, :, :], psP[:, :, :], inverse[:, :, :], ALU.mult)
            weights.lows(dve)

        @block.scalar
        def _(act):
            weights.highs(act)
            act.wait_ge(centred, 1)
            nc.scalar.activation(p[:, :], p[:, :], ACT.Exp).then_inc(expd, 1)

        @block.tensor
        def _(pe):
            pe.wait_ge(att_ready, 1)
            for t in range(ET):
                nc.tensor.transpose(psP[:, t, :], p[:, t * P:(t + 1) * P], g.ident[0:HEADS, 0:HEADS])
                last = nc.tensor.transpose(psS[:, t, :], top[:, t * P:(t + 1) * P], g.ident[0:HEADS, 0:HEADS])
            last.then_inc(turned, 1)


def edge_attend(nc, g, v_dram, split, bo, out):
    with ExitStack() as ctx:
        sb = lambda n, s, d=F32: ctx.enter_context(nc.sbuf_tensor(f"ea_{n}", s, d))
        sem = lambda n: nc.alloc_semaphore(f"ea_{n}")
        _, _, wo_hi, wo_lo = split[0]
        v, av = [sb(f"v{s}", [P, D]) for s in range(K)], [sb(f"av{s}", [P, D]) for s in range(K)]
        same, carry = [sb(f"same{s}", [P, P]) for s in range(K)], [sb(f"carry{s}", [P, P], F32R) for s in range(K)]
        s_hi, s_lo = ([sb(f"{n}{s}", [P, D], F32R) for s in range(K)] for n in ("s_hi", "s_lo"))
        y_hi, y_lo = [sb(f"y_hi{s}", [P, KC, P], F32R) for s in range(2)], [sb(f"y_lo{s}", [P, KC, P], F32R) for s in range(2)]
        sums, biased = [sb(f"sums{s}", [P, D]) for s in range(K)], [sb(f"biased{s}", [P, D]) for s in range(K)]
        bias_row = sb("bias_row", [P, D])
        psY = [ctx.enter_context(nc.psum_tensor(f"ea_psY{s}", [P, KC, P], F32)) for s in range(2)]
        ps = [ctx.enter_context(nc.psum_tensor(f"ea_ps{s}", [P, D], F32)) for s in range(K)]
        loaded, stored = [sem(f"loaded{s}") for s in range(K)], [sem(f"stored{s}") for s in range(K)]
        weighed, masks_ready, y_done, high, low = sem("weighed"), sem("masks_ready"), sem("y_done"), sem("high"), sem("low")
        summed, emptied, s_high, s_low = sem("summed"), sem("emptied"), sem("s_high"), sem("s_low")
        bias_in, rows_stored, biased_ready = sem("bias_in"), sem("rows_stored"), sem("biased_ready")
        block = ctx.enter_context(nc.Block())

        @block.gpsimd
        def _(pool):
            pool.wait_ge(bias_in, 16)

            def step(i, s):
                pool.wait_ge(emptied, i * K + s + 1)
                if later(i):
                    pool.wait_ge(stored[s], i * 16)
                nc.gpsimd.tensor_tensor(biased[s][:, :], sums[s][:, :], bias_row[:, :], ALU.add).then_inc(biased_ready, 1)

            rounds(pool, ET, step)

        @block.sync
        def _(sp):
            sp.dma_start(bias_row[:, :], bo.rearrange("(a n) -> a n", a=1).to_broadcast([P, D])).then_inc(bias_in, 16)

            def load(i, s):
                if later(i):
                    sp.wait_ge(weighed, i * K + s - K + 1)
                sp.dma_start(v[s][:, :], v_dram[bass.ds((i * K + s) * P, P), :]).then_inc(loaded[s], 16)

            def store(i, s):
                sp.wait_ge(biased_ready, i * K + s + 1)
                sp.dma_start(out[bass.ds((i * K + s) * P, P), :], biased[s][:, :]).then_inc(stored[s], 16)

            for s in range(K - 1):
                load(0, s)
            sp.wait_ge(bias_in, 16)
            sp.dma_start(out[EPAD:TROWS, :], bias_row[:, :]).then_inc(rows_stored, 16)

            def step(i, s):
                t = i * K + s
                if not (isinstance(t, int) and t + K - 1 >= ET):
                    load(*((i, K - 1) if s == 0 else (i + 1, s - 1)))
                if exists(back(i, s, 2)[0]):
                    store(*back(i, s, 2))

            rounds(sp, ET, step)
            store(ET // K - 1, K - 2)
            store(ET // K - 1, K - 1)
            sp.wait_ge(rows_stored, 16)
            for s in range(K):
                sp.wait_ge(stored[s], ET // K * 16)

        @block.vector
        def _(dve):
            def lows(i, s):
                dve.wait_ge(high, i * K + s + 1)
                nc.vector.tensor_tensor(y_lo[s % 2][:, :, :], psY[s % 2][:, :, :], y_hi[s % 2][:, :, :].bitcast(F32),
                                        ALU.subtract).then_inc(low, 1)

            def sum_lows(i, s):
                dve.wait_ge(s_high, i * K + s + 1)
                nc.vector.tensor_tensor(s_lo[s][:, :], ps[s][:, :], s_hi[s][:, :].bitcast(F32), ALU.subtract)\
                  .then_inc(s_low, 1)

            def step(i, s):
                t = i * K + s
                dve.wait_ge(loaded[s], i * 16 + 16)
                if later(i):
                    dve.wait_ge(summed, t - K + 1)
                nc.vector.tensor_tensor(av[s][:, :].rearrange("p (h d) -> p h d", h=HEADS),
                                        v[s][:, :].rearrange("p (h d) -> p h d", h=HEADS),
                                        g.att[:, bass.ds(t, 1), :].rearrange("p a b -> p (a b)").unsqueeze(2)
                                        .to_broadcast([P, HEADS, DK]), ALU.mult).then_inc(weighed, 1)
                nc.vector.tensor_scalar(same[s][:, :], g.key_row[:, 0, bass.ds(t * P, P)],
                                        g.rec[0][:, bass.ds(t, 1), 0], None, ALU.is_equal)
                nc.vector.tensor_scalar(carry[s][:, :], g.key_row[:, 0, bass.ds(t * P, P)],
                                        g.prev_last[:, 0, bass.ds(t, 1)], None, ALU.is_equal).then_inc(masks_ready, 1)
                if exists(back(i, s, 1)[0]):
                    lows(*back(i, s, 1))
                if exists(back(i, s, 2)[0]):
                    sum_lows(*back(i, s, 2))

            rounds(dve, ET, step)
            lows(ET // K - 1, K - 1)
            sum_lows(ET // K - 1, K - 2)
            sum_lows(ET // K - 1, K - 1)

        @block.scalar
        def _(act):
            def empty(i, s):
                act.wait_ge(summed, i * K + s + 1)
                if later(i):
                    act.wait_ge(biased_ready, i * K + s - K + 1)
                nc.scalar.activation(s_hi[s][:, :], ps[s][:, :], ACT.Copy).then_inc(s_high, 1)
                act.wait_ge(s_low, i * K + s + 1)
                nc.scalar.activation(sums[s][:, :], ps[s][:, :], ACT.Copy).then_inc(emptied, 1)

            def step(i, s):
                t = i * K + s
                act.wait_ge(y_done, t + 1)
                if exists(back(i, s, 2)[0]):
                    act.wait_ge(summed, t - 1)
                nc.scalar.activation(y_hi[s % 2][:, :, :], psY[s % 2][:, :, :], ACT.Copy).then_inc(high, 1)
                if exists(back(i, s, 1)[0]):
                    empty(*back(i, s, 1))

            rounds(act, ET, step)
            empty(ET // K - 1, K - 1)

        @block.tensor
        def _(pe):
            def project(i, s):
                t, h = i * K + s, s % 2
                pe.wait_ge(low, t + 1)
                if later(i):
                    pe.wait_ge(emptied, t - K + 1)
                alone = isinstance(t, int) and t == 0
                n = 0
                for a, b in ((y_hi, wo_hi), (y_hi, wo_lo), (y_lo, wo_hi)):
                    for c in range(KC):
                        last = nc.tensor.matmul(ps[s][:, :], a[h][:, c, :], b[:, c, :], start=n == 0,
                                                stop=alone and n == 3 * KC - 1)
                        n += 1
                if not alone:
                    pe.wait_ge(s_low, t)
                    nc.tensor.matmul(ps[s][:, :], carry[s][:, :], s_hi[s - 1][:, :], start=False, stop=False)
                    last = nc.tensor.matmul(ps[s][:, :], carry[s][:, :], s_lo[s - 1][:, :], start=False, stop=True)
                last.then_inc(summed, 1)

            def step(i, s):
                t, h = i * K + s, s % 2
                pe.wait_ge(masks_ready, t + 1)
                if exists(back(i, s, 2)[0]):
                    pe.wait_ge(low, t - 1)
                for c in range(KC):
                    last = nc.tensor.matmul(psY[h][:, c, :], av[s][:, c * P:(c + 1) * P], same[s][:, :],
                                            start=True, stop=True)
                last.then_inc(y_done, 1)
                if exists(back(i, s, 1)[0]):
                    project(*back(i, s, 1))

            rounds(pe, ET, step)
            project(ET // K - 1, K - 1)


G4 = 4
NG = -(-NT // G4)
S8, B4 = 8, 4


def bias_rows(src):
    return src.rearrange("(a n) -> a n", a=1).to_broadcast([P, D])


def tile_rows(t):
    return NLAST if isinstance(t, int) and t == NT - 1 else P


def node_mlp(nc, g, x, comp_a, comp_b, split, b1, b2, out):
    with ExitStack() as ctx:
        sb = lambda n, s, d=F32: ctx.enter_context(nc.sbuf_tensor(f"nm_{n}", s, d))
        sem = lambda n: nc.alloc_semaphore(f"nm_{n}")
        (_, _, w1_hi, w1_lo), (_, _, w2_hi, w2_lo) = split
        xb, x1 = ([[sb(f"{n}_{h}{r}", [P, D]) for r in range(G4)] for h in range(2)] for n in ("x", "x1"))
        u, ypre, y = ([sb(f"{n}{r}", [P, D]) for r in range(G4)] for n in ("u", "ypre", "y"))
        uT_hi, uT_lo = ([sb(f"{n}{h}", [P, KC, D], F32R) for h in range(2)] for n in ("uT_hi", "uT_lo"))
        hT = [sb(f"hT{m}", [P, D]) for m in range(KC)]
        hT_hi, hT_lo = sb("hT_hi", [P, KC, D], F32R), sb("hT_lo", [P, KC, D], F32R)
        b1_col, b2_row = sb("b1_col", [P, KC]), sb("b2_row", [P, D])
        idx = sb("idx", [P, 2, 2, G4], I32)
        st, mv = [sb(f"st{w}", [P, G4, 6]) for w in range(2)], [sb(f"mv{w}", [P, G4, 2]) for w in range(2)]
        std, rstd, shift = ([sb(f"{n}{w}", [P, G4]) for w in range(2)] for n in ("std", "rstd", "shift"))
        psT = [ctx.enter_context(nc.psum_tensor(f"nm_psT{s}", [P, KC, P], F32)) for s in range(2)]
        ps1 = [ctx.enter_context(nc.psum_tensor(f"nm_ps1{s}", [P, D], F32)) for s in range(KC)]
        ps2 = [ctx.enter_context(nc.psum_tensor(f"nm_ps2{s}", [P, D], F32)) for s in range(2)]
        got_x, got_a, got_c = ([[sem(f"{n}{h}{r}") for r in range(G4)] for h in range(2)] for n in ("got_x", "got_a", "got_c"))
        stored = [sem(f"stored{r}") for r in range(G4)]
        a_ready, c_ready, held, bias_in = sem("a_ready"), sem("c_ready"), sem("held"), sem("bias_in")
        measured, var_ready, std_ready, inverted, coef_ready = (sem(n) for n in (
            "measured", "var_ready", "std_ready", "inverted", "coef_ready"))
        y_added, y_measured, y_var_ready, y_std_ready, y_inverted, y_coef_ready = (sem(n) for n in (
            "y_added", "y_measured", "y_var_ready", "y_std_ready", "y_inverted", "y_coef_ready"))
        x1_ready, u_ready, x1_biased, turned, high, low = (sem(n) for n in (
            "x1_ready", "u_ready", "x1_biased", "turned", "high", "low"))
        h_done, h_ready, h_high, h_low, y_done, y_ready = (sem(n) for n in (
            "h_done", "h_ready", "h_high", "h_low", "y_done", "y_ready"))
        block = ctx.enter_context(nc.Block())

        def tiles(q):
            return range(NT - (NG - 1) * G4 if isinstance(q, int) and q == NG - 1 else G4)

        def width(q):
            return len(tiles(q)) * P

        def past(q, n):
            return not isinstance(q, int) or q >= n

        def each(f):
            def stage(i, h):
                for r in tiles(i * 2 + h):
                    f(i, h, r)
            return stage

        def tile(r, f):
            return lambda i, h: f(i, h, r) if r in tiles(i * 2 + h) else None

        def chunk(m, f):
            return lambda i, h: f(i, h, m)

        @block.sync
        def _(sp):
            with nc.allow_non_contiguous_dma(reason="a bias onto the partitions, once"):
                sp.dma_start(b1_col[:, :], b1.rearrange("(m p) -> p m", p=P)).then_inc(bias_in, 16)
            sp.dma_start(b2_row[:, :], bias_rows(b2)).then_inc(bias_in, 16)

            def load(i, h, r):
                t = (i * 2 + h) * G4 + r
                if past(i * 2 + h, 2):
                    sp.wait_ge(x1_ready, t - 2 * G4 + 1)
                    sp.wait_ge(u_ready, t - 2 * G4 + 1)
                n = tile_rows(t)
                sp.dma_start(xb[h][r][0:n, :], x[bass.ds(t * P, n), :]).then_inc(got_x[h][r], 16)

            def store(i, h, r):
                t = (i * 2 + h) * G4 + r
                sp.wait_ge(y_ready, t + 1)
                n = tile_rows(t)
                sp.dma_start(out[bass.ds(t * P, n), :], y[r][0:n, :]).then_inc(stored[r], 16)

            skewed(sp, NG, [(-3, each(load)), (1, each(store))], 2, ahead=3)
            for r in range(G4):
                sp.wait_ge(stored[r], 16 * (NG if r in tiles(NG - 1) else NG - 1))

        @block.gpsimd
        def _(pool):
            last_sum = pool.to_reg(TROWS - 1)
            pool.wait_ge(bias_in, 32)

            def add_a(i, h, r):
                if r == 0:
                    pool.wait_ge(a_ready, i * 2 + h + 1)
                hold(pool, got_x[h][r], i * 16 + 16, held)
                nc.gpsimd.indirect_dma_start(xb[h][r][:, :], None, comp_a,
                                             bass.IndirectOffsetOnAxis(idx[:, 0, h, r:r + 1], 0),
                                             bounds_check=last_sum, compute_op=ALU.add).then_inc(got_a[h][r], 16)

            def add_bias(i, h, r):
                pool.wait_ge(x1_ready, (i * 2 + h) * G4 + r + 1)
                nc.gpsimd.tensor_tensor(x1[h][r][:, :], x1[h][r][:, :], b2_row[:, :], ALU.add).then_inc(x1_biased, 1)

            def add_c(i, h, r):
                if r == 0:
                    pool.wait_ge(c_ready, i * 2 + h + 1)
                hold(pool, u_ready, (i * 2 + h) * G4 + r + 1, held)
                nc.gpsimd.indirect_dma_start(u[r][:, :], None, comp_b,
                                             bass.IndirectOffsetOnAxis(idx[:, 1, h, r:r + 1], 0),
                                             bounds_check=last_sum, compute_op=ALU.add).then_inc(got_c[h][r], 16)

            skewed(pool, NG, [(-3, each(add_a)), (-1, each(add_bias)), (-2, each(add_c))], 2, ahead=3)

        @block.tensor
        def _(pe):
            def turn(i, h, r):
                t = (i * 2 + h) * G4 + r
                pe.wait_ge(got_c[h][r], i * 16 + 16)
                if not (isinstance(t, int) and t < 2):
                    pe.wait_ge(low, t - 1)
                for k in range(KC):
                    last = nc.tensor.transpose(psT[r % 2][:, k, :], u[r][:, k * P:(k + 1) * P], g.ident[:, :])
                last.then_inc(turned, 1)

            def up(i, h, m):
                q = i * 2 + h
                w = width(q)
                if m == 0:
                    pe.wait_ge(low, q * G4 + len(tiles(q)))
                if past(q, 1):
                    pe.wait_ge(h_low, q * KC + m - KC + 1)
                n = 0
                for wt, ut in ((w1_hi, uT_hi[h]), (w1_lo, uT_hi[h]), (w1_hi, uT_lo[h])):
                    for k in range(KC):
                        last = nc.tensor.matmul(ps1[m][:, 0:w], wt[:, k, m * P:(m + 1) * P], ut[:, k, 0:w],
                                                start=n == 0, stop=n == 3 * KC - 1)
                        n += 1
                last.then_inc(h_done, 1)

            def down(i, h, r):
                q = i * 2 + h
                t = q * G4 + r
                if not (isinstance(t, int) and t < 2):
                    pe.wait_ge(y_added, t - 1)
                n = 0
                for k in range(KC):
                    if r == 0:
                        pe.wait_ge(h_low, q * KC + k + 1)
                    for ht, wt in ((hT_hi, w2_hi), (hT_hi, w2_lo), (hT_lo, w2_hi)):
                        last = nc.tensor.matmul(ps2[r % 2][:, :], ht[:, k, r * P:(r + 1) * P], wt[:, k, :],
                                                start=n == 0, stop=n == 3 * KC - 1)
                        n += 1
                last.then_inc(y_done, 1)

            stages = [(0, chunk(0, up))]
            for m in range(1, KC):
                stages += [(0, chunk(m, up)), (-1, tile(m - 1, turn))]
            skewed(pe, NG, stages + [(-1, tile(G4 - 1, turn)), (0, each(down))], 2, ahead=1)

        @block.scalar
        def _(act):
            act.wait_ge(bias_in, 32)

            def hidden(i, h, m):
                q = i * 2 + h
                w = width(q)
                act.wait_ge(h_done, q * KC + m + 1)
                if past(q, 1):
                    act.wait_ge(h_low, q * KC + m - KC + 1)
                    act.wait_ge(y_done, q * G4)
                nc.scalar.activation(hT[m][:, 0:w], ps1[m][:, 0:w], ACT.Relu, bias=b1_col[:, m:m + 1])\
                  .then_inc(h_ready, 1)
                act.wait_ge(h_ready, q * KC + m + 1)
                nc.scalar.activation(hT_hi[:, m, 0:w], hT[m][:, 0:w], ACT.Copy).then_inc(h_high, 1)

            def highs(i, h, r):
                q = i * 2 + h
                act.wait_ge(turned, q * G4 + r + 1)
                if past(q, 2):
                    act.wait_ge(h_done, (q - 1) * KC)
                nc.scalar.activation(uT_hi[h][:, :, r * P:(r + 1) * P], psT[r % 2][:, :, :], ACT.Copy).then_inc(high, 1)

            def y_root(i, h, r):
                act.wait_ge(y_var_ready, (i * 2 + h) * G4 + r + 1)
                nc.scalar.activation(std[1][:, r:r + 1], mv[1][:, r, 1:2], ACT.Sqrt, bias=g.eps_col[:, :])\
                  .then_inc(y_std_ready, 1)

            def root(i, h, r):
                act.wait_ge(var_ready, (i * 2 + h) * G4 + r + 1)
                nc.scalar.activation(std[0][:, r:r + 1], mv[0][:, r, 1:2], ACT.Sqrt, bias=g.eps_col[:, :])\
                  .then_inc(std_ready, 1)

            def apply(i, h, r):
                q = i * 2 + h
                t = q * G4 + r
                act.wait_ge(coef_ready, t + 1)
                if past(q, 2):
                    act.wait_ge(y_added, t - 2 * G4 + 1)
                nc.scalar.activation(x1[h][r][:, :], xb[h][r][:, :], ACT.Identity, bias=shift[0][:, r:r + 1],
                                     scale=rstd[0][:, r:r + 1]).then_inc(x1_ready, 1)

            def y_apply(i, h, r):
                q = i * 2 + h
                act.wait_ge(y_coef_ready, q * G4 + r + 1)
                if past(q, 1):
                    act.wait_ge(stored[r], q * 16)
                nc.scalar.activation(y[r][:, :], ypre[r][:, :], ACT.Identity, bias=shift[1][:, r:r + 1],
                                     scale=rstd[1][:, r:r + 1]).then_inc(y_ready, 1)

            stages = [(0, chunk(0, hidden)), (1, tile(G4 - 1, y_apply)), (-1, tile(G4 - 1, apply))]
            for m in range(1, KC):
                stages += [(0, chunk(m, hidden)), (-2, tile(m - 1, root)), (-1, tile(m - 1, highs))]
            stages += [(-1, tile(G4 - 1, highs)), (-2, tile(G4 - 1, root))]
            for r in range(G4):
                stages += [(0, tile(r, y_root))]
                if r > 0:
                    stages += [(-2, tile(r - 1, apply)), (0, tile(r - 1, y_apply))]
            skewed(act, NG, stages, 2, ahead=2)

        @block.vector
        def _(dve):
            def stage(k, ready):
                def stage_group(i, h):
                    n = len(tiles(i * 2 + h))
                    nc.vector.tensor_scalar(idx[:, k, h, 0:n], g.node_row[:, 1, bass.ds((i * 2 + h) * G4, n)], 0.0,
                                            None, ALU.add).then_inc(ready, 1)
                return stage_group

            def measure(i, h, r):
                t = (i * 2 + h) * G4 + r
                dve.wait_ge(got_a[h][r], i * 16 + 16)
                nc.vector.bn_stats(st[0][:, r, :], xb[h][r][:, :]).then_inc(measured, 1)
                hold(dve, measured, t + 1, held)
                nc.vector.bn_aggr(mv[0][:, r, :], st[0][:, r, :]).then_inc(var_ready, 1)

            def coefs(w, std_sem, inv_sem, coef_sem):
                def tile_coefs(i, h, r):
                    t = (i * 2 + h) * G4 + r
                    dve.wait_ge(std_sem, t + 1)
                    nc.vector.reciprocal(rstd[w][:, r:r + 1], std[w][:, r:r + 1]).then_inc(inv_sem, 1)
                    dve.wait_ge(inv_sem, t + 1)
                    nc.vector.tensor_scalar(shift[w][:, r:r + 1], mv[w][:, r, 0:1], rstd[w][:, r:r + 1], -1.0,
                                            ALU.mult, ALU.mult).then_inc(coef_sem, 1)
                return tile_coefs

            def lows(i, h, r):
                dve.wait_ge(high, (i * 2 + h) * G4 + r + 1)
                nc.vector.tensor_tensor(uT_lo[h][:, :, r * P:(r + 1) * P], psT[r % 2][:, :, :],
                                        uT_hi[h][:, :, r * P:(r + 1) * P].bitcast(F32), ALU.subtract).then_inc(low, 1)

            def hidden(i, h, m):
                q = i * 2 + h
                w = width(q)
                dve.wait_ge(h_high, q * KC + m + 1)
                nc.vector.tensor_tensor(hT_lo[:, m, 0:w], hT[m][:, 0:w], hT_hi[:, m, 0:w].bitcast(F32),
                                        ALU.subtract).then_inc(h_low, 1)

            def finish(i, h, r):
                q = i * 2 + h
                t = q * G4 + r
                dve.wait_ge(y_done, t + 1)
                dve.wait_ge(x1_biased, t + 1)
                if past(q, 1):
                    dve.wait_ge(y_ready, t - G4 + 1)
                nc.vector.tensor_tensor(ypre[r][:, :], ps2[r % 2][:, :], x1[h][r][:, :], ALU.add).then_inc(y_added, 1)
                dve.wait_ge(y_added, t + 1)
                nc.vector.bn_stats(st[1][:, r, :], ypre[r][:, :]).then_inc(y_measured, 1)
                hold(dve, y_measured, t + 1, held)
                nc.vector.bn_aggr(mv[1][:, r, :], st[1][:, r, :]).then_inc(y_var_ready, 1)

            def copy_u(i, h, r):
                q = i * 2 + h
                dve.wait_ge(coef_ready, q * G4 + r + 1)
                if past(q, 1):
                    dve.wait_ge(turned, q * G4 + r - G4 + 1)
                nc.vector.tensor_scalar(u[r][:, :], xb[h][r][:, :], rstd[0][:, r:r + 1], shift[0][:, r:r + 1],
                                        ALU.mult, ALU.add).then_inc(u_ready, 1)

            x_coefs = coefs(0, std_ready, inverted, coef_ready)
            y_coefs = coefs(1, y_std_ready, y_inverted, y_coef_ready)
            stages = [(-3, stage(0, a_ready)), (-2, stage(1, c_ready))]
            for m in range(KC):
                stages += [(0, chunk(m, hidden)), (-2, tile(m, measure))]
                if m > 0:
                    stages += [(-1, tile(m - 1, lows)), (-2, tile(m - 1, x_coefs))]
            stages += [(-1, tile(G4 - 1, lows)), (-2, tile(G4 - 1, x_coefs))]
            for r in range(G4):
                stages += [(0, tile(r, finish)), (-2, tile(r, copy_u))]
                if r > 0:
                    stages += [(0, tile(r - 1, y_coefs))]
            stages += [(0, tile(G4 - 1, y_coefs))]
            skewed(dve, NG, stages, 2, ahead=3)


def node_conv1(nc, g, x2, comp_a, comp_b, split, b, x3_out, g_out):
    S, B = S8, B4
    with ExitStack() as ctx:
        sb = lambda n, s, d=F32: ctx.enter_context(nc.sbuf_tensor(f"n3_{n}", s, d))
        sem = lambda n: nc.alloc_semaphore(f"n3_{n}")
        _, _, w_hi, w_lo = split[0]
        xb, x3, v, z, gz = ([sb(f"{n}{s}", [P, D]) for s in range(S)] for n in ("x", "x3", "v", "z", "gz"))
        vT_hi, vT_lo = ([sb(f"{n}{s}", [P, KC, P], F32R) for s in range(2)] for n in ("vT_hi", "vT_lo"))
        b_row = sb("b_row", [P, D])
        idx = sb("idx", [P, 2, S], I32)
        stats, mv = sb("stats", [P, S, 6]), sb("mv", [P, S, 2])
        std, rstd, shift = sb("std", [P, S]), sb("rstd", [P, S]), sb("shift", [P, S])
        psT = [ctx.enter_context(nc.psum_tensor(f"n3_psT{s}", [P, KC, P], F32)) for s in range(B)]
        ps = [ctx.enter_context(nc.psum_tensor(f"n3_ps{s}", [P, D], F32)) for s in range(B)]
        got_x, got_a, got_c, x3_stored, g_stored = ([sem(f"{n}{s}") for s in range(S)] for n in
                                                    ("got_x", "got_a", "got_c", "x3_stored", "g_stored"))
        a_ready, c_ready, held, bias_in = (sem(n) for n in ("a_ready", "c_ready", "held", "bias_in"))
        measured, var_ready, std_ready, inverted, coef_ready, x3_ready = (sem(n) for n in (
            "measured", "var_ready", "std_ready", "inverted", "coef_ready", "x3_ready"))
        v_ready, turned, high, low, z_done, z_ready, g_ready, act_held = (sem(n) for n in (
            "v_ready", "turned", "high", "low", "z_done", "z_ready", "g_ready", "act_held"))
        block = ctx.enter_context(nc.Block())

        @block.sync
        def _(sp):
            sp.dma_start(b_row[:, :], bias_rows(b)).then_inc(bias_in, 16)

            def load(i, s):
                t = i * S + s
                if later(i):
                    sp.wait_ge(x3_ready, t - S + 1)
                n = tile_rows(t)
                sp.dma_start(xb[s][0:n, :], x2[bass.ds(t * P, n), :]).then_inc(got_x[s], 16)

            def store_x3(i, s):
                t = i * S + s
                n = tile_rows(t)
                sp.wait_ge(x3_ready, t + 1)
                sp.dma_start(x3_out[bass.ds(t * P, n), :], x3[s][0:n, :]).then_inc(x3_stored[s], 16)

            def store_g(i, s):
                t = i * S + s
                n = tile_rows(t)
                sp.wait_ge(g_ready, t + 1)
                sp.dma_start(g_out[bass.ds(t * P, n), :], gz[s][0:n, :]).then_inc(g_stored[s], 16)

            skewed(sp, NT, [(-2, load), (5, store_x3), (11, store_g)], S, ahead=2, peel=3)
            for s in range(S):
                sp.wait_ge(x3_stored[s], 16 * len(range(s, NT, S)))
                sp.wait_ge(g_stored[s], 16 * len(range(s, NT, S)))

        @block.gpsimd
        def _(pool):
            last_sum = pool.to_reg(TROWS - 1)

            def add_a(i, s):
                pool.wait_ge(a_ready, i * S + s + 1)
                hold(pool, got_x[s], i * 16 + 16, held)
                nc.gpsimd.indirect_dma_start(xb[s][:, :], None, comp_a, bass.IndirectOffsetOnAxis(idx[:, 0, s:s + 1], 0),
                                             bounds_check=last_sum, compute_op=ALU.add).then_inc(got_a[s], 16)

            def add_c(i, s):
                pool.wait_ge(c_ready, i * S + s + 1)
                hold(pool, v_ready, i * S + s + 1, held)
                nc.gpsimd.indirect_dma_start(v[s][:, :], None, comp_b, bass.IndirectOffsetOnAxis(idx[:, 1, s:s + 1], 0),
                                             bounds_check=last_sum, compute_op=ALU.add).then_inc(got_c[s], 16)

            skewed(pool, NT, [(0, add_a), (5, add_c)], S, peel=3)

        @block.tensor
        def _(pe):
            def turn(i, s):
                t = i * S + s
                pe.wait_ge(got_c[s], i * 16 + 16)
                if not (isinstance(t, int) and t < B):
                    pe.wait_ge(low, t - B + 1)
                for k in range(KC):
                    last = nc.tensor.transpose(psT[s % B][:, k, :], v[s][:, k * P:(k + 1) * P], g.ident[:, :])
                last.then_inc(turned, 1)

            def project(i, s):
                t, h = i * S + s, s % 2
                pe.wait_ge(low, t + 1)
                if not (isinstance(t, int) and t < B):
                    pe.wait_ge(z_ready, t - B + 1)
                n = 0
                for vt, wt in ((vT_hi, w_hi), (vT_hi, w_lo), (vT_lo, w_hi)):
                    for k in range(KC):
                        last = nc.tensor.matmul(ps[s % B][:, :], vt[h][:, k, :], wt[:, k, :], start=n == 0,
                                                stop=n == 3 * KC - 1)
                        n += 1
                last.then_inc(z_done, 1)

            skewed(pe, NT, [(7, turn), (8, project)], S, peel=3)

        @block.scalar
        def _(act):
            def root(i, s):
                act.wait_ge(var_ready, i * S + s + 1)
                nc.scalar.activation(std[:, s:s + 1], mv[:, s, 1:2], ACT.Sqrt, bias=g.eps_col[:, :]).then_inc(std_ready, 1)

            def apply(i, s):
                t = i * S + s
                act.wait_ge(coef_ready, t + 1)
                if later(i):
                    act.wait_ge(x3_stored[s], i * 16)
                    act.wait_ge(v_ready, t - S + 1)
                nc.scalar.activation(x3[s][:, :], xb[s][:, :], ACT.Identity, bias=shift[:, s:s + 1],
                                     scale=rstd[:, s:s + 1]).then_inc(x3_ready, 1)
                act.wait_ge(x3_ready, t + 1)
                if later(i):
                    act.wait_ge(turned, t - S + 1)
                nc.scalar.activation(v[s][:, :], x3[s][:, :], ACT.Copy, scale=g.dis[:, bass.ds(t, 1)]).then_inc(v_ready, 1)

            def highs(i, s):
                t = i * S + s
                act.wait_ge(turned, t + 1)
                if not (isinstance(t, int) and t < 2):
                    act.wait_ge(z_done, t - 1)
                nc.scalar.activation(vT_hi[s % 2][:, :, :], psT[s % B][:, :, :], ACT.Copy).then_inc(high, 1)

            def relu(i, s):
                t = i * S + s
                act.wait_ge(z_ready, t + 1)
                if later(i):
                    hold(act, g_stored[s], i * 16, act_held)
                nc.scalar.activation(gz[s][:, :], z[s][:, :], ACT.Relu, scale=g.dis[:, bass.ds(t, 1)]).then_inc(g_ready, 1)

            skewed(act, NT, [(7, highs), (10, relu), (4, apply), (2, root)], S, peel=3)

        @block.vector
        def _(dve):
            def stage_a(i, s):
                nc.vector.tensor_scalar(idx[:, 0, s:s + 1], g.node_row[:, 0, bass.ds(i * S + s, 1)], 0.0, None, ALU.add)\
                  .then_inc(a_ready, 1)

            def stage_c(i, s):
                nc.vector.tensor_scalar(idx[:, 1, s:s + 1], g.node_row[:, 1, bass.ds(i * S + s, 1)], 0.0, None, ALU.add)\
                  .then_inc(c_ready, 1)

            def measure(i, s):
                dve.wait_ge(got_a[s], i * 16 + 16)
                nc.vector.bn_stats(stats[:, s, :], xb[s][:, :]).then_inc(measured, 1)

            def aggregate(i, s):
                hold(dve, measured, i * S + s + 1, held)
                nc.vector.bn_aggr(mv[:, s, :], stats[:, s, :]).then_inc(var_ready, 1)

            def coefs(i, s):
                t = i * S + s
                dve.wait_ge(std_ready, t + 1)
                nc.vector.reciprocal(rstd[:, s:s + 1], std[:, s:s + 1]).then_inc(inverted, 1)
                dve.wait_ge(inverted, t + 1)
                nc.vector.tensor_scalar(shift[:, s:s + 1], mv[:, s, 0:1], rstd[:, s:s + 1], -1.0,
                                        ALU.mult, ALU.mult).then_inc(coef_ready, 1)

            def lows(i, s):
                dve.wait_ge(high, i * S + s + 1)
                nc.vector.tensor_tensor(vT_lo[s % 2][:, :, :], psT[s % B][:, :, :], vT_hi[s % 2][:, :, :].bitcast(F32),
                                        ALU.subtract).then_inc(low, 1)

            def out(i, s):
                t = i * S + s
                dve.wait_ge(z_done, t + 1)
                if later(i):
                    dve.wait_ge(g_ready, t - S + 1)
                nc.vector.scalar_tensor_tensor(z[s][:, :], ps[s % B][:, :], g.dis[:, bass.ds(t, 1)], b_row[:, :],
                                               ALU.mult, ALU.add).then_inc(z_ready, 1)

            dve.wait_ge(bias_in, 16)
            skewed(dve, NT, [(-1, stage_a), (7, lows), (9, out), (3, coefs), (1, measure), (4, stage_c), (1, aggregate)],
                   S, ahead=1, peel=3)


def node_conv2(nc, g, x3_in, g_in, comp, split, b, out):
    S, B = S8, B4
    with ExitStack() as ctx:
        sb = lambda n, s, d=F32: ctx.enter_context(nc.sbuf_tensor(f"n4_{n}", s, d))
        sem = lambda n: nc.alloc_semaphore(f"n4_{n}")
        _, _, w_hi, w_lo = split[0]
        x3, v, pre, y = ([sb(f"{n}{s}", [P, D]) for s in range(S)] for n in ("x3", "v", "pre", "y"))
        vT_hi, vT_lo = ([sb(f"{n}{s}", [P, KC, P], F32R) for s in range(2)] for n in ("vT_hi", "vT_lo"))
        b_row = sb("b_row", [P, D])
        idx = sb("idx", [P, S], I32)
        stats, mv = sb("stats", [P, S, 6]), sb("mv", [P, S, 2])
        std, rstd, shift = sb("std", [P, S]), sb("rstd", [P, S]), sb("shift", [P, S])
        psT = [ctx.enter_context(nc.psum_tensor(f"n4_psT{s}", [P, KC, P], F32)) for s in range(B)]
        ps = [ctx.enter_context(nc.psum_tensor(f"n4_ps{s}", [P, D], F32)) for s in range(B)]
        got_x, got_g, got_c, stored = ([sem(f"{n}{s}") for s in range(S)] for n in ("got_x", "got_g", "got_c", "stored"))
        c_ready, held, bias_in, x3_biased = (sem(n) for n in ("c_ready", "held", "bias_in", "x3_biased"))
        turned, high, low, z_done = (sem(n) for n in ("turned", "high", "low", "z_done"))
        added, measured, var_ready, std_ready, inverted, coef_ready, y_ready = (sem(n) for n in (
            "added", "measured", "var_ready", "std_ready", "inverted", "coef_ready", "y_ready"))
        block = ctx.enter_context(nc.Block())

        @block.sync
        def _(sp):
            sp.dma_start(b_row[:, :], bias_rows(b)).then_inc(bias_in, 16)

            def load_g(i, s):
                t = i * S + s
                n = tile_rows(t)
                if later(i):
                    sp.wait_ge(turned, t - S + 1)
                sp.dma_start(v[s][0:n, :], g_in[bass.ds(t * P, n), :]).then_inc(got_g[s], 16)

            def load_x3(i, s):
                t = i * S + s
                n = tile_rows(t)
                if later(i):
                    sp.wait_ge(added, t - S + 1)
                sp.dma_start(x3[s][0:n, :], x3_in[bass.ds(t * P, n), :]).then_inc(got_x[s], 16)

            def store(i, s):
                t = i * S + s
                n = tile_rows(t)
                sp.wait_ge(y_ready, t + 1)
                sp.dma_start(out[bass.ds(t * P, n), :], y[s][0:n, :]).then_inc(stored[s], 16)

            skewed(sp, NT, [(-3, load_g), (-1, load_x3), (7, store)], S, ahead=3)
            for s in range(S):
                sp.wait_ge(stored[s], 16 * len(range(s, NT, S)))

        @block.gpsimd
        def _(pool):
            last_sum = pool.to_reg(TROWS - 1)
            pool.wait_ge(bias_in, 16)

            def add_sums(i, s):
                pool.wait_ge(c_ready, i * S + s + 1)
                hold(pool, got_g[s], i * 16 + 16, held)
                nc.gpsimd.indirect_dma_start(v[s][:, :], None, comp, bass.IndirectOffsetOnAxis(idx[:, s:s + 1], 0),
                                             bounds_check=last_sum, compute_op=ALU.add).then_inc(got_c[s], 16)

            def add_bias(i, s):
                pool.wait_ge(got_x[s], i * 16 + 16)
                nc.gpsimd.tensor_tensor(x3[s][:, :], x3[s][:, :], b_row[:, :], ALU.add).then_inc(x3_biased, 1)

            skewed(pool, NT, [(-1, add_sums), (1, add_bias)], S, ahead=1)

        @block.tensor
        def _(pe):
            def turn(i, s):
                t = i * S + s
                pe.wait_ge(got_c[s], i * 16 + 16)
                if not (isinstance(t, int) and t < B):
                    pe.wait_ge(low, t - B + 1)
                for k in range(KC):
                    last = nc.tensor.transpose(psT[s % B][:, k, :], v[s][:, k * P:(k + 1) * P], g.ident[:, :])
                last.then_inc(turned, 1)

            def project(i, s):
                t, h = i * S + s, s % 2
                pe.wait_ge(low, t + 1)
                if not (isinstance(t, int) and t < B):
                    pe.wait_ge(added, t - B + 1)
                n = 0
                for vt, wt in ((vT_hi, w_hi), (vT_hi, w_lo), (vT_lo, w_hi)):
                    for k in range(KC):
                        last = nc.tensor.matmul(ps[s % B][:, :], vt[h][:, k, :], wt[:, k, :], start=n == 0,
                                                stop=n == 3 * KC - 1)
                        n += 1
                last.then_inc(z_done, 1)

            skewed(pe, NT, [(1, turn), (2, project)], S)

        @block.scalar
        def _(act):
            def highs(i, s):
                t = i * S + s
                act.wait_ge(turned, t + 1)
                if not (isinstance(t, int) and t < 2):
                    act.wait_ge(z_done, t - 1)
                nc.scalar.activation(vT_hi[s % 2][:, :, :], psT[s % B][:, :, :], ACT.Copy).then_inc(high, 1)

            def root(i, s):
                act.wait_ge(var_ready, i * S + s + 1)
                nc.scalar.activation(std[:, s:s + 1], mv[:, s, 1:2], ACT.Sqrt, bias=g.eps_col[:, :]).then_inc(std_ready, 1)

            def apply(i, s):
                act.wait_ge(coef_ready, i * S + s + 1)
                if later(i):
                    act.wait_ge(stored[s], i * 16)
                nc.scalar.activation(y[s][:, :], pre[s][:, :], ACT.Identity, bias=shift[:, s:s + 1],
                                     scale=rstd[:, s:s + 1]).then_inc(y_ready, 1)

            skewed(act, NT, [(1, highs), (6, apply), (4, root)], S)

        @block.vector
        def _(dve):
            def stage(i, s):
                if later(i):
                    dve.wait_ge(got_c[s], i * 16)
                nc.vector.tensor_scalar(idx[:, s:s + 1], g.node_row[:, 1, bass.ds(i * S + s, 1)], 0.0, None, ALU.add)\
                  .then_inc(c_ready, 1)

            def coefs(i, s):
                t = i * S + s
                dve.wait_ge(std_ready, t + 1)
                nc.vector.reciprocal(rstd[:, s:s + 1], std[:, s:s + 1]).then_inc(inverted, 1)
                dve.wait_ge(inverted, t + 1)
                nc.vector.tensor_scalar(shift[:, s:s + 1], mv[:, s, 0:1], rstd[:, s:s + 1], -1.0,
                                        ALU.mult, ALU.mult).then_inc(coef_ready, 1)

            def lows(i, s):
                dve.wait_ge(high, i * S + s + 1)
                nc.vector.tensor_tensor(vT_lo[s % 2][:, :, :], psT[s % B][:, :, :], vT_hi[s % 2][:, :, :].bitcast(F32),
                                        ALU.subtract).then_inc(low, 1)

            def out_pre(i, s):
                t = i * S + s
                dve.wait_ge(z_done, t + 1)
                dve.wait_ge(x3_biased, t + 1)
                if later(i):
                    dve.wait_ge(y_ready, t - S + 1)
                nc.vector.scalar_tensor_tensor(pre[s][:, :], ps[s % B][:, :], g.dis[:, bass.ds(t, 1)], x3[s][:, :],
                                               ALU.mult, ALU.add).then_inc(added, 1)
                dve.wait_ge(added, t + 1)
                nc.vector.bn_stats(stats[:, s, :], pre[s][:, :]).then_inc(measured, 1)
                hold(dve, measured, t + 1, held)
                nc.vector.bn_aggr(mv[:, s, :], stats[:, s, :]).then_inc(var_ready, 1)

            skewed(dve, NT, [(-3, stage), (1, lows), (3, out_pre), (5, coefs)], S, ahead=3)


MUL = 128
HID = 64
RB = 8
SILU_2MOM = 1.679177
AVG_NEIGHBORS = 10.0
RW = 256
RN = EPAD // RW


def radial(nc, g, w1, w2, w3, then):
    S = 8
    G = 4
    NK = ET // G
    with ExitStack() as ctx:
        sb = lambda n, s, d=F32: ctx.enter_context(nc.sbuf_tensor(f"ra_{n}", s, d))
        sem = lambda n: nc.alloc_semaphore(f"ra_{n}")
        wt = [sb("w1", [RB, HID]), sb("w2", [HID, HID]), sb("w3", [HID, HID])]
        attr = [sb(f"attr{h}", [P, RW // P, RB]) for h in range(2)]
        attr_T = [sb(f"attr_T{h}", [RB, RW]) for h in range(2)]
        hid = [[sb(f"hid{k}{h}", [HID, RW]) for h in range(2)] for k in range(2)]
        key_diag = [sb(f"key_diag{s}", [P, G, P]) for s in range(2)]
        rec_out, pos_out = sb("rec_out", [P, S, REC]), sb("pos_out", [P, S], I32)
        bank = [ctx.enter_context(nc.psum_tensor(f"ra_bank{h}", [P, G * P], F32)) for h in range(2)]
        psA = [b[0:RB, 0:RW] for b in bank]
        psH = [[ctx.enter_context(nc.psum_tensor(f"ra_ps{k}{h}", [HID, RW], F32)) for h in range(2)] for k in range(3)]
        w_in, staged, turned, attr_ready = sem("w_in"), sem("staged"), sem("turned"), sem("attr_ready")
        held, act_held, dve_held, pool_held = (sem(n) for n in ("held", "act_held", "dve_held", "pool_held"))
        done, ready = [sem(f"done{k}") for k in range(3)], [sem(f"ready{k}") for k in range(3)]
        diag_ready, row_ready, row_copied = sem("diag_ready"), sem("row_ready"), sem("row_copied")
        rec_staged = sem("rec_staged")
        reloaded, ids_ready = sem("reloaded"), sem("ids_ready")
        weights = Weights(nc, ctx, then)
        scattered = [sem(f"scattered{s}") for s in range(S)]
        block = ctx.enter_context(nc.Block())

        @block.sync
        def _(sp):
            for t, src in zip(wt, (w1, w2, w3)):
                sp.dma_start(t[:, :], src).then_inc(w_in, 16)
            weights.load(sp)
            for s in range(S):
                sp.wait_ge(scattered[s], ET // S * 16)
            sp.dma_start(g.rec[0][:, :, :], g.rec_dram[0].rearrange("(t p) c -> p t c", p=P)).then_inc(reloaded, 16)

        @block.gpsimd
        def _(pool):
            g.last_edge = pool.to_reg(EPAD - 1)

            def scatter(i, s):
                hold(pool, rec_staged, i * S + s + 1, pool_held)
                scatter_tile(nc, g, 0, rec_out, pos_out, s, scattered[s])

            skewed(pool, ET, [(0, scatter)], S)

        @block.vector
        def _(dve):
            def stage(i, s):
                if later(i):
                    dve.wait_ge(scattered[s], i * 16)
                stage_tile(nc, g, 0, rec_out, pos_out, i * S + s, s, rec_staged)

            skewed(dve, ET, [(0, stage)], S)

            for n, o in enumerate((1, 0)):
                if o == 0:
                    dve.wait_ge(reloaded, 16)
                    sorted_ids(nc, g, 0, dve, ids_ready)

                def diagonals(i, s, n=n, o=o):
                    t = i * 2 + s
                    u = t + n * NK
                    if not (isinstance(u, int) and u < 2):
                        hold(dve, row_ready, u - 1, dve_held)
                    nc.vector.tensor_tensor(key_diag[s][:, :, :], g.ident[:, :].unsqueeze(1).to_broadcast([P, G, P]),
                                            g.rec[o][:, bass.ds(t * G, G), o].unsqueeze(2).to_broadcast([P, G, P]),
                                            ALU.mult).then_inc(diag_ready, 1)

                skewed(dve, NK, [(0, diagonals)], 2, peel=1)
            weights.lows(dve)

        @block.tensor
        def _(pe):
            pe.wait_ge(w_in, 48)

            def layer(k):
                def run(i, s):
                    t, h = i * K + s, s % 2
                    if not (isinstance(t, int) and t < 2):
                        pe.wait_ge(ready[k], t - 1)
                    hold(pe, attr_ready if k == 0 else ready[k - 1], t + 1, held)
                    src = attr_T[h] if k == 0 else hid[k - 1][h]
                    nc.tensor.matmul(psH[k][h][:, :], wt[k][:, :], src[:, :], start=True, stop=True).then_inc(done[k], 1)
                return run

            def turn(i, s):
                t, h = i * K + s, s % 2
                pe.wait_ge(staged, t + 1)
                if not (isinstance(t, int) and t < 2):
                    pe.wait_ge(attr_ready, t - 1)
                for j in range(RW // P):
                    m = nc.tensor.transpose(psA[h][:, j * P:(j + 1) * P], attr[h][:, j, :], g.ident[:, :])
                m.then_inc(turned, 1)

            skewed(pe, RN, [(0, turn), (1, layer(0)), (2, layer(1)), (3, layer(2))], K)
            pe.wait_ge(attr_ready, RN)
            for n in range(2):
                def spread(i, s, n=n):
                    u = i * 2 + s + n * NK
                    pe.wait_ge(diag_ready, u + 1)
                    if not (isinstance(u, int) and u < 2):
                        pe.wait_ge(row_copied, u - 1)
                    nc.tensor.matmul(bank[s][:, :], g.ones[:, :], key_diag[s][:, :, :].rearrange("p g e -> p (g e)"),
                                     start=True, stop=True).then_inc(row_ready, 1)

                skewed(pe, NK, [(0, spread)], 2, peel=1)

        @block.scalar
        def _(act):
            def stage(i, s):
                t, h = i * K + s, s % 2
                if not (isinstance(t, int) and t < 2):
                    hold(act, turned, t - 1, act_held)
                nc.scalar.activation(attr[h][:, :, :], g.rec[1][:, bass.ds(t * (RW // P), RW // P), 6:14], ACT.Copy)\
                   .then_inc(staged, 1)

            def copy_attr(i, s):
                t, h = i * K + s, s % 2
                act.wait_ge(turned, t + 1)
                if not (isinstance(t, int) and t < 2):
                    act.wait_ge(done[0], t - 1)
                nc.scalar.activation(attr_T[h][:, :], psA[h][:, :], ACT.Copy).then_inc(attr_ready, 1)

            def layer(k):
                def run(i, s):
                    t, h = i * K + s, s % 2
                    act.wait_ge(done[k], t + 1)
                    if k < 2 and not (isinstance(t, int) and t < 2):
                        act.wait_ge(done[k + 1], t - 1)
                    out = hid[k][h][:, :] if k < 2 else g.hid3[:, bass.ds(t * RW, RW)]
                    scale = RB ** -0.5 if k == 0 else SILU_2MOM * HID ** -0.5
                    nc.scalar.activation(out, psH[k][h][:, :], ACT.Silu, scale=scale).then_inc(ready[k], 1)
                return run

            skewed(act, RN, [(-1, stage), (0, copy_attr), (1, layer(0)), (2, layer(1)), (3, layer(2))], K, ahead=1)
            weights.highs(act)
            for n, o in enumerate((1, 0)):
                def keep(i, s, n=n, o=o):
                    t = i * 2 + s
                    hold(act, row_ready, t + n * NK + 1, act_held)
                    nc.scalar.activation(g.key_row[:, o, bass.ds(t * G * P, G * P)], bank[s][:, :], ACT.Copy)\
                       .then_inc(row_copied, 1)

                skewed(act, NK, [(0, keep)], 2, peel=1)


def edge_messages(nc, g, x, split, w_mlp4, x_edges, out):
    NM = 2 * 4
    SCALE = MUL ** -0.5 * SILU_2MOM * HID ** -0.5 * (2 * MUL) ** -0.5 / AVG_NEIGHBORS
    with ExitStack() as ctx:
        sb = lambda n, s, d=F32: ctx.enter_context(nc.sbuf_tensor(f"em_{n}", s, d))
        sem = lambda n: nc.alloc_semaphore(f"em_{n}")
        up = [(hi[:, 0, :], lo[:, 0, :]) for _, _, hi, lo in split[:2]]
        down = [(hi, lo) for _, _, hi, lo in split[2:]]
        w4 = sb("w4", [HID, D])
        x_in = [sb(f"x{s}", [P, D]) for s in range(K)]
        xT_hi, xT_lo = ([sb(f"{n}{s}", [P, 4, P], F32R) for s in range(2)] for n in ("xT_hi", "xT_lo"))
        hid = [sb(f"hid{s}", [HID, P]) for s in range(2)]
        s_up = [sb(f"s_up{s}", [P, 4, P]) for s in range(2)]
        msg = [sb(f"msg{s}", [P, NM, P]) for s in range(2)]
        dot = [[sb(f"dot{s}{m}", [P, P]) for m in range(3)] for s in range(2)]
        same, carry = [sb(f"same{s}", [P, P]) for s in range(K)], [sb(f"carry{s}", [P, P], F32R) for s in range(K)]
        s_hi, s_lo = ([sb(f"{n}{s}", [P, 4, P], F32R) for s in range(2)] for n in ("s_hi", "s_lo"))
        mT_hi, mT_lo = ([sb(f"{n}{s}", [P, NM, P], F32R) for s in range(2)] for n in ("mT_hi", "mT_lo"))
        sums = [sb(f"sums{s}", [P, D]) for s in range(K)]
        idx, tab_slot, tab_idx = sb("idx", [P, K], I32), sb("tab_slot", [P, K, 4]), sb("tab_idx", [P, K], I32)
        pb = lambda n, s: ctx.enter_context(nc.psum_tensor(f"em_{n}", s, F32))
        psT, psU, psW, psM = pb("psT", [P, 4, P]), pb("psU", [P, 4, P]), pb("psW", [P, D]), [pb("psM0", [P, 4, P]), pb("psM1", [P, 4, P])]
        ps = [pb(f"ps{s}", [P, 4, P]) for s in range(2)]
        got, stored = [sem(f"got{s}") for s in range(K)], [sem(f"stored{s}") for s in range(K)]
        x_stored, tab_got = [sem(f"x_stored{s}") for s in range(K)], [sem(f"tab_got{s}") for s in range(K)]
        tab_staged, tab_kept, s_high, s_low = sem("tab_staged"), sem("tab_kept"), sem("s_high"), sem("s_low")
        ready, held, w_in = sem("slot_ready"), sem("held"), sem("w_in")
        turned, high, low, hid_ready, upped, s_ready = (sem(n) for n in ("turned", "high", "low", "hid_ready", "upped", "s_ready"))
        dot0, dot1, dot2, msg_ready, masks_ready = (sem(n) for n in ("dot0", "dot1", "dot2", "msg_ready", "masks_ready"))
        m_done, m_high, m_low, summed, emptied = (sem(n) for n in ("m_done", "m_high", "m_low", "summed", "emptied"))
        block = ctx.enter_context(nc.Block())
        vectors = lambda ap: ap.rearrange("p (v m) -> p m v", m=3)

        @block.sync
        def _(sp):
            sp.dma_start(w4[:, :], w_mlp4).then_inc(w_in, 16)

            def store_x(i, s):
                sp.wait_ge(got[s], i * 16 + 16)
                sp.dma_start(x_edges[bass.ds((i * K + s) * P, P), :], x_in[s][:, :]).then_inc(x_stored[s], 16)

            def store(i, s):
                t = i * K + s
                sp.wait_ge(emptied, t + 1)
                sp.dma_start(out[bass.ds(t * P, P), :], sums[s][:, :]).then_inc(stored[s], 16)

            skewed(sp, ET, [(0, store_x), (4, store)], K)
            for s in range(K):
                sp.wait_ge(x_stored[s], ET // K * 16)
                sp.wait_ge(stored[s], ET // K * 16)

        @block.gpsimd
        def _(pool):
            last_row, last_node = pool.to_reg(N - 1), pool.to_reg(NT * P - 1)

            def step(i, s):
                t = i * K + s
                if later(i):
                    pool.wait_ge(turned, t - K + 1)
                    pool.wait_ge(x_stored[s], i * 16)
                hold(pool, ready, t + 1, held)
                nc.gpsimd.indirect_dma_start(x_in[s][:, :], None, x, bass.IndirectOffsetOnAxis(idx[:, s:s + 1], 0),
                                             bounds_check=last_row, oob_is_err=False).then_inc(got[s], 16)
                hold(pool, tab_staged, t + 1, held)
                nc.gpsimd.indirect_dma_start(
                    tab_slot[:, s, :], None, g.ntab_dram, bass.IndirectOffsetOnAxis(tab_idx[:, s:s + 1], 0),
                    bounds_check=last_node, oob_is_err=False).then_inc(tab_got[s], 16)

            rounds(pool, ET, step)

        @block.tensor
        def _(pe):
            pe.wait_ge(w_in, 16)

            def turn(i, s):
                t = i * K + s
                pe.wait_ge(got[s], i * 16 + 16)
                if not (isinstance(t, int) and t == 0):
                    pe.wait_ge(low, t)
                nc.tensor.transpose(psT[:, 0, :], x_in[s][:, 0:MUL], g.ident[:, :])
                for m in range(3):
                    last = nc.tensor.transpose(psT[:, 1 + m, :], vectors(x_in[s][:, MUL:D])[:, m, :], g.ident[:, :])
                last.then_inc(turned, 1)

            def lift(i, s):
                t, h = i * K + s, s % 2
                pe.wait_ge(low, t + 1)
                pe.wait_ge(hid_ready, t + 1)
                if not (isinstance(t, int) and t == 0):
                    pe.wait_ge(msg_ready, t)
                for m in range(4):
                    w_hi, w_lo = up[min(m, 1)]
                    for n, (a, b) in enumerate(((xT_hi, w_hi), (xT_hi, w_lo), (xT_lo, w_hi))):
                        nc.tensor.matmul(psU[:, m, :], a[h][:, m, :], b, start=n == 0, stop=n == 2)
                nc.tensor.matmul(psW[:, :], hid[h][:, :], w4[:, :], start=True, stop=True).then_inc(upped, 1)

            def gather(i, s):
                t, h = i * K + s, s % 2
                pe.wait_ge(msg_ready, t + 1)
                pe.wait_ge(masks_ready, t + 1)
                if not (isinstance(t, int) and t == 0):
                    pe.wait_ge(m_low, t)
                for c in range(NM):
                    last = nc.tensor.matmul(psM[c // 4][:, c % 4, :], msg[h][:, c, :], same[s][:, :], start=True, stop=True)
                last.then_inc(m_done, 1)

            def project(i, s):
                t, h = i * K + s, s % 2
                pe.wait_ge(m_low, t + 1)
                if exists(back(i, s, 2)[0]):
                    pe.wait_ge(emptied, t - 1)
                alone = isinstance(t, int) and t == 0
                if not alone:
                    pe.wait_ge(s_low, t)
                    whole = lambda ap: ap[:, :, :].rearrange("p m v -> p (m v)")
                    for n, part in enumerate((s_hi, s_lo)):
                        nc.tensor.matmul(whole(ps[h]), carry[s][:, :], whole(part[1 - h]), start=n == 0, stop=False)
                for r in range(4):
                    w_hi, w_lo = down[min(r, 1)]
                    n = 0
                    for a, b in ((mT_hi, w_hi), (mT_hi, w_lo), (mT_lo, w_hi)):
                        for c in range(2):
                            last = nc.tensor.matmul(ps[h][:, r, :], a[h][:, 2 * r + c, :], b[:, c, :], start=alone and n == 0,
                                                    stop=n == 5 and (alone or r == 3))
                            n += 1
                last.then_inc(summed, 1)

            def step(i, s):
                turn(i, s)
                for k, f in ((1, lift), (2, gather), (3, project)):
                    if exists(back(i, s, k)[0]):
                        f(*back(i, s, k))

            rounds(pe, ET, step)
            n = ET - 1
            for k, f in ((0, lift), (1, gather), (2, project), (0, gather), (1, project), (0, project)):
                f(*divmod(n - k, K))

        @block.scalar
        def _(act):
            def highs(i, s):
                t, h = i * K + s, s % 2
                if exists(back(i, s, 2)[0]):
                    act.wait_ge(upped, t - 1)
                nc.scalar.activation(hid[h][:, :], g.hid3[:, bass.ds(t * P, P)], ACT.Copy).then_inc(hid_ready, 1)
                act.wait_ge(turned, t + 1)
                nc.scalar.activation(xT_hi[h][:, :, :], psT[:, :, :], ACT.Copy).then_inc(high, 1)

            def lifted(i, s):
                t, h = i * K + s, s % 2
                act.wait_ge(upped, t + 1)
                if exists(back(i, s, 2)[0]):
                    act.wait_ge(msg_ready, t - 1)
                nc.scalar.activation(s_up[h][:, :, :], psU[:, :, :], ACT.Copy, scale=SCALE).then_inc(s_ready, 1)

            def message_highs(i, s):
                t, h = i * K + s, s % 2
                act.wait_ge(m_done, t + 1)
                if exists(back(i, s, 2)[0]):
                    act.wait_ge(summed, t - 1)
                for b in range(2):
                    last = nc.scalar.activation(mT_hi[h][:, 4 * b:4 * b + 4, :], psM[b][:, :, :], ACT.Copy)
                last.then_inc(m_high, 1)

            def sum_highs(i, s):
                t, h = i * K + s, s % 2
                act.wait_ge(summed, t + 1)
                nc.scalar.activation(s_hi[h][:, :, :], ps[h][:, :, :], ACT.Copy).then_inc(s_high, 1)

            def empty(i, s):
                t, h = i * K + s, s % 2
                act.wait_ge(s_low, t + 1)
                if later(i):
                    act.wait_ge(stored[s], i * 16)
                nc.scalar.activation(sums[s][:, 0:MUL], ps[h][:, 0, :], ACT.Copy)
                nc.scalar.activation(sums[s][:, MUL:D].rearrange("p (v m) -> p v m", m=3),
                                     ps[h][:, 1:4, :].rearrange("p m v -> p v m"), ACT.Copy).then_inc(emptied, 1)

            skewed(act, ET, [(0, highs), (1, lifted), (2, message_highs), (3, sum_highs), (4, empty)], K)

        @block.vector
        def _(dve):
            def stage(t, s):
                nc.vector.tensor_scalar(idx[:, s:s + 1], g.src_row[:, 1, bass.ds(t, 1)], 0.0, None, ALU.add)\
                  .then_inc(ready, 1)
                nc.vector.tensor_scalar(tab_idx[:, s:s + 1], g.src_any[:, 1, bass.ds(t, 1)], 0.0, None, ALU.add)\
                  .then_inc(tab_staged, 1)

            def lows(i, s):
                t, h = i * K + s, s % 2
                dve.wait_ge(high, t + 1)
                nc.vector.tensor_tensor(xT_lo[h][:, :, :], psT[:, :, :], xT_hi[h][:, :, :].bitcast(F32),
                                        ALU.subtract).then_inc(low, 1)
                dve.wait_ge(tab_got[s], i * 16 + 16)
                nc.vector.tensor_scalar(g.src_tab[:, bass.ds(t, 1), :].rearrange("p a b -> p (a b)"),
                                        tab_slot[:, s, :], 0.0, None, ALU.add).then_inc(tab_kept, 1)
                if not (isinstance(t, int) and t + K >= ET):
                    dve.wait_ge(got[s], i * 16 + 16)
                    stage(t + K, s)
                if later(i):
                    dve.wait_ge(summed, t - K + 1)
                nc.vector.tensor_scalar(same[s][:, :], g.key_row[:, 1, bass.ds(t * P, P)],
                                        g.rec[1][:, bass.ds(t, 1), 1], None, ALU.is_equal)
                nc.vector.tensor_scalar(carry[s][:, :], g.key_row[:, 1, bass.ds(t * P, P)],
                                        g.prev_last[:, 1, bass.ds(t, 1)], None, ALU.is_equal).then_inc(masks_ready, 1)

            def messages(i, s):
                t, h = i * K + s, s % 2
                y = [g.rec[1][:, bass.ds(t, 1), 2 + m] for m in range(4)]
                sv, w, o = s_up[h], psW, msg[h]
                dve.wait_ge(s_ready, t + 1)
                if exists(back(i, s, 2)[0]):
                    dve.wait_ge(m_done, t - 1)
                    dve.wait_ge(msg_ready, t - 1)
                nc.vector.tensor_scalar(dot[h][0][:, :], sv[:, 1, :], y[1], None, ALU.mult).then_inc(dot0, 1)
                nc.vector.scalar_tensor_tensor(o[:, 0, :], w[:, 0:MUL], y[0], sv[:, 0, :], ALU.mult, ALU.mult)
                dve.wait_ge(dot0, t + 1)
                nc.vector.scalar_tensor_tensor(dot[h][1][:, :], sv[:, 2, :], y[2], dot[h][0][:, :], ALU.mult, ALU.add)\
                  .then_inc(dot1, 1)
                for m in range(3):
                    nc.vector.scalar_tensor_tensor(o[:, 2 + 2 * m, :], w[:, MUL:2 * MUL], y[1 + m], sv[:, 0, :],
                                                   ALU.mult, ALU.mult)
                dve.wait_ge(dot1, t + 1)
                nc.vector.scalar_tensor_tensor(dot[h][2][:, :], sv[:, 3, :], y[3], dot[h][1][:, :], ALU.mult, ALU.add)\
                  .then_inc(dot2, 1)
                nc.vector.scalar_tensor_tensor(o[:, :, :].rearrange("p (a b) v -> p b a v", b=2)[:, 1, 1:4, :],
                                               w[:, 2 * MUL:3 * MUL].unsqueeze(1).to_broadcast([P, 3, MUL]), y[0],
                                               sv[:, 1:4, :], ALU.mult, ALU.mult)
                dve.wait_ge(dot2, t + 1)
                nc.vector.scalar_tensor_tensor(o[:, 1, :], w[:, 3 * MUL:4 * MUL], 3.0 ** -0.5, dot[h][2][:, :],
                                               ALU.mult, ALU.mult).then_inc(msg_ready, 1)

            def message_lows(i, s):
                t, h = i * K + s, s % 2
                dve.wait_ge(m_high, t + 1)
                for b in range(2):
                    last = nc.vector.tensor_tensor(mT_lo[h][:, 4 * b:4 * b + 4, :], psM[b][:, :, :],
                                                   mT_hi[h][:, 4 * b:4 * b + 4, :].bitcast(F32), ALU.subtract)
                last.then_inc(m_low, 1)

            for s in range(K):
                stage(s, s)

            def sum_lows(i, s):
                h = s % 2
                dve.wait_ge(s_high, i * K + s + 1)
                nc.vector.tensor_tensor(s_lo[h][:, :, :], ps[h][:, :, :], s_hi[h][:, :, :].bitcast(F32), ALU.subtract)\
                  .then_inc(s_low, 1)

            skewed(dve, ET, [(4, sum_lows), (0, lows), (1, messages), (2, message_lows)], K)
            dve.wait_ge(tab_kept, ET)
            nc.vector.tensor_copy(g.src_comp[:, :, :], g.src_tab[:, :, 0:2].rearrange("p t o -> p o t"))


class Shared:
    pass


def persistent(nc, ctx, g):
    sb = lambda n, s, d=F32: ctx.enter_context(nc.sbuf_tensor(n, s, d))
    dram = lambda n, s: nc.dram_tensor(n, s, F32, kind="Internal").ap()
    g.ident, g.ones, g.ident_bf = sb("ident", [P, P]), sb("ones", [P, P]), sb("ident_bf", [P, P], BF16)
    g.before, g.after = sb("before", [P, P]), sb("after", [P, P])
    g.last_row, g.one_col, g.eps_col = sb("last_row", [P, 1]), sb("one_col", [P, 1]), sb("eps_col", [P, 1])
    g.zeros = sb("zero_rows", [P, D])
    g.node_row, g.dis = sb("node_row", [P, 2, NT], I32), sb("dis", [P, NT])
    g.rec = [sb(f"rec{o}", [P, ET, REC]) for o in range(2)]
    g.src_any, g.src_row, g.dst_row = (sb(n, [P, 2, ET], I32) for n in ("src_any", "src_row", "dst_row"))
    g.prev_last = sb("prev_last", [P, 2, ET])
    g.src_tab, g.src_comp = sb("src_tab", [P, ET, 4]), sb("src_comp", [P, 2, ET], I32)
    g.key_row = sb("key_row", [P, 2, EPAD])
    g.ntab_dram = dram("ntab_dram", [NT * P, 4])
    g.rec_dram = [dram(f"rec_dram{o}", [EPAD, REC]) for o in range(2)]


def prepare(nc, g):
    with ExitStack() as ctx:
        sb = lambda n, s, d=F32: ctx.enter_context(nc.sbuf_tensor(n, s, d))
        g.hot_hi, g.hot_lo = sb("hot_hi", [P, 2, ET, NT], BF16), sb("hot_lo", [P, 2, ET, P], BF16)
        g.keys, g.ntab = sb("keys", [P, 2, ET]), sb("ntab", [NT, P, 4])
        g.iota = sb("iota_row", [P, P])
        load_edges(nc, g)
        sort_positions(nc, g)


def graph_network(nc, x, src, dst, edge_attr_4, edge_attr_8, w_up0, w_up1, w_mlp1, w_mlp2, w_mlp3, w_mlp4,
                  w_out0, w_out1, mlp_w1, mlp_b1, mlp_w2, mlp_b2, wq, bq, wk, bk, wv, bv, wo, bo,
                  conv_w1, conv_b1, conv_w2, conv_b2, out):
    g = Shared()
    g.src, g.dst, g.edge_attr_4, g.edge_attr_8 = src, dst, edge_attr_4, edge_attr_8
    table = lambda n, rows: nc.dram_tensor(n, [rows, D], F32, kind="Internal").ap()
    messages, x1_sums, attended, x3_sums, conv_sums, v, x_edges = (table(n, TROWS) for n in (
        "messages", "x1_sums", "attended", "x3_sums", "conv_sums", "v_edges", "x_edges"))
    g.summed_tables = (messages, x1_sums, x3_sums, conv_sums)
    x2, x3, hidden = (table(n, N) for n in ("x2", "x3", "conv_hidden"))
    with ExitStack() as ctx:
        persistent(nc, ctx, g)
        stage = nc.cleanup_on_exit
        with ExitStack() as ctx:
            g.rec_in = ctx.enter_context(nc.sbuf_tensor("rec_in", [P, ET, REC], F32))
            g.position = ctx.enter_context(nc.sbuf_tensor("position", [P, 2, ET], F32))
            with stage():
                prepare(nc, g)
            g.hid3 = ctx.enter_context(nc.sbuf_tensor("hid3", [HID, EPAD], F32))
            split = [split_weight(nc, ctx, n, w, k, MUL) for n, w, k in
                     (("up0", w_up0, 1), ("up1", w_up1, 1), ("out0", w_out0, 2), ("out1", w_out1, 2))]
            with stage():
                radial(nc, g, w_mlp1, w_mlp2, w_mlp3, split)
            with stage():
                edge_messages(nc, g, x, split, w_mlp4, x_edges, messages)
        with ExitStack() as ctx:
            split = [split_weight(nc, ctx, n, w, KC, D) for n, w in (("w1", mlp_w1), ("w2", mlp_w2))]
            with stage():
                edge_sums(nc, g, "e1", x_edges, x1_sums, comp=messages, comp_order=1, in_order=True, then=split)
            with stage():
                node_mlp(nc, g, x, messages, x1_sums, split, mlp_b1, mlp_b2, x2)
        with ExitStack() as ctx:
            g.att = ctx.enter_context(nc.sbuf_tensor("att", [P, ET, HEADS], F32))
            g.logits_T = ctx.enter_context(nc.sbuf_tensor("logits_T", [HEADS, EPAD], F32))
            with stage():
                edge_logits(nc, g, x2, (wq, wk, wv), (bq, bk, bv), v)
            split = [split_weight(nc, ctx, "wo", wo, KC, D)]
            with stage():
                edge_softmax(nc, g, split)
            with stage():
                edge_attend(nc, g, v, split, bo, attended)
        with ExitStack() as ctx:
            split = [split_weight(nc, ctx, "conv1_w", conv_w1, KC, D)]
            with stage():
                edge_sums(nc, g, "e3", x2, x3_sums, comp=attended, comp_order=0, by_degree=True, then=split)
            with stage():
                node_conv1(nc, g, x2, attended, x3_sums, split, conv_b1, x3, hidden)
        with ExitStack() as ctx:
            split = [split_weight(nc, ctx, "conv2_w", conv_w2, KC, D)]
            with stage():
                edge_sums(nc, g, "e4", hidden, conv_sums, normed=False, then=split)
            with stage():
                node_conv2(nc, g, x3, hidden, conv_sums, split, conv_b2, out)


_INS = ['x', 'src', 'dst', 'edge_attr_4', 'edge_attr_8', 'L0_gnn_W_up0', 'L0_gnn_W_up1', 'L0_gnn_W_mlp1',
        'L0_gnn_W_mlp2', 'L0_gnn_W_mlp3', 'L0_gnn_W_mlp4', 'L0_gnn_W_out0', 'L0_gnn_W_out1', 'L1_gnn_W1',
        'L1_gnn_b1', 'L1_gnn_W2', 'L1_gnn_b2', 'L2_gnn_Wq', 'L2_gnn_bq', 'L2_gnn_Wk', 'L2_gnn_bk', 'L2_gnn_Wv',
        'L2_gnn_bv', 'L2_gnn_Wo', 'L2_gnn_bo', 'L3_gnn_W1', 'L3_gnn_b1', 'L3_gnn_W2', 'L3_gnn_b2']
_OUTS = [((10000, 512), 'float32')]


def kernel(**inputs):
    import numpy as _np
    import concourse.bacc as _bacc
    from concourse import mybir as _mybir
    from concourse.bass_utils import run_bass_kernel_spmd as _run

    nc = _bacc.Bacc("TRN2", target_bir_lowering=False, num_devices=1)
    arrays, args = {}, []
    for name in _INS:
        a = _np.ascontiguousarray(inputs[name])
        arrays[f"in_{name}_dram"] = a
        args.append(nc.dram_tensor(f"in_{name}_dram", a.shape, _mybir.dt.from_np(a.dtype), kind="ExternalInput").ap())
    for i, (shape, dtype) in enumerate(_OUTS):
        dt = _mybir.dt.from_np(_np.dtype(dtype))
        args.append(nc.dram_tensor(f"out_{i}_dram", shape, dt, kind="ExternalOutput").ap())
    graph_network(nc, *args)
    r = _run(nc, [arrays], core_ids=[0])
    got = tuple(r.results[0][f"out_{i}_dram"] for i in range(len(_OUTS)))
    return got[0]
```
